# Optimizing a Trainium2 kernel written in Bass

```python
import numpy as np
import jax
import jax.numpy as jnp

def _softmax(x, axis=-1):
    return jax.nn.softmax(x, axis=axis)

def _gelu(x):
    return jax.nn.gelu(x, approximate=True)

def _silu(x):
    return jax.nn.silu(x)

def _sigmoid(x):
    return jax.nn.sigmoid(x)

def _layernorm(x, axis=-1, eps=1e-05):
    m = jnp.mean(x, axis=axis, keepdims=True)
    v = jnp.var(x, axis=axis, keepdims=True)
    return (x - m) / jnp.sqrt(v + eps)

def _scatter_add(tgt, idx, src, axis=0):
    return tgt.at[idx].add(src)

def _segment_sum(src, seg, n):
    return jax.ops.segment_sum(src, seg, n)
kernel_name = 'mk_macaron_d4_jaxref_r8_f74919'

def setup_inputs(seed: int=0):
    np.random.seed(seed)
    _w = jnp.asarray

    def _L0_attn_setup():
        import jax, jax.numpy as jnp
        import numpy as np
        B, N, D = (2, 256, 128)
        H, DH = (16, 64)
        key = jax.random.key(seed)
        ks = jax.random.split(key, 5)
        s = 0.02
        return {'x': jax.random.normal(ks[0], (B, N, D), dtype=jnp.float32), 'W_w': jax.random.normal(ks[1], (3 * H * DH, D), dtype=jnp.float32) * s, 'W_b': jax.random.normal(ks[2], (3 * H * DH,), dtype=jnp.float32) * s, 'out_w': jax.random.normal(ks[3], (D, H * DH), dtype=jnp.float32) * s, 'out_b': jax.random.normal(ks[4], (D,), dtype=jnp.float32) * s}
    _L0_attn_in = _L0_attn_setup()

    def _L0_ffn_setup():
        import jax, jax.numpy as jnp
        import numpy as np
        key = jax.random.key(seed)
        kx, kw = jax.random.split(key)
        x = jax.random.normal(kx, (32, 512, 128), dtype=jnp.float32)
        weight = jax.random.normal(kw, (128, 128), dtype=jnp.float32) * 0.01
        return {'x': x, 'weight': weight}
    _L0_ffn_in = _L0_ffn_setup()

    def _L1_attn_setup():
        import jax, jax.numpy as jnp
        import numpy as np
        from jax import lax
        D_MODEL = 128
        N_LAYERS = 4
        D_STATE = 16
        EXPAND = 2
        D_CONV = 4
        D_INNER = EXPAND * D_MODEL
        DT_RANK = (D_MODEL + 15) // 16
        EPS = 1e-05

        def _layernorm(x, w, b):
            mu = jnp.mean(x, -1, keepdims=True)
            var = jnp.mean(jnp.square(x - mu), -1, keepdims=True)
            return (x - mu) * lax.rsqrt(var + EPS) * w + b

        def _silu(x):
            return x * jax.nn.sigmoid(x)

        def _mamba(x, in_w, cw, cb, xp_w, dt_w, dt_b, A_log, Dp, out_w):
            B, S, _ = x.shape
            xz = jnp.einsum('bsd,ed->bse', x, in_w)
            x_in, z = jnp.split(xz, 2, axis=-1)
            xp = jnp.pad(x_in.transpose(0, 2, 1), ((0, 0), (0, 0), (D_CONV - 1, 0)))
            xc = lax.conv_general_dilated(xp, cw, (1,), 'VALID', feature_group_count=D_INNER)
            xc = _silu(xc + cb[None, :, None]).transpose(0, 2, 1)
            dbl = jnp.einsum('bsd,ed->bse', xc, xp_w)
            dtr = dbl[..., :DT_RANK]
            Bm = dbl[..., DT_RANK:DT_RANK + D_STATE]
            Cm = dbl[..., DT_RANK + D_STATE:]
            dt = jax.nn.softplus(jnp.einsum('bsr,dr->bsd', dtr, dt_w) + dt_b)
            A = -jnp.exp(A_log)

            def step(h, inp):
                dt_t, B_t, C_t, u_t = inp
                dA = jnp.exp(dt_t[..., None] * A)
                h = h * dA + (dt_t * u_t)[..., None] * B_t[:, None, :]
                y = jnp.einsum('bdn,bn->bd', h, C_t)
                return (h, y)
            h0 = jnp.zeros((B, D_INNER, D_STATE), x.dtype)
            _, ys = lax.scan(step, h0, (dt.transpose(1, 0, 2), Bm.transpose(1, 0, 2), Cm.transpose(1, 0, 2), xc.transpose(1, 0, 2)))
            y = ys.transpose(1, 0, 2) + xc * Dp
            y = y * _silu(z)
            return jnp.einsum('bse,de->bsd', y, out_w)
        key = jax.random.key(seed)
        ks = jax.random.split(key, 12)
        B, S = (2, 256)
        L = N_LAYERS
        s = lambda k, shape, sc: jax.random.normal(k, shape, jnp.float32) * sc
        inp = {'x': jax.random.normal(ks[0], (B, S, D_MODEL), jnp.float32), 'in_proj_w': s(ks[1], (L, 2 * D_INNER, D_MODEL), D_MODEL ** (-0.5)), 'conv_w': s(ks[2], (L, D_INNER, 1, D_CONV), D_CONV ** (-0.5)), 'conv_b': jnp.zeros((L, D_INNER), jnp.float32), 'x_proj_w': s(ks[3], (L, DT_RANK + 2 * D_STATE, D_INNER), D_INNER ** (-0.5)), 'dt_proj_w': s(ks[4], (L, D_INNER, DT_RANK), DT_RANK ** (-0.5)), 'dt_proj_b': jnp.full((L, D_INNER), -4.6, jnp.float32), 'A_log': jnp.tile(jnp.log(jnp.arange(1, D_STATE + 1, dtype=jnp.float32))[None, None, :], (L, D_INNER, 1)), 'D_skip': jnp.ones((L, D_INNER), jnp.float32), 'out_proj_w': s(ks[5], (L, D_MODEL, D_INNER), D_INNER ** (-0.5)), 'ln_w': jnp.ones((L, D_MODEL), jnp.float32), 'ln_b': jnp.zeros((L, D_MODEL), jnp.float32), 'fnorm_w': jnp.ones((D_MODEL,), jnp.float32), 'fnorm_b': jnp.zeros((D_MODEL,), jnp.float32)}
        return inp
    _L1_attn_in = _L1_attn_setup()

    def _L1_ffn_setup():
        import jax, jax.numpy as jnp
        import numpy as np
        DIM = 128
        EXPERT_DIM = 64
        N_EXPERTS = 16
        TOPK = 2
        SHARED_HIDDEN = EXPERT_DIM * TOPK
        B, T = (4, 128)

        def _moe_forward(x, router_w, router_bias, up_proj, gate_proj, down_proj, sh_gate, sh_up, sh_down):
            Bb, Tt, D = x.shape
            flat = x.reshape(Bb * Tt, D)
            N = flat.shape[0]
            logits = flat @ router_w.T
            topk_scores, topk_idx = jax.lax.top_k(logits + router_bias, TOPK)
            topk_scores = jax.nn.softmax(topk_scores, axis=-1)
            combine = jnp.zeros((N, N_EXPERTS), flat.dtype)
            combine = combine.at[jnp.arange(N)[:, None], topk_idx].add(topk_scores)
            up_all = jnp.einsum('nd,kde->nke', flat, up_proj)
            gate_all = jnp.einsum('nd,kde->nke', flat, gate_proj)
            hidden = jax.nn.silu(gate_all) * up_all
            down_all = jnp.einsum('nke,ked->nkd', hidden, down_proj)
            out = jnp.einsum('nk,nkd->nd', combine, down_all)
            sh_hidden = jax.nn.silu(flat @ sh_gate.T) * (flat @ sh_up.T)
            out = out + sh_hidden @ sh_down.T
            return out.reshape(Bb, Tt, D)
        key = jax.random.key(seed)
        ks = jax.random.split(key, 9)
        std = 0.02
        return {'x': jax.random.normal(ks[0], (B, T, DIM), jnp.float32), 'router_w': jax.random.normal(ks[1], (N_EXPERTS, DIM), jnp.float32) * std, 'router_bias': jnp.zeros((N_EXPERTS,), jnp.float32), 'up_proj': jax.random.normal(ks[2], (N_EXPERTS, DIM, EXPERT_DIM), jnp.float32) * std, 'gate_proj': jax.random.normal(ks[3], (N_EXPERTS, DIM, EXPERT_DIM), jnp.float32) * std, 'down_proj': jax.random.normal(ks[4], (N_EXPERTS, EXPERT_DIM, DIM), jnp.float32) * std, 'sh_gate': jax.random.normal(ks[5], (SHARED_HIDDEN, DIM), jnp.float32) * std, 'sh_up': jax.random.normal(ks[6], (SHARED_HIDDEN, DIM), jnp.float32) * std, 'sh_down': jax.random.normal(ks[7], (DIM, SHARED_HIDDEN), jnp.float32) * std}
    _L1_ffn_in = _L1_ffn_setup()

    def _L2_attn_setup():
        import jax, jax.numpy as jnp
        import numpy as np
        D_MODEL = 128
        N_HEADS = 16
        WINDOW = 64
        HEAD_DIM = D_MODEL // N_HEADS
        HALF = WINDOW // 2
        NWIN = WINDOW + 1
        LN_EPS = 1e-05

        def _layernorm(x, g, b):
            mu = jnp.mean(x, axis=-1, keepdims=True)
            var = jnp.var(x, axis=-1, keepdims=True)
            return (x - mu) * jax.lax.rsqrt(var + LN_EPS) * g + b

        def _linear_attention(q, k, v):
            q = jax.nn.elu(q) + 1.0
            k = jax.nn.elu(k) + 1.0
            kv = jnp.einsum('bsd,bse->bde', k, v)
            num = jnp.einsum('bsd,bde->bse', q, kv)
            denom = jnp.einsum('bsd,bd->bs', q, k.sum(axis=1))
            return num / (denom[..., None] + 1e-06)

        def _window_attention(q, k, v, rel_bias):
            B, S, _ = q.shape
            qh = q.reshape(B, S, N_HEADS, HEAD_DIM).transpose(0, 2, 1, 3)
            kh = k.reshape(B, S, N_HEADS, HEAD_DIM).transpose(0, 2, 1, 3)
            vh = v.reshape(B, S, N_HEADS, HEAD_DIM).transpose(0, 2, 1, 3)
            kp = jnp.pad(kh, ((0, 0), (0, 0), (HALF, HALF), (0, 0)))
            vp = jnp.pad(vh, ((0, 0), (0, 0), (HALF, HALF), (0, 0)))
            pos = jnp.arange(S)
            scale = np.float32(1.0 / np.sqrt(HEAD_DIM))

            def score_step(_, w):
                off = w - HALF
                ks = jax.lax.dynamic_slice_in_dim(kp, w, S, axis=2)
                s = jnp.einsum('bhsd,bhsd->bhs', qh, ks) * scale
                s = s + rel_bias[off + WINDOW][None, :, None]
                valid = (pos + off >= 0) & (pos + off < S)
                s = jnp.where(valid[None, None, :], s, -jnp.inf)
                return (None, s)
            _, scores = jax.lax.scan(score_step, None, jnp.arange(NWIN))
            attn = jax.nn.softmax(scores, axis=0)

            def out_step(acc, aw):
                a, w = aw
                vs = jax.lax.dynamic_slice_in_dim(vp, w, S, axis=2)
                return (acc + a[..., None] * vs, None)
            out, _ = jax.lax.scan(out_step, jnp.zeros_like(qh), (attn, jnp.arange(NWIN)))
            return out.transpose(0, 2, 1, 3).reshape(B, S, D_MODEL)
        key = jax.random.key(seed)
        ks = jax.random.split(key, 16)

        def lin(k, fan_in, shape):
            return (jax.random.normal(k, shape, jnp.float32) / np.sqrt(fan_in)).astype(jnp.float32)
        D = D_MODEL
        inp = {'x': jax.random.normal(ks[0], (2, 256, D), jnp.float32), 'wq_lin': lin(ks[1], D, (D, D)), 'bq_lin': jnp.zeros((D,), jnp.float32), 'wk_lin': lin(ks[2], D, (D, D)), 'bk_lin': jnp.zeros((D,), jnp.float32), 'wv_lin': lin(ks[3], D, (D, D)), 'bv_lin': jnp.zeros((D,), jnp.float32), 'wq_loc': lin(ks[4], D, (D, D)), 'bq_loc': jnp.zeros((D,), jnp.float32), 'wk_loc': lin(ks[5], D, (D, D)), 'bk_loc': jnp.zeros((D,), jnp.float32), 'wv_loc': lin(ks[6], D, (D, D)), 'bv_loc': jnp.zeros((D,), jnp.float32), 'wo': lin(ks[7], D, (D, D)), 'bo': jnp.zeros((D,), jnp.float32), 'wg1': lin(ks[8], 3 * D, (3 * D, D)), 'bg1': jnp.zeros((D,), jnp.float32), 'wg2': lin(ks[9], D, (D, D)), 'bg2': jnp.zeros((D,), jnp.float32), 'rel_bias': jax.random.normal(ks[10], (2 * WINDOW + 1, N_HEADS), jnp.float32), 'ln_g': jnp.ones((D,), jnp.float32), 'ln_b': jnp.zeros((D,), jnp.float32)}
        return inp
    _L2_attn_in = _L2_attn_setup()

    def _L2_ffn_setup():
        import jax, jax.numpy as jnp
        import numpy as np
        E = 16
        K = 4
        B, S, H, I = (4, 128, 128, 256)
        key = jax.random.key(seed)
        k0, k1, k2, k3 = jax.random.split(key, 4)
        scale = 0.02
        return {'hidden_states': jax.random.normal(k0, (B, S, H), jnp.float32), 'router_w': jax.random.normal(k1, (H, E), jnp.float32) * scale, 'router_b': jnp.zeros((E,), jnp.float32), 'w1': jax.random.normal(k2, (E, H, I), jnp.float32) * scale, 'b1': jnp.zeros((E, I), jnp.float32), 'w2': jax.random.normal(k3, (E, I, H), jnp.float32) * scale, 'b2': jnp.zeros((E, H), jnp.float32)}
    _L2_ffn_in = _L2_ffn_setup()

    def _L3_attn_setup():
        import jax, jax.numpy as jnp
        import numpy as np
        EPS = 1e-12
        HEADS = 16
        DIM_KEYS = 16
        DIM_VALUES = 64

        def l2norm(t):
            n = jnp.linalg.norm(t, axis=-1, keepdims=True)
            return t / jnp.maximum(n, EPS)

        def tanh_norm(t):
            n = jnp.linalg.norm(t, axis=-1, keepdims=True)
            return jnp.tanh(n) * (t / jnp.maximum(n, EPS))

        def split_heads(x, h):
            b, n, hd = x.shape
            return x.reshape(b, n, h, hd // h).transpose(0, 2, 1, 3)
        key = jax.random.key(seed)
        k1, k2, k3, k4 = jax.random.split(key, 4)
        b, n, dim = (4, 256, 128)
        dim_inner = (DIM_KEYS + DIM_VALUES) * HEADS
        tokens = jax.random.normal(k1, (b, n, dim), dtype=jnp.float32)
        Wqg = jax.random.normal(k2, (dim, dim_inner), dtype=jnp.float32) * dim ** (-0.5)
        Wkv = jax.random.normal(k3, (dim, dim_inner), dtype=jnp.float32) * dim ** (-0.5)
        Wout = jax.random.normal(k4, (DIM_VALUES * HEADS, dim), dtype=jnp.float32) * (DIM_VALUES * HEADS) ** (-0.5)
        return {'tokens': tokens, 'Wqg': Wqg, 'Wkv': Wkv, 'Wout': Wout}
    _L3_attn_in = _L3_attn_setup()

    def _L3_ffn_setup():
        import jax, jax.numpy as jnp
        import numpy as np
        GROUP = 16
        EPS = 1e-05

        def _dequant(q, scale):
            w = q.astype(jnp.float32) / 7.5 - 1.0
            return w * jnp.repeat(scale, GROUP, axis=1)

        def _qlora_linear(x, q, scale, bias, la, lb):
            w = _dequant(q, scale)
            base = jnp.einsum('btd,od->bto', x, w) + bias
            lora = jnp.einsum('btr,or->bto', jnp.einsum('btd,rd->btr', x, la), lb)
            return base + lora

        def _layernorm(x, g, b):
            mu = jnp.mean(x, axis=-1, keepdims=True)
            var = jnp.mean(jnp.square(x - mu), axis=-1, keepdims=True)
            return (x - mu) * jax.lax.rsqrt(var + EPS) * g + b
        key = jax.random.key(seed)
        ks = jax.random.split(key, 6)
        D, R, B, T = (128, 32, 8, 512)
        x = jax.random.normal(ks[0], (B, T, D), dtype=jnp.float32)
        qweights = jax.random.randint(ks[1], (6, D, D), 0, 16, dtype=jnp.int32)
        scales = jax.random.uniform(ks[2], (6, D, D // GROUP), dtype=jnp.float32)
        biases = jax.random.normal(ks[3], (6, D), dtype=jnp.float32) * 0.02
        lora_a = jax.random.normal(ks[4], (6, R, D), dtype=jnp.float32) * 0.02
        lora_b = jax.random.normal(ks[5], (6, D, R), dtype=jnp.float32) * 0.02
        ln_gamma = jnp.ones((3, D), dtype=jnp.float32)
        ln_beta = jnp.zeros((3, D), dtype=jnp.float32)
        return {'x': x, 'qweights': qweights, 'scales': scales, 'biases': biases, 'lora_a': lora_a, 'lora_b': lora_b, 'ln_gamma': ln_gamma, 'ln_beta': ln_beta}
    _L3_ffn_in = _L3_ffn_setup()
    _d = {'L0_attn_x': _L0_attn_in['x'], 'L0_attn_W_w': _L0_attn_in['W_w'], 'L0_attn_W_b': _L0_attn_in['W_b'], 'L0_attn_out_w': _L0_attn_in['out_w'], 'L0_attn_out_b': _L0_attn_in['out_b'], 'L0_ffn_weight': _L0_ffn_in['weight'], 'L1_attn_in_proj_w': _L1_attn_in['in_proj_w'], 'L1_attn_conv_w': _L1_attn_in['conv_w'], 'L1_attn_conv_b': _L1_attn_in['conv_b'], 'L1_attn_x_proj_w': _L1_attn_in['x_proj_w'], 'L1_attn_dt_proj_w': _L1_attn_in['dt_proj_w'], 'L1_attn_dt_proj_b': _L1_attn_in['dt_proj_b'], 'L1_attn_A_log': _L1_attn_in['A_log'], 'L1_attn_D_skip': _L1_attn_in['D_skip'], 'L1_attn_out_proj_w': _L1_attn_in['out_proj_w'], 'L1_attn_ln_w': _L1_attn_in['ln_w'], 'L1_attn_ln_b': _L1_attn_in['ln_b'], 'L1_attn_fnorm_w': _L1_attn_in['fnorm_w'], 'L1_attn_fnorm_b': _L1_attn_in['fnorm_b'], 'L1_ffn_router_w': _L1_ffn_in['router_w'], 'L1_ffn_router_bias': _L1_ffn_in['router_bias'], 'L1_ffn_up_proj': _L1_ffn_in['up_proj'], 'L1_ffn_gate_proj': _L1_ffn_in['gate_proj'], 'L1_ffn_down_proj': _L1_ffn_in['down_proj'], 'L1_ffn_sh_gate': _L1_ffn_in['sh_gate'], 'L1_ffn_sh_up': _L1_ffn_in['sh_up'], 'L1_ffn_sh_down': _L1_ffn_in['sh_down'], 'L2_attn_wq_lin': _L2_attn_in['wq_lin'], 'L2_attn_bq_lin': _L2_attn_in['bq_lin'], 'L2_attn_wk_lin': _L2_attn_in['wk_lin'], 'L2_attn_bk_lin': _L2_attn_in['bk_lin'], 'L2_attn_wv_lin': _L2_attn_in['wv_lin'], 'L2_attn_bv_lin': _L2_attn_in['bv_lin'], 'L2_attn_wq_loc': _L2_attn_in['wq_loc'], 'L2_attn_bq_loc': _L2_attn_in['bq_loc'], 'L2_attn_wk_loc': _L2_attn_in['wk_loc'], 'L2_attn_bk_loc': _L2_attn_in['bk_loc'], 'L2_attn_wv_loc': _L2_attn_in['wv_loc'], 'L2_attn_bv_loc': _L2_attn_in['bv_loc'], 'L2_attn_wo': _L2_attn_in['wo'], 'L2_attn_bo': _L2_attn_in['bo'], 'L2_attn_wg1': _L2_attn_in['wg1'], 'L2_attn_bg1': _L2_attn_in['bg1'], 'L2_attn_wg2': _L2_attn_in['wg2'], 'L2_attn_bg2': _L2_attn_in['bg2'], 'L2_attn_rel_bias': _L2_attn_in['rel_bias'], 'L2_attn_ln_g': _L2_attn_in['ln_g'], 'L2_attn_ln_b': _L2_attn_in['ln_b'], 'L2_ffn_router_w': _L2_ffn_in['router_w'], 'L2_ffn_router_b': _L2_ffn_in['router_b'], 'L2_ffn_w1': _L2_ffn_in['w1'], 'L2_ffn_b1': _L2_ffn_in['b1'], 'L2_ffn_w2': _L2_ffn_in['w2'], 'L2_ffn_b2': _L2_ffn_in['b2'], 'L3_attn_Wqg': _L3_attn_in['Wqg'], 'L3_attn_Wkv': _L3_attn_in['Wkv'], 'L3_attn_Wout': _L3_attn_in['Wout'], 'L3_ffn_qweights': _L3_ffn_in['qweights'], 'L3_ffn_scales': _L3_ffn_in['scales'], 'L3_ffn_biases': _L3_ffn_in['biases'], 'L3_ffn_lora_a': _L3_ffn_in['lora_a'], 'L3_ffn_lora_b': _L3_ffn_in['lora_b'], 'L3_ffn_ln_gamma': _L3_ffn_in['ln_gamma'], 'L3_ffn_ln_beta': _L3_ffn_in['ln_beta']}
    _x0 = _d['L0_attn_x']
    _d['L0_attn_x'] = jax.random.normal(jax.random.fold_in(jax.random.key(seed), 1), (8, 256, 128), dtype=_x0.dtype)
    del _x0
    return _d

def reference(L0_attn_x, L0_attn_W_w, L0_attn_W_b, L0_attn_out_w, L0_attn_out_b, L0_ffn_weight, L1_attn_in_proj_w, L1_attn_conv_w, L1_attn_conv_b, L1_attn_x_proj_w, L1_attn_dt_proj_w, L1_attn_dt_proj_b, L1_attn_A_log, L1_attn_D_skip, L1_attn_out_proj_w, L1_attn_ln_w, L1_attn_ln_b, L1_attn_fnorm_w, L1_attn_fnorm_b, L1_ffn_router_w, L1_ffn_router_bias, L1_ffn_up_proj, L1_ffn_gate_proj, L1_ffn_down_proj, L1_ffn_sh_gate, L1_ffn_sh_up, L1_ffn_sh_down, L2_attn_wq_lin, L2_attn_bq_lin, L2_attn_wk_lin, L2_attn_bk_lin, L2_attn_wv_lin, L2_attn_bv_lin, L2_attn_wq_loc, L2_attn_bq_loc, L2_attn_wk_loc, L2_attn_bk_loc, L2_attn_wv_loc, L2_attn_bv_loc, L2_attn_wo, L2_attn_bo, L2_attn_wg1, L2_attn_bg1, L2_attn_wg2, L2_attn_bg2, L2_attn_rel_bias, L2_attn_ln_g, L2_attn_ln_b, L2_ffn_router_w, L2_ffn_router_b, L2_ffn_w1, L2_ffn_b1, L2_ffn_w2, L2_ffn_b2, L3_attn_Wqg, L3_attn_Wkv, L3_attn_Wout, L3_ffn_qweights, L3_ffn_scales, L3_ffn_biases, L3_ffn_lora_a, L3_ffn_lora_b, L3_ffn_ln_gamma, L3_ffn_ln_beta):

    def _L0_attn_ref(x, W_w, W_b, out_w, out_b):
        import jax, jax.numpy as jnp
        import numpy as np
        B, N, D = (2, 256, 128)
        H, DH = (16, 64)
        b, n, _ = x.shape
        qkv = x @ W_w.T + W_b
        Q, K, V = jnp.split(qkv, 3, axis=-1)
        split_heads = lambda t: t.reshape(b, n, H, DH).transpose(0, 2, 1, 3)
        q, k, v = map(split_heads, (Q, K, V))
        scale = DH ** (-0.5)
        dots = jnp.einsum('bhik,bhjk->bhij', q, k) * scale
        attn = jax.nn.softmax(dots, axis=-1)
        out = jnp.einsum('bhij,bhjk->bhik', attn, v)
        out = out.transpose(0, 2, 1, 3).reshape(b, n, H * DH)
        return out @ out_w.T + out_b

    def _L0_ffn_ref(x, weight):
        import jax, jax.numpy as jnp
        import numpy as np
        b_weight = jnp.sign(weight)
        return jnp.einsum('bsi,oi->bso', x, b_weight)

    def _L1_attn_ref(x, in_proj_w, conv_w, conv_b, x_proj_w, dt_proj_w, dt_proj_b, A_log, D_skip, out_proj_w, ln_w, ln_b, fnorm_w, fnorm_b):
        import jax, jax.numpy as jnp
        import numpy as np
        from jax import lax
        D_MODEL = 128
        N_LAYERS = 4
        D_STATE = 16
        EXPAND = 2
        D_CONV = 4
        D_INNER = EXPAND * D_MODEL
        DT_RANK = (D_MODEL + 15) // 16
        EPS = 1e-05

        def _layernorm(x, w, b):
            mu = jnp.mean(x, -1, keepdims=True)
            var = jnp.mean(jnp.square(x - mu), -1, keepdims=True)
            return (x - mu) * lax.rsqrt(var + EPS) * w + b

        def _silu(x):
            return x * jax.nn.sigmoid(x)

        def _mamba(x, in_w, cw, cb, xp_w, dt_w, dt_b, A_log, Dp, out_w):
            B, S, _ = x.shape
            xz = jnp.einsum('bsd,ed->bse', x, in_w)
            x_in, z = jnp.split(xz, 2, axis=-1)
            xp = jnp.pad(x_in.transpose(0, 2, 1), ((0, 0), (0, 0), (D_CONV - 1, 0)))
            xc = lax.conv_general_dilated(xp, cw, (1,), 'VALID', feature_group_count=D_INNER)
            xc = _silu(xc + cb[None, :, None]).transpose(0, 2, 1)
            dbl = jnp.einsum('bsd,ed->bse', xc, xp_w)
            dtr = dbl[..., :DT_RANK]
            Bm = dbl[..., DT_RANK:DT_RANK + D_STATE]
            Cm = dbl[..., DT_RANK + D_STATE:]
            dt = jax.nn.softplus(jnp.einsum('bsr,dr->bsd', dtr, dt_w) + dt_b)
            A = -jnp.exp(A_log)

            def step(h, inp):
                dt_t, B_t, C_t, u_t = inp
                dA = jnp.exp(dt_t[..., None] * A)
                h = h * dA + (dt_t * u_t)[..., None] * B_t[:, None, :]
                y = jnp.einsum('bdn,bn->bd', h, C_t)
                return (h, y)
            h0 = jnp.zeros((B, D_INNER, D_STATE), x.dtype)
            _, ys = lax.scan(step, h0, (dt.transpose(1, 0, 2), Bm.transpose(1, 0, 2), Cm.transpose(1, 0, 2), xc.transpose(1, 0, 2)))
            y = ys.transpose(1, 0, 2) + xc * Dp
            y = y * _silu(z)
            return jnp.einsum('bse,de->bsd', y, out_w)
        for i in range(N_LAYERS):
            xn = _layernorm(x, ln_w[i], ln_b[i])
            x = _mamba(xn, in_proj_w[i], conv_w[i], conv_b[i], x_proj_w[i], dt_proj_w[i], dt_proj_b[i], A_log[i], D_skip[i], out_proj_w[i]) + x
        return x

    def _L1_ffn_ref(x, router_w, router_bias, up_proj, gate_proj, down_proj, sh_gate, sh_up, sh_down):
        import jax, jax.numpy as jnp
        import numpy as np
        DIM = 128
        EXPERT_DIM = 64
        N_EXPERTS = 16
        TOPK = 2
        SHARED_HIDDEN = EXPERT_DIM * TOPK
        B, T = (4, 128)

        def _moe_forward(x, router_w, router_bias, up_proj, gate_proj, down_proj, sh_gate, sh_up, sh_down):
            Bb, Tt, D = x.shape
            flat = x.reshape(Bb * Tt, D)
            N = flat.shape[0]
            logits = flat @ router_w.T
            topk_scores, topk_idx = jax.lax.top_k(logits + router_bias, TOPK)
            topk_scores = jax.nn.softmax(topk_scores, axis=-1)
            combine = jnp.zeros((N, N_EXPERTS), flat.dtype)
            combine = combine.at[jnp.arange(N)[:, None], topk_idx].add(topk_scores)
            up_all = jnp.einsum('nd,kde->nke', flat, up_proj)
            gate_all = jnp.einsum('nd,kde->nke', flat, gate_proj)
            hidden = jax.nn.silu(gate_all) * up_all
            down_all = jnp.einsum('nke,ked->nkd', hidden, down_proj)
            out = jnp.einsum('nk,nkd->nd', combine, down_all)
            sh_hidden = jax.nn.silu(flat @ sh_gate.T) * (flat @ sh_up.T)
            out = out + sh_hidden @ sh_down.T
            return out.reshape(Bb, Tt, D)
        return _moe_forward(x, router_w, router_bias, up_proj, gate_proj, down_proj, sh_gate, sh_up, sh_down)

    def _L2_attn_ref(x, wq_lin, bq_lin, wk_lin, bk_lin, wv_lin, bv_lin, wq_loc, bq_loc, wk_loc, bk_loc, wv_loc, bv_loc, wo, bo, wg1, bg1, wg2, bg2, rel_bias, ln_g, ln_b):
        import jax, jax.numpy as jnp
        import numpy as np
        D_MODEL = 128
        N_HEADS = 16
        WINDOW = 64
        HEAD_DIM = D_MODEL // N_HEADS
        HALF = WINDOW // 2
        NWIN = WINDOW + 1
        LN_EPS = 1e-05

        def _layernorm(x, g, b):
            mu = jnp.mean(x, axis=-1, keepdims=True)
            var = jnp.var(x, axis=-1, keepdims=True)
            return (x - mu) * jax.lax.rsqrt(var + LN_EPS) * g + b

        def _linear_attention(q, k, v):
            q = jax.nn.elu(q) + 1.0
            k = jax.nn.elu(k) + 1.0
            kv = jnp.einsum('bsd,bse->bde', k, v)
            num = jnp.einsum('bsd,bde->bse', q, kv)
            denom = jnp.einsum('bsd,bd->bs', q, k.sum(axis=1))
            return num / (denom[..., None] + 1e-06)

        def _window_attention(q, k, v, rel_bias):
            B, S, _ = q.shape
            qh = q.reshape(B, S, N_HEADS, HEAD_DIM).transpose(0, 2, 1, 3)
            kh = k.reshape(B, S, N_HEADS, HEAD_DIM).transpose(0, 2, 1, 3)
            vh = v.reshape(B, S, N_HEADS, HEAD_DIM).transpose(0, 2, 1, 3)
            kp = jnp.pad(kh, ((0, 0), (0, 0), (HALF, HALF), (0, 0)))
            vp = jnp.pad(vh, ((0, 0), (0, 0), (HALF, HALF), (0, 0)))
            pos = jnp.arange(S)
            scale = np.float32(1.0 / np.sqrt(HEAD_DIM))

            def score_step(_, w):
                off = w - HALF
                ks = jax.lax.dynamic_slice_in_dim(kp, w, S, axis=2)
                s = jnp.einsum('bhsd,bhsd->bhs', qh, ks) * scale
                s = s + rel_bias[off + WINDOW][None, :, None]
                valid = (pos + off >= 0) & (pos + off < S)
                s = jnp.where(valid[None, None, :], s, -jnp.inf)
                return (None, s)
            _, scores = jax.lax.scan(score_step, None, jnp.arange(NWIN))
            attn = jax.nn.softmax(scores, axis=0)

            def out_step(acc, aw):
                a, w = aw
                vs = jax.lax.dynamic_slice_in_dim(vp, w, S, axis=2)
                return (acc + a[..., None] * vs, None)
            out, _ = jax.lax.scan(out_step, jnp.zeros_like(qh), (attn, jnp.arange(NWIN)))
            return out.transpose(0, 2, 1, 3).reshape(B, S, D_MODEL)
        h = _layernorm(x, ln_g, ln_b)
        lin_out = _linear_attention(h @ wq_lin + bq_lin, h @ wk_lin + bk_lin, h @ wv_lin + bv_lin)
        win_out = _window_attention(h @ wq_loc + bq_loc, h @ wk_loc + bk_loc, h @ wv_loc + bv_loc, rel_bias)
        gate_in = jnp.concatenate([lin_out, win_out, h], axis=-1)
        gate = jax.nn.sigmoid(jnp.maximum(gate_in @ wg1 + bg1, 0.0) @ wg2 + bg2)
        out = gate * lin_out + (1.0 - gate) * win_out
        return out @ wo + bo + x

    def _L2_ffn_ref(hidden_states, router_w, router_b, w1, b1, w2, b2):
        import jax, jax.numpy as jnp
        import numpy as np
        E = 16
        K = 4
        B, S, H, I = (4, 128, 128, 256)
        b, s, h = hidden_states.shape
        logits = hidden_states @ router_w + router_b
        probs = jax.nn.softmax(logits, axis=-1)
        topw, topi = jax.lax.top_k(probs, K)
        topw = topw / jnp.sum(topw, axis=-1, keepdims=True)
        combine = jnp.sum(jax.nn.one_hot(topi, E, dtype=hidden_states.dtype) * topw[..., None], axis=2)
        x = hidden_states.reshape(b * s, h)
        c = combine.reshape(b * s, E)

        def body(acc, expert):
            w1e, b1e, w2e, b2e, ce = expert
            hmid = jax.nn.gelu(x @ w1e + b1e, approximate=False)
            return (acc + (hmid @ w2e + b2e) * ce[:, None], None)
        out, _ = jax.lax.scan(body, jnp.zeros_like(x), (w1, b1, w2, b2, c.T))
        return out.reshape(b, s, h)

    def _L3_attn_ref(tokens, Wqg, Wkv, Wout):
        import jax, jax.numpy as jnp
        import numpy as np
        EPS = 1e-12
        HEADS = 16
        DIM_KEYS = 16
        DIM_VALUES = 64

        def l2norm(t):
            n = jnp.linalg.norm(t, axis=-1, keepdims=True)
            return t / jnp.maximum(n, EPS)

        def tanh_norm(t):
            n = jnp.linalg.norm(t, axis=-1, keepdims=True)
            return jnp.tanh(n) * (t / jnp.maximum(n, EPS))

        def split_heads(x, h):
            b, n, hd = x.shape
            return x.reshape(b, n, h, hd // h).transpose(0, 2, 1, 3)
        qg = split_heads(tokens @ Wqg, HEADS)
        kv = split_heads(tokens @ Wkv, HEADS)
        queries, gates = (qg[..., :DIM_KEYS], qg[..., DIM_KEYS:])
        keys, values = (kv[..., :DIM_KEYS], kv[..., DIM_KEYS:])
        queries, keys, values = (l2norm(queries), l2norm(keys), l2norm(values))
        sim = jnp.einsum('bhid,bhjd->bhij', queries, keys)
        attn = jnp.square(jax.nn.relu(sim))
        aggr = jnp.einsum('bhij,bhjd->bhid', attn, values)
        out = tanh_norm(aggr) * jnp.tanh(jax.nn.silu(gates))
        b, h, n, d = out.shape
        out = out.transpose(0, 2, 1, 3).reshape(b, n, h * d)
        return out @ Wout

    def _L3_ffn_ref(x, qweights, scales, biases, lora_a, lora_b, ln_gamma, ln_beta):
        import jax, jax.numpy as jnp
        import numpy as np
        GROUP = 16
        EPS = 1e-05

        def _dequant(q, scale):
            w = q.astype(jnp.float32) / 7.5 - 1.0
            return w * jnp.repeat(scale, GROUP, axis=1)

        def _qlora_linear(x, q, scale, bias, la, lb):
            w = _dequant(q, scale)
            base = jnp.einsum('btd,od->bto', x, w) + bias
            lora = jnp.einsum('btr,or->bto', jnp.einsum('btd,rd->btr', x, la), lb)
            return base + lora

        def _layernorm(x, g, b):
            mu = jnp.mean(x, axis=-1, keepdims=True)
            var = jnp.mean(jnp.square(x - mu), axis=-1, keepdims=True)
            return (x - mu) * jax.lax.rsqrt(var + EPS) * g + b
        h = x
        for blk in range(3):
            i0, i1 = (2 * blk, 2 * blk + 1)
            y = _qlora_linear(h, qweights[i0], scales[i0], biases[i0], lora_a[i0], lora_b[i0])
            y = _layernorm(y, ln_gamma[blk], ln_beta[blk])
            y = jax.nn.gelu(y, approximate=False)
            y = _qlora_linear(y, qweights[i1], scales[i1], biases[i1], lora_a[i1], lora_b[i1])
            h = y + h
        return h
    x = L0_attn_x
    x = x + 0.5 * _L0_ffn_ref(_layernorm(x, axis=-1), L0_ffn_weight)
    x = x + _L0_attn_ref(_layernorm(x, axis=-1), L0_attn_W_w, L0_attn_W_b, L0_attn_out_w, L0_attn_out_b)
    x = x + 0.5 * _L0_ffn_ref(_layernorm(x, axis=-1), L0_ffn_weight)
    x = x + 0.5 * _L1_ffn_ref(_layernorm(x, axis=-1), L1_ffn_router_w, L1_ffn_router_bias, L1_ffn_up_proj, L1_ffn_gate_proj, L1_ffn_down_proj, L1_ffn_sh_gate, L1_ffn_sh_up, L1_ffn_sh_down)
    x = x + _L1_attn_ref(_layernorm(x, axis=-1), L1_attn_in_proj_w, L1_attn_conv_w, L1_attn_conv_b, L1_attn_x_proj_w, L1_attn_dt_proj_w, L1_attn_dt_proj_b, L1_attn_A_log, L1_attn_D_skip, L1_attn_out_proj_w, L1_attn_ln_w, L1_attn_ln_b, L1_attn_fnorm_w, L1_attn_fnorm_b)
    x = x + 0.5 * _L1_ffn_ref(_layernorm(x, axis=-1), L1_ffn_router_w, L1_ffn_router_bias, L1_ffn_up_proj, L1_ffn_gate_proj, L1_ffn_down_proj, L1_ffn_sh_gate, L1_ffn_sh_up, L1_ffn_sh_down)
    x = x + 0.5 * _L2_ffn_ref(_layernorm(x, axis=-1), L2_ffn_router_w, L2_ffn_router_b, L2_ffn_w1, L2_ffn_b1, L2_ffn_w2, L2_ffn_b2)
    x = x + _L2_attn_ref(_layernorm(x, axis=-1), L2_attn_wq_lin, L2_attn_bq_lin, L2_attn_wk_lin, L2_attn_bk_lin, L2_attn_wv_lin, L2_attn_bv_lin, L2_attn_wq_loc, L2_attn_bq_loc, L2_attn_wk_loc, L2_attn_bk_loc, L2_attn_wv_loc, L2_attn_bv_loc, L2_attn_wo, L2_attn_bo, L2_attn_wg1, L2_attn_bg1, L2_attn_wg2, L2_attn_bg2, L2_attn_rel_bias, L2_attn_ln_g, L2_attn_ln_b)
    x = x + 0.5 * _L2_ffn_ref(_layernorm(x, axis=-1), L2_ffn_router_w, L2_ffn_router_b, L2_ffn_w1, L2_ffn_b1, L2_ffn_w2, L2_ffn_b2)
    x = x + 0.5 * _L3_ffn_ref(_layernorm(x, axis=-1), L3_ffn_qweights, L3_ffn_scales, L3_ffn_biases, L3_ffn_lora_a, L3_ffn_lora_b, L3_ffn_ln_gamma, L3_ffn_ln_beta)
    x = x + _L3_attn_ref(_layernorm(x, axis=-1), L3_attn_Wqg, L3_attn_Wkv, L3_attn_Wout)
    x = x + 0.5 * _L3_ffn_ref(_layernorm(x, axis=-1), L3_ffn_qweights, L3_ffn_scales, L3_ffn_biases, L3_ffn_lora_a, L3_ffn_lora_b, L3_ffn_ln_gamma, L3_ffn_ln_beta)
    return x

_drawn_inputs = setup_inputs


def setup_inputs(seed=0):
    import zlib

    import numpy as np

    out = dict(_drawn_inputs(seed))
    spreads = {'L1_attn_conv_b': (0.0, 0.763),
     'L1_attn_dt_proj_b': (-4.599999904632568, 0.6),
     'L1_attn_D_skip': (1.0, 0.6),
     'L1_attn_ln_w': (1.0, 0.2),
     'L1_attn_ln_b': (0.0, 0.537),
     'L1_attn_fnorm_w': (1.0, 0.2),
     'L1_attn_fnorm_b': (0.0, 0.1),
     'L1_ffn_router_bias': (0.0, 0.8),
     'L2_attn_bq_lin': (0.0, 2.0),
     'L2_attn_bk_lin': (0.0, 2.0),
     'L2_attn_bv_lin': (0.0, 2.0),
     'L2_attn_bq_loc': (0.0, 2.0),
     'L2_attn_bk_loc': (0.0, 2.0),
     'L2_attn_bv_loc': (0.0, 2.0),
     'L2_attn_bo': (0.0, 2.0),
     'L2_attn_bg1': (0.0, 2.0),
     'L2_attn_bg2': (0.0, 2.0),
     'L2_attn_ln_g': (1.0, 0.6),
     'L2_attn_ln_b': (0.0, 2.0),
     'L2_ffn_router_b': (0.0, 2.0),
     'L2_ffn_b1': (0.0, 2.0),
     'L2_ffn_b2': (0.0, 2.0),
     'L3_ffn_ln_gamma': (1.0, 0.6),
     'L3_ffn_ln_beta': (0.0, 0.8)}
    factors = {'L0_attn_W_w': 8.0,
     'L0_attn_W_b': 8.0,
     'L0_attn_out_w': 8.0,
     'L0_attn_out_b': 8.0,
     'L1_attn_x_proj_w': 3.919,
     'L1_attn_dt_proj_w': 8.0,
     'L1_attn_A_log': 5.837,
     'L1_ffn_router_w': 8.0,
     'L1_ffn_up_proj': 8.0,
     'L1_ffn_gate_proj': 8.0,
     'L1_ffn_down_proj': 8.0,
     'L1_ffn_sh_gate': 8.0,
     'L1_ffn_sh_up': 8.0,
     'L1_ffn_sh_down': 8.0,
     'L2_attn_wq_lin': 64.0,
     'L2_attn_wk_lin': 64.0,
     'L2_attn_wv_lin': 40.057,
     'L2_attn_wq_loc': 25.296,
     'L2_attn_wk_loc': 24.813,
     'L2_attn_wv_loc': 18.795,
     'L2_attn_wo': 11.921,
     'L2_attn_wg1': 49.81,
     'L2_attn_wg2': 45.01,
     'L2_attn_rel_bias': 47.064,
     'L2_ffn_router_w': 64.0,
     'L2_ffn_w1': 64.0,
     'L2_ffn_w2': 64.0,
     'L3_attn_Wqg': 64.0,
     'L3_attn_Wkv': 64.0,
     'L3_attn_Wout': 64.0,
     'L3_ffn_biases': 64.0,
     'L3_ffn_lora_a': 64.0,
     'L3_ffn_lora_b': 64.0,
     'L3_ffn_scales': 8.0}
    for name, (base, spread) in spreads.items():
        noise = np.random.default_rng([zlib.crc32(name.encode()), seed]).standard_normal(out[name].shape)
        drawn = base * np.exp(spread * noise) if base else spread * noise
        out[name] = jnp.asarray(drawn.astype(out[name].dtype))
    for name, factor in factors.items():
        out[name] = (out[name] * factor).astype(out[name].dtype)
    return out
```

```python
from contextlib import ExitStack

import numpy as np

import concourse.bass as bass
from concourse import mybir

F32 = mybir.dt.float32
BF16 = mybir.dt.bfloat16
I32 = mybir.dt.int32
U32 = mybir.dt.uint32
ALU = mybir.AluOpType
ACT = mybir.ActivationFunctionType
AX_X = mybir.AxisListType.X

P = 128
B, S = 8, 256
TS = S // P
W = TS * P
EPS = 1e-5

PACKS = {
    "a0": dict(ffn=128, wq=1024, wk=1024, wv=1024, wo=1024, bq=8, bk=8, bv=1024, bo=128),
    "m1": dict(rw=16, rb=32, up=1024, gate=1024, down=1024, shg=128, shu=128, shd=128),
    "mb": {f"{n}{l}": c for l in range(4) for n, c in dict(
        taps=1024, inx=256, inz=256, cb=2, xp=208, dtw=256, dtb=2, alog=32, dsk=2,
        outw=256, lnw=1, lnb=1).items()},
    "m2": dict(rw=16, rb=32, w1=4096, b1=32, w2=4096, b2=128),
    "a2": dict(wql=128, wkl=128, wvl=128, bql=1, bkl=128, bvl=128, wq4=512, wk4=512, bq4=4, bk4=4,
               wvc=128, bvc=128, wo=128, bo=128, wg1=384, bg1=1, wg2=128, bg2=1, lng=1, lnb=1,
               band=16 * 192),
    "f3": dict(scale=768, bias=768, la=768, lb=768, gam=3, bet=3),
    "a3": dict(wq4=512, wk4=512, wg=1024, wv=1024, wo=1024),
}


def pack_width(name):
    return sum(PACKS[name].values())


def pack_offset(name, field):
    at = 0
    for f, n in PACKS[name].items():
        if f == field:
            return at, n
        at += n
    raise KeyError(field)


class Core:
    pass


def make_sems(K, stage, names):
    sems = [K.sem_scope.enter_context(K.nc.semaphore(f"{stage}_{n}")) for n in names.split()]
    K.live_sems += sems
    return sems


def clear_sems(K):
    with K.nc.Block() as block:
        @block.sync
        def _(sp):
            for sem in K.live_sems:
                sp.sem_clear(sem)
    K.live_sems = []
    K.sem_scope.close()


def field(K, pack, name):
    at, n = pack_offset(pack, name)
    return K.pack[pack][:, at:at + n]


def chain(eng, sem):
    count = [0]
    eng.sem_clear(sem)

    def link(ins):
        count[0] += 1
        ins.then_inc(sem, 1)
        eng.wait_ge(sem, count[0])
    return link



class Norm:
    def __init__(self, K, stage):
        self.stats, self.rstd, self.xn, self.xt, self.pool = make_sems(
            K, stage, "ln_stats ln_rstd ln_xn ln_transposed ln_pool_chain")
        sb = K.sb
        self.bn = sb(f"{stage}_ln_bn", [P, TS, 6])
        self.mv = sb(f"{stage}_ln_mv", [P, TS, 2])
        self.rs = sb(f"{stage}_ln_rs", [P, TS])
        self.out = sb(f"{stage}_ln_xn", [P, W])


def norm_vector(K, N, dve, link, src, n, before=None):
    for j in range(TS):
        i = dve.bn_stats(N.bn[:, j, :], src(j))
    link(i)
    for j in range(TS):
        i = dve.bn_aggr(N.mv[:, j, :], N.bn[:, j, :])
    i.then_inc(N.stats, 1)
    dve.wait_ge(N.rstd, n + 1)
    for j in range(TS):
        i = dve.tensor_scalar(N.out[:, j * P:(j + 1) * P], src(j), N.mv[:, j, 0:1], N.rs[:, j:j + 1],
                              ALU.subtract, ALU.mult)
    i.then_inc(N.xn, 1)


def norm_pool(K, N, pool, n):
    pool.wait_ge(N.stats, n + 1)
    pool.sem_inc(N.pool, 1)
    pool.tensor_scalar(N.rs[:, :], N.mv[:, :, 1], EPS, None, ALU.add).then_inc(N.pool, 1)
    pool.wait_ge(N.pool, 2 * (n + 1))
    pool.tensor_tensor(N.rs[:, :], N.rs[:, :], K.neg_half[:, 0:TS], ALU.pow).then_inc(N.rstd, 1)


def norm_tensor(K, N, pe, n, dst):
    pe.wait_ge(N.xn, n + 1)
    for j in range(TS):
        i = pe.transpose(dst[:, j * P:(j + 1) * P], N.out[:, j * P:(j + 1) * P], K.ident[:, :])
    i.then_inc(N.xt, 1)



def stage_signed_ffn(K, tag):
    nc = K.nc
    with ExitStack() as scope:
        K.scope = scope
        N = Norm(K, tag)
        xnt = K.sb(f"{tag}_xnt", [P, W])
        sgn = K.sb(f"{tag}_sign", [P, P])
        neg = K.sb(f"{tag}_negative", [P, P])
        link_s, xnt_ready, prod, done = make_sems(K, tag, "dve_chain xnt_ready product_ready seq_done")
        with nc.Block() as block:
            K.start_loads(block, tag)

            @block.vector
            def _(dve):
                dve.sem_inc(done, 1)
                link = chain(dve, link_s)
                dve.wait_ge(K.loaded["a0"], 16)
                w = field(K, "a0", "ffn")
                link(dve.tensor_scalar(neg[:, :], w, 0.0, None, ALU.is_lt))
                link(dve.scalar_tensor_tensor(sgn[:, :], w, 0.0, neg[:, :], ALU.is_gt, ALU.subtract))
                with dve.Fori(0, B) as s:
                    link = chain(dve, link_s)
                    norm_vector(K, N, dve, link, lambda j: K.x[:, bass.ds(s * W + j * P, P)], s)
                    dve.wait_ge(N.xt, s + 1)
                    dve.tensor_copy(xnt[:, :], K.ps[0][:, 0:W]).then_inc(xnt_ready, 1)
                    dve.wait_ge(prod, s + 1)
                    xs = K.x[:, bass.ds(s * W, W)]
                    dve.scalar_tensor_tensor(xs, K.ps[1][:, 0:W], 0.5, xs, ALU.mult, ALU.add).then_inc(done, 1)

            @block.gpsimd
            def _(pool):
                with pool.Fori(0, B) as s:
                    norm_pool(K, N, pool, s)

            @block.tensor
            def _(pe):
                pe.wait_ge(K.consts_ready, K.N_CONST)
                with pe.Fori(0, B) as s:
                    norm_tensor(K, N, pe, s, K.ps[0])
                    pe.wait_ge(xnt_ready, s + 1)
                    pe.wait_ge(done, s + 1)
                    for j in range(TS):
                        i = pe.matmul(K.ps[1][:, j * P:(j + 1) * P], xnt[:, j * P:(j + 1) * P], sgn[:, :],
                                      start=True, stop=True)
                    i.then_inc(prod, 1)



def stage_softmax_attention(K, tag):
    nc = K.nc
    H, DH = 16, 64
    G = H // 2
    with ExitStack() as scope:
        K.scope = scope
        sb = K.sb
        N = Norm(K, tag)
        xnt = sb(f"{tag}_xnt", [P, W])
        v = sb(f"{tag}_v", [P, TS, H * DH])
        qt = sb(f"{tag}_qt", [P, 2, S])
        kt = sb(f"{tag}_kt", [P, 2, S])
        nmax = sb(f"{tag}_nmax", [P, H, TS])
        rsum = sb(f"{tag}_rsum", [P, H, TS])
        rinv = sb(f"{tag}_rinv", [P, H, TS])
        probs = sb(f"{tag}_probs", [P, 3, TS, S])
        probst = sb(f"{tag}_probst", [P, 2, TS * S])
        outt = sb(f"{tag}_outt", [P, G, S])
        (link_s, xnt_ready, v_ps, v_ready, qk_ps, qk_ready, sc_ready, max_ready, exp_ready,
         inv_ready, norm_ready, pt_ps, pt_ready, o_ps, o_ready, y_ps, done, pool_step) = make_sems(
            K, tag, "dve_chain xnt_ready v_product v_ready qk_product qk_ready scores_ready max_ready "
                    "exp_ready inv_ready probs_ready probst_product probst_ready out_product out_ready "
                    "y_product seq_done pool_step")
        wq, wk, wv, wo = (field(K, "a0", n) for n in ("wq", "wk", "wv", "wo"))
        bq, bk, bv, bo = (field(K, "a0", n) for n in ("bq", "bk", "bv", "bo"))
        STEPS = H + 3
        with nc.Block() as block:
            K.start_loads(block, tag)

            @block.vector
            def _(dve):
                dve.sem_inc(done, 1)
                dve.wait_ge(K.loaded["a0"], 16)
                with dve.Fori(0, B) as s:
                    link = chain(dve, link_s)
                    norm_vector(K, N, dve, link, lambda j: K.x[:, bass.ds(s * W + j * P, P)], s)
                    dve.wait_ge(N.xt, s + 1)
                    dve.tensor_copy(xnt[:, :], K.ps[0][:, 0:W]).then_inc(xnt_ready, 1)
                    for n in range(4):
                        j, c = n // 2, n % 2
                        dve.wait_ge(v_ps, s * 4 + n + 1)
                        dve.tensor_tensor(v[:, j, c * 512:(c + 1) * 512], K.ps[(1, 7)[n % 2]][:, :],
                                          bv[:, c * 512:(c + 1) * 512], ALU.add).then_inc(v_ready, 1)

                    def queries_keys(g):
                        dve.wait_ge(qk_ps, s * G + g + 1)
                        dve.tensor_scalar(qt[:, g % 2, :], K.ps[0][:, 0:S], bq[:, g:g + 1], DH ** -0.5,
                                          ALU.add, ALU.mult)
                        dve.tensor_scalar(kt[:, g % 2, :], K.ps[0][:, S:2 * S], bk[:, g:g + 1], None,
                                          ALU.add).then_inc(qk_ready, 1)

                    queries_keys(0)
                    for i in range(STEPS):
                        if i < H:
                            dve.wait_ge(sc_ready, s * H + i + 1)
                            dve.tensor_reduce(nmax[:, i, :], K.ps[2 + i % 2][:, :].rearrange("p (t k) -> p t k", t=TS),
                                              AX_X, ALU.max, negate=True).then_inc(max_ready, 1)
                        if i % 2 == 0 and i + 2 < H:
                            queries_keys(i // 2 + 1)
                        if 1 <= i <= H:
                            dve.wait_ge(exp_ready, s * H + i)
                            dve.reciprocal(rinv[:, i - 1, :], rsum[:, i - 1, :]).then_inc(inv_ready, 1)
                        if i >= 4 and i % 2 == 0:
                            g = (i - 4) // 2
                            dve.wait_ge(o_ps, s * H + 2 * g + 2)
                            dve.tensor_copy(outt[:, g, :], K.ps[6 + g % 2][:, 0:S]).then_inc(o_ready, 1)
                    xs = K.x[:, bass.ds(s * W, W)]
                    for j in range(TS):
                        xj = K.x[:, bass.ds(s * W + j * P, P)]
                        i = dve.tensor_tensor(xj, xj, bo, ALU.add)
                    link(i)
                    dve.wait_ge(y_ps, s + 1)
                    dve.tensor_tensor(xs, K.ps[1][:, 0:W], xs, ALU.add).then_inc(done, 1)

            @block.gpsimd
            def _(pool):
                with pool.Fori(0, B) as s:
                    norm_pool(K, N, pool, s)
                    for h in range(H):
                        pool.wait_ge(inv_ready, s * H + h + 1)
                        pool.sem_inc(pool_step, 1)
                        for t in range(TS):
                            i = pool.tensor_scalar(probs[:, h % 3, t, :], probs[:, h % 3, t, :],
                                                   rinv[:, h, t:t + 1], None, ALU.mult)
                        i.then_inc(norm_ready, 1)

            @block.scalar
            def _(act):
                act.wait_ge(K.loaded["a0"], 16)
                with act.Fori(0, B) as s:
                    act.wait_ge(done, s + 1)
                    for i in range(STEPS):
                        if i < H:
                            act.wait_ge(max_ready, s * H + i + 1)
                            if i >= 3:
                                act.wait_ge(pt_ps, s * H + i - 2)
                            for t in range(TS):
                                k = act.activation(probs[:, i % 3, t, :], K.ps[2 + i % 2][:, t * S:(t + 1) * S],
                                                   ACT.Exp, bias=nmax[:, i, t:t + 1],
                                                   accum_out=rsum[:, i, t:t + 1])
                            k.then_inc(exp_ready, 1)
                        if 2 <= i < H + 2:
                            h = i - 2
                            act.wait_ge(pt_ps, s * H + h + 1)
                            if h >= 2:
                                act.wait_ge(o_ps, s * H + h - 1)
                            act.activation(probst[:, h % 2, :], K.ps[4 + h % 2][:, :],
                                           ACT.Copy).then_inc(pt_ready, 1)

            @block.tensor
            def _(pe):
                pe.wait_ge(K.consts_ready, K.N_CONST)
                pe.wait_ge(K.loaded["a0"], 16)
                with pe.Fori(0, B) as s:
                    norm_tensor(K, N, pe, s, K.ps[0])
                    pe.wait_ge(xnt_ready, s + 1)
                    pe.wait_ge(done, s + 1)
                    for n in range(4):
                        j, c = n // 2, n % 2
                        if n >= 2:
                            pe.wait_ge(v_ready, s * 4 + n - 1)
                        pe.matmul(K.ps[(1, 7)[n % 2]][:, :], xnt[:, j * P:(j + 1) * P],
                                  wv[:, c * 512:(c + 1) * 512], start=True, stop=True).then_inc(v_ps, 1)

                    def project(g):
                        if g >= 1:
                            pe.wait_ge(qk_ready, s * G + g)
                        pe.matmul(K.ps[0][:, 0:S], wq[:, g * P:(g + 1) * P], xnt[:, :], start=True, stop=True)
                        pe.matmul(K.ps[0][:, S:2 * S], wk[:, g * P:(g + 1) * P], xnt[:, :],
                                  start=True, stop=True).then_inc(qk_ps, 1)

                    project(0)
                    pe.wait_ge(v_ready, s * 4 + 4)
                    for i in range(STEPS):
                        if i < H:
                            g, r = i // 2, 64 * (i % 2)
                            pe.wait_ge(qk_ready, s * G + g + 1)
                            if i >= 2:
                                pe.wait_ge(exp_ready, s * H + i - 1)
                            for t in range(TS):
                                k = pe.matmul(K.ps[2 + i % 2][:, t * S:(t + 1) * S],
                                              qt[r:r + 64, g % 2, t * P:(t + 1) * P], kt[r:r + 64, g % 2, :],
                                              start=True, stop=True)
                            k.then_inc(sc_ready, 1)
                            if i % 2 == 0 and g + 1 < G:
                                project(g + 1)
                        if 2 <= i < H + 2:
                            h = i - 2
                            pe.wait_ge(norm_ready, s * H + h + 1)
                            if h >= 2:
                                pe.wait_ge(pt_ready, s * H + h - 1)
                            for c in range(TS):
                                for t in range(TS):
                                    k = pe.transpose(K.ps[4 + h % 2][:, c * S + t * P:c * S + (t + 1) * P],
                                                     probs[:, h % 3, t, c * P:(c + 1) * P], K.ident[:, :])
                            k.then_inc(pt_ps, 1)
                        if 3 <= i:
                            h = i - 3
                            g, r = h // 2, 64 * (h % 2)
                            pe.wait_ge(pt_ready, s * H + h + 1)
                            if h % 2 == 0 and g >= 2:
                                pe.wait_ge(o_ready, s * G + g - 1)
                            for c in range(TS):
                                k = pe.matmul(K.ps[6 + g % 2][r:r + 64, 0:S], v[:, c, h * DH:(h + 1) * DH],
                                              probst[:, h % 2, c * S:(c + 1) * S], start=(c == 0), stop=(c == 1))
                            k.then_inc(o_ps, 1)
                    for j in range(TS):
                        for g in range(G):
                            if j == 0:
                                pe.wait_ge(o_ready, s * G + g + 1)
                            k = pe.matmul(K.ps[1][:, j * P:(j + 1) * P], outt[:, g, j * P:(j + 1) * P],
                                          wo[:, g * P:(g + 1) * P], start=(g == 0), stop=(g == G - 1))
                    k.then_inc(y_ps, 1)



E = 16
HI, MID, LO = 0, 32, 64
PARTS = LO + E


class Router:
    def __init__(self, K, stage, topk):
        sb = K.sb
        self.topk = topk
        self.lg_ps, self.top, self.wexp, self.comb, self.combt_ps, self.parts = make_sems(
            K, stage, "logits_product top_ready weights_exp comb_ready combt_product parts_ready")
        self.lg = sb(f"{stage}_logits", [P, TS, E])
        self.top8 = sb(f"{stage}_top8", [P, TS, 8])
        self.idx = sb(f"{stage}_idx", [P, TS, 8], U32)
        self.idxf = sb(f"{stage}_idxf", [P, TS, 8])
        self.negm = sb(f"{stage}_negmax", [P, TS])
        self.wexps = sb(f"{stage}_wexp", [P, TS, topk])
        self.wsum = sb(f"{stage}_wsum", [P, TS])
        self.winv = sb(f"{stage}_winv", [P, TS])
        self.hot = sb(f"{stage}_onehot", [P, TS, topk, E])
        self.raw = sb(f"{stage}_comb_raw", [P, TS, E])
        self.out = sb(f"{stage}_comb", [P, TS, E])
        self.t32 = sb(f"{stage}_combt", [E, W])
        self.rest = sb(f"{stage}_comb_rest", [E, W])
        self.mid = sb(f"{stage}_comb_mid", [E, W], BF16)
        self.part = sb(f"{stage}_comb_parts", [PARTS, W], BF16)


def route_tensor_logits(K, R, pe, xnt, rw):
    for j in range(TS):
        i = pe.matmul(K.ps[1][:, j * E:(j + 1) * E], xnt[:, j * P:(j + 1) * P], rw, start=True, stop=True)
    i.then_inc(R.lg_ps, 1)


def route_vector(K, R, dve, link, s, rb):
    dve.wait_ge(R.lg_ps, s + 1)
    link(dve.tensor_tensor(R.lg[:, :, :].rearrange("p t e -> p (t e)"), K.ps[1][:, 0:TS * E], rb, ALU.add))
    for j in range(TS):
        i = dve.max(R.top8[:, j, :], R.lg[:, j, :])
    link(i)
    dve.tensor_scalar(R.negm[:, :], R.top8[:, :, 0], -1.0, None, ALU.mult).then_inc(R.top, 1)
    for j in range(TS):
        i = dve.max_index(R.idx[:, j, :], R.top8[:, j, :], R.lg[:, j, :])
    link(i)
    link(dve.tensor_copy(R.idxf[:, :, :], R.idx[:, :, :]))
    dve.wait_ge(R.wexp, s + 1)
    dve.tensor_reduce(R.wsum[:, :], R.wexps[:, :, :], AX_X, ALU.add)
    for j in range(TS):
        for k in range(R.topk):
            i = dve.tensor_scalar(R.hot[:, j, k, :], K.iota16[:, :], R.idxf[:, j, k:k + 1],
                                  R.wexps[:, j, k:k + 1], ALU.is_equal, ALU.mult)
    link(i)
    dve.reciprocal(R.winv[:, :], R.wsum[:, :])
    for j in range(TS):
        i = dve.tensor_reduce(R.raw[:, j, :], R.hot[:, j, :, :].rearrange("p k e -> p e k"), AX_X, ALU.add)
    link(i)
    for j in range(TS):
        i = dve.tensor_scalar(R.out[:, j, :], R.raw[:, j, :], R.winv[:, j:j + 1], None, ALU.mult)
    i.then_inc(R.comb, 1)


def route_scalar(K, R, act, s):
    act.wait_ge(R.top, s + 1)
    for j in range(TS):
        i = act.activation(R.wexps[:, j, :], R.top8[:, j, 0:R.topk], ACT.Exp, bias=R.negm[:, j:j + 1])
    i.then_inc(R.wexp, 1)


def route_tensor_transpose(K, R, pe, s):
    pe.wait_ge(R.comb, s + 1)
    for j in range(TS):
        i = pe.transpose(K.ps[1][0:E, W + j * P:W + (j + 1) * P], R.out[:, j, :], K.ident[:, :])
    i.then_inc(R.combt_ps, 1)


def route_vector_parts(K, R, dve, link, s):
    dve.wait_ge(R.combt_ps, s + 1)
    link(dve.tensor_copy(R.t32[:, :], K.ps[1][0:E, W:2 * W]))
    link(dve.tensor_copy(R.part[HI:HI + E, :], R.t32[:, :]))
    link(dve.tensor_tensor(R.rest[:, :], R.t32[:, :], R.part[HI:HI + E, :], ALU.subtract))
    link(dve.tensor_copy(R.mid[:, :], R.rest[:, :]))
    dve.tensor_copy(R.part[MID:MID + E, :], R.mid[:, :])
    dve.tensor_tensor(R.part[LO:LO + E, :], R.rest[:, :], R.mid[:, :], ALU.subtract).then_inc(R.parts, 1)



def stage_gated_experts(K, tag):
    nc = K.nc
    G = E // 2
    with ExitStack() as scope:
        K.scope = scope
        sb = K.sb
        N = Norm(K, tag)
        R = Router(K, tag, 2)
        xnt = sb(f"{tag}_xnt", [P, W])
        act_g = sb(f"{tag}_silu", [P, 2, W])
        gated = sb(f"{tag}_gated", [P, 2, W])
        hid = sb(f"{tag}_hidden", [P, 3, W])
        (link_s, xnt_ready, gu_ps, silu_ready, c_ps, gated_ready, hid_ready, y_ps, done, down_done, zeroed) = make_sems(
            K, tag, "dve_chain xnt_ready gate_up_product silu_ready comb_product gated_ready hidden_ready "
                    "y_product seq_done down_issued parts_zeroed")
        f = lambda n: field(K, "m1", n)
        GATE = [f("gate")[:, g * P:(g + 1) * P] for g in range(G)] + [f("shg")]
        UP = [f("up")[:, g * P:(g + 1) * P] for g in range(G)] + [f("shu")]
        DOWN = [f("down")[:, g * P:(g + 1) * P] for g in range(G)] + [f("shd")]
        ORDER = [G] + list(range(G))
        NG = G + 1
        with nc.Block() as block:
            K.start_loads(block, tag)

            @block.vector
            def _(dve):
                dve.sem_inc(done, 1)
                dve.wait_ge(K.consts_ready, K.N_CONST)
                dve.wait_ge(K.loaded["m1"], 16)
                link = chain(dve, link_s)
                link(dve.memset(R.part[:, :], 0.0))
                with dve.Fori(0, B) as s:
                    link = chain(dve, link_s)
                    norm_vector(K, N, dve, link, lambda j: K.x[:, bass.ds(s * W + j * P, P)], s)
                    dve.wait_ge(N.xt, s + 1)
                    dve.tensor_copy(xnt[:, :], K.ps[0][:, 0:W]).then_inc(xnt_ready, 1)
                    route_vector(K, R, dve, link, s, f("rb"))
                    route_vector_parts(K, R, dve, link, s)
                    for n, g in enumerate(ORDER):
                        dve.wait_ge(silu_ready, s * NG + n + 1)
                        if n >= 3:
                            dve.wait_ge(down_done, s * NG + n - 2)
                        dst = hid[:, n % 3, :] if g == G else gated[:, n % 2, :]
                        i = dve.tensor_tensor(dst, act_g[:, n % 2, :], K.ps[2 + n % 2][:, W:2 * W], ALU.mult)
                        if g == G:
                            link(i)
                            dve.sem_inc(gated_ready, 1)
                            dve.sem_inc(hid_ready, 1)
                        else:
                            i.then_inc(gated_ready, 1)
                            dve.wait_ge(gated_ready, s * NG + n + 1)
                            dve.wait_ge(c_ps, s * G + n)
                            dve.tensor_tensor(hid[:, n % 3, :], gated[:, n % 2, :], K.ps[4 + n % 2][:, 0:W],
                                              ALU.mult).then_inc(hid_ready, 1)
                    dve.wait_ge(y_ps, s + 1)
                    for j in range(TS):
                        xj = K.x[:, bass.ds(s * W + j * P, P)]
                        i = dve.scalar_tensor_tensor(xj, K.ps[6 + j][:, 0:P], 0.5, xj, ALU.mult, ALU.add)
                    i.then_inc(done, 1)

            @block.gpsimd
            def _(pool):
                with pool.Fori(0, B) as s:
                    norm_pool(K, N, pool, s)

            @block.scalar
            def _(act):
                with act.Fori(0, B) as s:
                    route_scalar(K, R, act, s)
                    for n in range(NG):
                        act.wait_ge(gu_ps, s * NG + n + 1)
                        if n >= 2:
                            act.wait_ge(gated_ready, s * NG + n - 1)
                        act.activation(act_g[:, n % 2, :], K.ps[2 + n % 2][:, 0:W], ACT.Silu).then_inc(silu_ready, 1)

            @block.tensor
            def _(pe):
                pe.wait_ge(K.consts_ready, K.N_CONST)
                pe.wait_ge(K.loaded["m1"], 16)
                with pe.Fori(0, B) as s:
                    norm_tensor(K, N, pe, s, K.ps[0])
                    pe.wait_ge(xnt_ready, s + 1)
                    pe.wait_ge(done, s + 1)
                    route_tensor_logits(K, R, pe, xnt, f("rw"))

                    def gate_up(n):
                        if n >= 2:
                            pe.wait_ge(gated_ready, s * NG + n - 1)
                        pe.matmul(K.ps[2 + n % 2][:, 0:W], GATE[ORDER[n]], xnt[:, :], start=True, stop=True)
                        pe.matmul(K.ps[2 + n % 2][:, W:2 * W], UP[ORDER[n]], xnt[:, :],
                                  start=True, stop=True).then_inc(gu_ps, 1)

                    def spread(n):
                        g = ORDER[n]
                        if n >= 3:
                            pe.wait_ge(hid_ready, s * NG + n - 1)
                        pe.matmul(K.ps[4 + n % 2][:, 0:W], K.sel64[:, 2 * g * 64:(2 * g + 2) * 64],
                                  R.part[:, :], start=True, stop=True).then_inc(c_ps, 1)

                    gate_up(0)
                    gate_up(1)
                    route_tensor_transpose(K, R, pe, s)
                    pe.wait_ge(R.parts, s + 1)
                    for n in range(NG):
                        if n >= 1 and n + 1 < NG:
                            gate_up(n + 1)
                        if n + 1 < NG:
                            spread(n + 1)
                        pe.wait_ge(hid_ready, s * NG + n + 1)
                        for j in range(TS):
                            i = pe.matmul(K.ps[6 + j][:, 0:P], hid[:, n % 3, j * P:(j + 1) * P], DOWN[ORDER[n]],
                                          start=(n == 0), stop=(n == NG - 1))
                        i.then_inc(down_done, 1)
                        if n == NG - 1:
                            pe.wait_ge(down_done, s * NG + NG)
                            pe.sem_inc(y_ps, 1)



def stage_gelu_experts(K, tag):
    nc = K.nc
    with ExitStack() as scope:
        K.scope = scope
        sb = K.sb
        N = Norm(K, tag)
        R = Router(K, tag, 4)
        xnt = sb(f"{tag}_xnt", [P, W])
        gelu = sb(f"{tag}_gelu", [P, 2, 2, W])
        hid = sb(f"{tag}_hidden", [P, 3, 2, W])
        (link_s, xnt_ready, h_ps, gelu_ready, c_ps, hid_ready, y_ps, done, down_done) = make_sems(
            K, tag, "dve_chain xnt_ready hidden_product gelu_ready comb_product hidden_ready "
                    "y_product seq_done down_issued")
        f = lambda n: field(K, "m2", n)
        w1, b1, w2 = f("w1"), f("b1"), f("w2")
        with nc.Block() as block:
            K.start_loads(block, tag)

            @block.vector
            def _(dve):
                dve.sem_inc(done, 1)
                dve.wait_ge(K.consts_ready, K.N_CONST)
                dve.wait_ge(K.loaded["m2"], 16)
                link = chain(dve, link_s)
                link(dve.memset(R.part[:, :], 0.0))
                with dve.Fori(0, B) as s:
                    link = chain(dve, link_s)
                    norm_vector(K, N, dve, link, lambda j: K.x[:, bass.ds(s * W + j * P, P)], s)
                    dve.wait_ge(N.xt, s + 1)
                    dve.tensor_copy(xnt[:, :], K.ps[0][:, 0:W]).then_inc(xnt_ready, 1)
                    route_vector(K, R, dve, link, s, f("rb"))
                    route_vector_parts(K, R, dve, link, s)
                    for e in range(E):
                        dve.wait_ge(gelu_ready, s * E + e + 1)
                        dve.wait_ge(c_ps, s * E + e + 1)
                        if e >= 3:
                            dve.wait_ge(down_done, s * E + e - 2)
                        for c in range(2):
                            i = dve.tensor_tensor(hid[:, e % 3, c, :], gelu[:, e % 2, c, :], K.ps[4 + e % 2][:, 0:W],
                                                  ALU.mult)
                        i.then_inc(hid_ready, 1)
                    dve.wait_ge(y_ps, s + 1)
                    for j in range(TS):
                        xj = K.x[:, bass.ds(s * W + j * P, P)]
                        i = dve.scalar_tensor_tensor(xj, K.ps[6 + j][:, 0:P], 0.5, xj, ALU.mult, ALU.add)
                    i.then_inc(done, 1)

            @block.gpsimd
            def _(pool):
                with pool.Fori(0, B) as s:
                    norm_pool(K, N, pool, s)

            @block.scalar
            def _(act):
                act.wait_ge(K.loaded["m2"], 16)
                with act.Fori(0, B) as s:
                    route_scalar(K, R, act, s)
                    for e in range(E):
                        act.wait_ge(h_ps, s * E + e + 1)
                        if e >= 2:
                            act.wait_ge(hid_ready, s * E + e - 1)
                        for c in range(2):
                            i = act.activation(gelu[:, e % 2, c, :], K.ps[2 + e % 2][:, c * W:(c + 1) * W], ACT.Gelu,
                                               bias=b1[:, 2 * e + c:2 * e + c + 1])
                        i.then_inc(gelu_ready, 1)

            @block.tensor
            def _(pe):
                pe.wait_ge(K.consts_ready, K.N_CONST)
                pe.wait_ge(K.loaded["m2"], 16)
                with pe.Fori(0, B) as s:
                    norm_tensor(K, N, pe, s, K.ps[0])
                    pe.wait_ge(xnt_ready, s + 1)
                    pe.wait_ge(done, s + 1)
                    route_tensor_logits(K, R, pe, xnt, f("rw"))

                    def hidden(e):
                        if e >= 2:
                            pe.wait_ge(gelu_ready, s * E + e - 1)
                        for c in range(2):
                            i = pe.matmul(K.ps[2 + e % 2][:, c * W:(c + 1) * W],
                                          w1[:, e * 256 + c * P:e * 256 + (c + 1) * P], xnt[:, :],
                                          start=True, stop=True)
                        i.then_inc(h_ps, 1)

                    def spread(e):
                        if e >= 2:
                            pe.wait_ge(hid_ready, s * E + e - 1)
                        pe.matmul(K.ps[4 + e % 2][:, 0:W], K.sel[0:PARTS, e * P:(e + 1) * P], R.part[:, :],
                                  start=True, stop=True).then_inc(c_ps, 1)

                    hidden(0)
                    hidden(1)
                    route_tensor_transpose(K, R, pe, s)
                    pe.wait_ge(R.parts, s + 1)
                    for j in range(TS):
                        pe.matmul(K.ps[6 + j][:, 0:P], R.t32[:, j * P:(j + 1) * P], f("b2")[0:E, :],
                                  start=True, stop=False)
                    spread(0)
                    spread(1)
                    for e in range(E):
                        pe.wait_ge(hid_ready, s * E + e + 1)
                        if e + 2 < E:
                            hidden(e + 2)
                            spread(e + 2)
                        for c in range(2):
                            for j in range(TS):
                                i = pe.matmul(K.ps[6 + j][:, 0:P], hid[:, e % 3, c, j * P:(j + 1) * P],
                                              w2[:, (2 * e + c) * P:(2 * e + c + 1) * P],
                                              start=False, stop=(e == E - 1 and c == 1))
                        i.then_inc(down_done, 1)
                    pe.wait_ge(down_done, s * E + E)
                    pe.sem_inc(y_ps, 1)



def stage_state_space(K, tag):
    nc = K.nc
    L, NS, KC = 4, 16, 4
    C = 2
    with ExitStack() as scope:
        K.scope = scope
        sb = K.sb
        xm = sb(f"{tag}_xm", [P, B * W])
        aneg = sb(f"{tag}_a_neg", [P, L, C * NS])
        xpad = sb(f"{tag}_xn_padded", [P, KC - 1 + S])
        xc = sb(f"{tag}_conv", [P, 2, C, S])
        zs = sb(f"{tag}_gate", [P, 2, C, S])
        dt = sb(f"{tag}_dt", [P, 2, C, S])
        du = sb(f"{tag}_dt_u", [P, 2, C, S])
        part = sb(f"{tag}_bc_parts", [96, 2, S], BF16)
        rest = sb(f"{tag}_bc_rest", [96, S])
        mid = sb(f"{tag}_bc_mid", [96, S], BF16)
        dtr = sb(f"{tag}_dt_rank", [P, S])
        v = sb(f"{tag}_dt_raw", [P, C, S])
        va = sb(f"{tag}_dt_abs", [P, C, S])
        ve = sb(f"{tag}_dt_exp", [P, C, S])
        vl = sb(f"{tag}_dt_ln", [P, C, S])
        vu = sb(f"{tag}_dt_one_plus", [P, C, S])
        da = sb(f"{tag}_decay", [P, 3, C, S])
        csb = sb(f"{tag}_c_spread", [P, 3, S])
        dbu = sb(f"{tag}_dbu", [P, 2, C, S])
        h = sb(f"{tag}_state", [P, 3, C, S])
        hc = sb(f"{tag}_state_c", [P, 3, C, S])
        yf = sb(f"{tag}_y", [P, C, S])
        yg = sb(f"{tag}_y_gated", [P, C, S])

        N0 = Norm(K, f"{tag}_in")
        dve_s, exp_s, fold_s = make_sems(K, f"{tag}_in", "dve_chain a_exp folded")
        with nc.Block() as block:
            K.start_loads(block, tag)

            @block.vector
            def _(dve):
                link = chain(dve, dve_s)
                link(dve.memset(xpad[:, :], 0.0))
                with dve.Fori(0, B) as s:
                    link = chain(dve, dve_s)
                    for j in range(TS):
                        i = dve.bn_stats(N0.bn[:, j, :], K.x[:, bass.ds(s * W + j * P, P)])
                    link(i)
                    for j in range(TS):
                        i = dve.bn_aggr(N0.mv[:, j, :], N0.bn[:, j, :])
                    i.then_inc(N0.stats, 1)
                    dve.wait_ge(N0.rstd, s + 1)
                    for j in range(TS):
                        dve.tensor_scalar(xm[:, bass.ds(s * W + j * P, P)], K.x[:, bass.ds(s * W + j * P, P)],
                                          N0.mv[:, j, 0:1], N0.rs[:, j:j + 1], ALU.subtract, ALU.mult)
                dve.wait_ge(exp_s, L)
                dve.tensor_scalar(aneg[:, :, :], aneg[:, :, :], -1.0, None, ALU.mult)

            @block.gpsimd
            def _(pool):
                with pool.Fori(0, B) as s:
                    norm_pool(K, N0, pool, s)
                pool.wait_ge(K.loaded["mb"], 16)
                for l in range(L):
                    taps, inx = field(K, "mb", f"taps{l}"), field(K, "mb", f"inx{l}")
                    for k in range(KC):
                        t = taps[:, k * 256:(k + 1) * 256]
                        pool.tensor_tensor(t, t, inx, ALU.mult).then_inc(fold_s, 1)

            @block.scalar
            def _(act):
                act.wait_ge(K.loaded["mb"], 16)
                for l in range(L):
                    act.activation(aneg[:, l, :], field(K, "mb", f"alog{l}"), ACT.Exp).then_inc(exp_s, 1)

        clear_sems(K)
        for l in range(L):
            state_space_layer(K, f"{tag}{l}", l, dict(locals()))
            clear_sems(K)
        add_s, = make_sems(K, tag, "added")
        with nc.Block() as block:
            @block.vector
            def _(dve):
                dve.tensor_tensor(K.x[:, :], K.x[:, :], xm[:, :], ALU.add).then_inc(add_s, 1)
                dve.wait_ge(add_s, 1)


def state_space_layer(K, tag, l, m):
    nc = K.nc
    NS, KC, C = m["NS"], m["KC"], m["C"]
    (xm, aneg, xpad, xc, zs, dt, du, part, rest, mid, dtr, v, va, ve, vl, vu, da, csb, dbu, h, hc, yf, yg) = (
        m[n] for n in "xm aneg xpad xc zs dt du part rest mid dtr v va ve vl vu da csb dbu h hc yf yg".split())
    f = lambda n: field(K, "mb", f"{n}{l}")
    with ExitStack() as scope:
        K.scope = scope
        N = Norm(K, tag)
        (dve_s, act_s, pool_s, xn_ready, xin_ps, z_ps, xc_ready, z_ready, bc_ps, part_ready, dtr_ready, dt_ps,
         v_ready, ln_ready, dt_ready, du_ready, b_ps, c_ps, c_ready, da_ready, h_ready, hc_ready, sum_done,
         yg_ready, out_ps, done, b_used, pool_hold, states_done) = make_sems(
            K, tag, "dve_chain act_chain pool_chain xn_ready conv_product gate_product conv_ready gate_ready "
                    "bc_product parts_ready dt_rank_ready dt_product dt_raw_ready ln_ready dt_ready dtu_ready "
                    "b_spread c_spread c_ready decay_ready state_ready state_c_ready sum_issued y_gated_ready "
                    "out_product seq_done b_used pool_hold states_done")
        AT_NORM, AT_IN, AT_SILU, AT_BC, AT_DT, AT_LN, AT_DU = 0, 2, 4, 6, 8, 9, 11

        def over_sequences(eng, prepare, main):
            prepare(0, 0, range(NS))
            with eng.Fori(0, B - 2, 2) as s:
                for q in range(2):
                    main(s + q, q, True)
            main(B - 2, 0, True)
            main(B - 1, 1, False)

        with nc.Block() as block:
            @block.vector
            def _(dve):
                dve.sem_inc(done, 1)
                def prepare(s, q, places):
                    for n in places:
                        if n == AT_NORM:
                            link = chain(dve, dve_s)
                            norm_vector(K, N, dve, link, lambda j: xm[:, bass.ds(s * W + j * P, P)], s)
                        if n == AT_BC:
                            link = chain(dve, dve_s)
                            dve.wait_ge(bc_ps, s + 1)
                            link(dve.tensor_copy(part[:, q, :], K.ps[0][0:96, 0:S]))
                            link(dve.tensor_tensor(rest[:, :], K.ps[0][0:96, 0:S], part[:, q, :], ALU.subtract))
                            link(dve.tensor_copy(mid[:, :], rest[:, :]))
                            dve.tensor_copy(part[32:64, q, :], mid[32:64, :]).then_inc(part_ready, 1)
                            dve.tensor_tensor(part[64:96, q, :], rest[64:96, :], mid[64:96, :],
                                              ALU.subtract).then_inc(part_ready, 1)

                def main(s, q, nxt):
                    dve.wait_ge(du_ready, s + 1)
                    for n in range(NS):
                        dve.wait_ge(b_ps, s * NS + n + 1)
                        for c in range(C):
                            i = dve.tensor_tensor(dbu[:, n % 2, c, :], du[:, q, c, :], K.ps[2 + n % 2][:, 0:S],
                                                  ALU.mult)
                        i.then_inc(b_used, 1)
                        for c in range(C):
                            dve.wait_ge(da_ready, (s * NS + n) * C + c + 1)
                            if c == 0:
                                dve.wait_ge(b_used, s * NS + n + 1)
                                if n == 0:
                                    dve.wait_ge(states_done, s + 1)
                                if n >= 3:
                                    dve.wait_ge(hc_ready, (s * NS + n - 2) * C)
                            dve.tensor_tensor_scan(h[:, n % 3, c, :], da[:, n % 3, c, :], dbu[:, n % 2, c, :],
                                                   0.0, ALU.mult, ALU.add).then_inc(h_ready, 1)
                        if nxt:
                            prepare(s + 1, 1 - q, [n])
                    link = chain(dve, dve_s)
                    dve.wait_ge(sum_done, (s + 1) * NS)
                    for c in range(C):
                        i = dve.scalar_tensor_tensor(yf[:, c, :], xc[:, q, c, :], f("dsk")[:, c:c + 1],
                                                     K.ps[6 + c][:, 0:S], ALU.mult, ALU.add)
                    link(i)
                    dve.tensor_tensor(yg[:, :, :], yf[:, :, :], zs[:, q, :, :], ALU.mult).then_inc(yg_ready, 1)
                    dve.wait_ge(out_ps, s + 1)
                    xs = xm[:, bass.ds(s * W, W)]
                    dve.tensor_tensor(xs, K.ps[0][:, 0:W], xs, ALU.add).then_inc(done, 1)
                dve.sem_inc(states_done, 1)
                over_sequences(dve, prepare, main)

            @block.gpsimd
            def _(pool):
                def prepare(s, q, places):
                    for n in places:
                        if n == AT_NORM:
                            norm_pool(K, N, pool, s)
                        if n == AT_DU:
                            pool.wait_ge(ln_ready, s + 1)
                            pool.sem_inc(pool_hold, 1)
                            pool.sem_clear(pool_s)
                            pool.tensor_tensor(vu[:, :, :], va[:, :, :], ve[:, :, :], ALU.subtract).then_inc(pool_s, 1)
                            pool.wait_ge(pool_s, 1)
                            pool.tensor_tensor(vl[:, :, :], vl[:, :, :], vu[:, :, :], ALU.subtract).then_inc(pool_s, 1)
                            pool.wait_ge(pool_s, 2)
                            pool.tensor_tensor(dt[:, q, :, :], v[:, :, :], vl[:, :, :], ALU.add).then_inc(dt_ready, 1)
                            pool.wait_ge(dt_ready, s + 1)
                            pool.tensor_tensor(du[:, q, :, :], dt[:, q, :, :], xc[:, q, :, :], ALU.mult).then_inc(du_ready, 1)

                def main(s, q, nxt):
                    for n in range(NS):
                        pool.wait_ge(c_ready, s * NS + n + 1)
                        if n == 0:
                            pool.wait_ge(states_done, s + 1)
                        if n >= 3:
                            pool.wait_ge(sum_done, s * NS + n - 2)
                        for c in range(C):
                            pool.wait_ge(h_ready, (s * NS + n) * C + c + 1)
                            pool.tensor_tensor(hc[:, n % 3, c, :], h[:, n % 3, c, :], csb[:, n % 3, :],
                                               ALU.mult).then_inc(hc_ready, 1)
                        if nxt:
                            prepare(s + 1, 1 - q, [n])
                over_sequences(pool, prepare, main)

            @block.scalar
            def _(act):
                def prepare(s, q, places):
                    for n in places:
                        if n == AT_IN:
                            act.wait_ge(N.xt, s + 1)
                            act.activation(xpad[:, KC - 1:KC - 1 + S], K.ps[0][:, 0:S], ACT.Identity,
                                           bias=f("lnb"), scale=f("lnw")).then_inc(xn_ready, 1)
                        if n == AT_SILU:
                            act.wait_ge(xin_ps, s + 1)
                            for c in range(C):
                                i = act.activation(xc[:, q, c, :], K.ps[0][:, c * S:(c + 1) * S], ACT.Silu,
                                                   bias=f("cb")[:, c:c + 1])
                            i.then_inc(xc_ready, 1)
                            act.wait_ge(z_ps, s + 1)
                            act.activation(zs[:, q, :, :].rearrange("p c t -> p (c t)"), K.ps[1][:, :],
                                           ACT.Silu).then_inc(z_ready, 1)
                        if n == AT_BC:
                            act.wait_ge(bc_ps, s + 1)
                            act.activation(dtr[96:104, :], K.ps[0][96:104, 0:S], ACT.Copy).then_inc(dtr_ready, 1)
                        if n == AT_LN:
                            act.sem_clear(act_s)
                            act.wait_ge(dt_ps, s + 1)
                            for c in range(C):
                                i = act.activation(v[:, c, :], K.ps[1][:, c * S:(c + 1) * S], ACT.Identity,
                                                   bias=f("dtb")[:, c:c + 1])
                            i.then_inc(v_ready, 1)
                            act.wait_ge(v_ready, s + 1)
                            act.activation(va[:, :, :], v[:, :, :], ACT.Abs).then_inc(act_s, 1)
                            act.wait_ge(act_s, 1)
                            act.activation(ve[:, :, :], va[:, :, :], ACT.Exp, scale=-1.0).then_inc(act_s, 1)
                            act.wait_ge(act_s, 2)
                            act.activation(vu[:, :, :], ve[:, :, :], ACT.Identity, bias=K.ones[:, 0:1]).then_inc(act_s, 1)
                            act.activation(v[:, :, :], v[:, :, :], ACT.Relu)
                            act.wait_ge(act_s, 3)
                            act.activation(vl[:, :, :], vu[:, :, :], ACT.Ln)
                            act.activation(va[:, :, :], vu[:, :, :], ACT.Identity,
                                           bias=K.neg_one[:, 0:1]).then_inc(ln_ready, 1)

                def main(s, q, nxt):
                    act.wait_ge(du_ready, s + 1)
                    for n in range(NS):
                        if n == 0:
                            act.wait_ge(states_done, s + 1)
                        if n >= 3:
                            act.wait_ge(h_ready, (s * NS + n - 2) * C)
                        for c in range(C):
                            act.activation(da[:, n % 3, c, :], dt[:, q, c, :], ACT.Exp,
                                           scale=aneg[:, l, c * NS + n:c * NS + n + 1]).then_inc(da_ready, 1)
                        act.wait_ge(c_ps, s * NS + n + 1)
                        if n >= 3:
                            act.wait_ge(hc_ready, (s * NS + n - 2) * C)
                        act.activation(csb[:, n % 3, :], K.ps[4 + n % 2][:, 0:S], ACT.Copy).then_inc(c_ready, 1)
                        if nxt:
                            prepare(s + 1, 1 - q, [n])
                over_sequences(act, prepare, main)

            @block.tensor
            def _(pe):
                def prepare(s, q, places):
                    for n in places:
                        if n == AT_IN:
                            norm_tensor(K, N, pe, s, K.ps[0])
                            pe.wait_ge(xn_ready, s + 1)
                            for c in range(C):
                                for k in range(KC):
                                    i = pe.matmul(K.ps[0][:, c * S:(c + 1) * S],
                                                  f("taps")[:, k * 256 + c * P:k * 256 + (c + 1) * P],
                                                  xpad[:, k:k + S], start=(k == 0), stop=(k == KC - 1))
                            i.then_inc(xin_ps, 1)
                            for c in range(C):
                                i = pe.matmul(K.ps[1][:, c * S:(c + 1) * S], f("inz")[:, c * P:(c + 1) * P],
                                              xpad[:, KC - 1:KC - 1 + S], start=True, stop=True)
                            i.then_inc(z_ps, 1)
                        if n == AT_BC:
                            pe.wait_ge(xc_ready, s + 1)
                            for c in range(C):
                                i = pe.matmul(K.ps[0][0:104, 0:S], f("xp")[:, c * 104:(c + 1) * 104],
                                              xc[:, q, c, :], start=(c == 0), stop=(c == C - 1))
                            i.then_inc(bc_ps, 1)
                        if n == AT_DT:
                            pe.wait_ge(dtr_ready, s + 1)
                            pe.wait_ge(z_ready, s + 1)
                            for c in range(C):
                                i = pe.matmul(K.ps[1][:, c * S:(c + 1) * S], f("dtw")[96:104, c * P:(c + 1) * P],
                                              dtr[96:104, :], start=True, stop=True)
                            i.then_inc(dt_ps, 1)

                def main(s, q, nxt):
                    pe.wait_ge(part_ready, 2 * (s + 1))

                    def spread(n):
                        if n >= 2:
                            pe.wait_ge(b_used, s * NS + n - 1)
                        pe.matmul(K.ps[2 + n % 2][:, 0:S], K.sel[:, n * P:(n + 1) * P], part[:, q, :],
                                  start=True, stop=True).then_inc(b_ps, 1)
                        if n >= 2:
                            pe.wait_ge(c_ready, s * NS + n - 1)
                        pe.matmul(K.ps[4 + n % 2][:, 0:S], K.sel[:, (NS + n) * P:(NS + n + 1) * P], part[:, q, :],
                                  start=True, stop=True).then_inc(c_ps, 1)

                    spread(0)
                    spread(1)
                    for n in range(NS):
                        if n == 0:
                            pe.wait_ge(done, s + 1)
                        if nxt:
                            prepare(s + 1, 1 - q, [n])
                        for c in range(C):
                            pe.wait_ge(hc_ready, (s * NS + n) * C + c + 1)
                            i = pe.matmul(K.ps[6 + c][:, 0:S], K.ident[:, :], hc[:, n % 3, c, :],
                                          start=(n == 0), stop=(n == NS - 1))
                        i.then_inc(sum_done, 1)
                        if n + 2 < NS:
                            spread(n + 2)
                    pe.wait_ge(sum_done, (s + 1) * NS)
                    pe.sem_inc(states_done, 1)
                    pe.wait_ge(yg_ready, s + 1)
                    if nxt:
                        pe.wait_ge(part_ready, 2 * (s + 2))
                        pe.wait_ge(dtr_ready, s + 2)
                    for j in range(TS):
                        for c in range(C):
                            i = pe.matmul(K.ps[0][:, j * P:(j + 1) * P], yg[:, c, j * P:(j + 1) * P],
                                          f("outw")[:, c * P:(c + 1) * P], start=(c == 0), stop=(c == C - 1))
                    i.then_inc(out_ps, 1)
                over_sequences(pe, prepare, main)



def stage_window_linear_attention(K, tag):
    nc = K.nc
    H, DH, HALF = 16, 8, 32
    G, KW = 4, 160
    KEY0 = (0, S - KW)
    BAND0 = (HALF, 0)
    BW = P + 2 * HALF
    SCALE = float(np.float32(1.0 / np.sqrt(DH)))
    with ExitStack() as scope:
        K.scope = scope
        sb = K.sb
        N = Norm(K, f"{tag}_a")
        M = Norm(K, f"{tag}_b")
        ht = sb(f"{tag}_ht", [P, W])
        band = field(K, "a2", "band").rearrange("p (h j) -> p h j", h=H)
        qmin = sb(f"{tag}_qmin", [P, S])
        qmax = sb(f"{tag}_qmax", [P, S])
        ql = sb(f"{tag}_ql", [P, S])
        klin = sb(f"{tag}_klin", [P, TS, P])
        kmin = sb(f"{tag}_kmin", [P, TS, P])
        kl = sb(f"{tag}_kl", [P, TS, P])
        vo = sb(f"{tag}_v_ones", [P, TS, 2 * P])
        kvs = sb(f"{tag}_kv_ksum", [P, 2 * P])
        den = sb(f"{tag}_den", [P, S])
        dinv = sb(f"{tag}_dinv", [P, S])
        lint = sb(f"{tag}_lin_t", [P, S])
        q4 = sb(f"{tag}_q4", [P, G, S])
        k4 = sb(f"{tag}_k4", [P, G, S])
        vw = sb(f"{tag}_v_window", [P, TS, P])
        vtail = sb(f"{tag}_v_tail", [HALF, P])
        sc = sb(f"{tag}_scores", [P, 2, TS, KW])
        mx = sb(f"{tag}_max", [P, H, TS])
        nmx = sb(f"{tag}_nmax", [P, H, TS])
        rsum = sb(f"{tag}_rsum", [P, TS, H])
        rinv = sb(f"{tag}_rinv", [P, TS, H])
        pr = sb(f"{tag}_probs", [P, 3, TS, KW])
        pt = sb(f"{tag}_probst", [P, 2, 2, TS * P])
        win = sb(f"{tag}_win", [P, TS, P])
        wint = sb(f"{tag}_win_t", [P, S])
        g1 = sb(f"{tag}_gate1", [P, S])
        gate = sb(f"{tag}_gate", [P, S])
        diff = sb(f"{tag}_diff", [P, S])
        gd = sb(f"{tag}_gate_diff", [P, S])
        ot = sb(f"{tag}_out_t", [P, S])
        (dve_s, masked, ht_ready, ql_ps, qmin_ready, qexp_ready, kv_ps, kmin_ready, kexp_ready, kl_ready, kvs_ps,
         kvs_ready, lin_ps, lin_ready, qk_ps, qk_ready, v_ps, v_ready, sc_ps, max_ready, exp_ready, pt_ps, pt_ready,
         o_ps, win_ready, wint_ps, wint_ready, g1_ps, g1_ready, g2_ps, gate_ready, ot_ready, y_ps, done,
         hold) = make_sems(
            K, tag, "dve_chain band_masked ht_ready ql_product qmin_ready qexp_ready kv_product kmin_ready "
                    "kexp_ready kl_ready kv_sum_product kv_sum_ready lin_product lin_ready qk_product qk_ready "
                    "v_product v_ready scores_product max_ready exp_ready probst_product probst_ready out_product "
                    "win_ready wint_product wint_ready gate1_product gate1_ready gate2_product gate_ready "
                    "mix_ready y_product seq_done hold")
        f = lambda n: field(K, "a2", n)
        STEPS = H + 3
        at, _ = pack_offset("a2", "wkl")
        wkv = K.pack["a2"][:, at:at + 2 * P]
        at, _ = pack_offset("a2", "bkl")
        bkv = K.pack["a2"][:, at:at + 2 * P]
        with nc.Block() as block:
            K.start_loads(block, tag)

            @block.vector
            def _(dve):
                dve.sem_inc(done, 1)
                dve.wait_ge(K.loaded["a2"], 16)
                link = chain(dve, dve_s)
                link(dve.memset(vo[:, :, :], 1.0))
                dve.wait_ge(masked, 2)
                with dve.Fori(0, B) as s:
                    link = chain(dve, dve_s)
                    norm_vector(K, N, dve, link, lambda j: K.x[:, bass.ds(s * W + j * P, P)], s)
                    dve.wait_ge(N.xn, s + 1)
                    norm_vector(K, M, dve, link, lambda j: N.out[:, j * P:(j + 1) * P], s)
                    dve.wait_ge(ql_ps, s + 1)
                    dve.tensor_scalar(qmin[:, :], K.ps[1][:, 0:S], f("bql"), 0.0, ALU.add, ALU.min).then_inc(qmin_ready, 1)
                    link(dve.tensor_scalar(qmax[:, :], K.ps[1][:, 0:S], f("bql"), 0.0, ALU.add, ALU.max))
                    dve.wait_ge(kv_ps, s + 1)
                    for j in range(TS):
                        dve.tensor_tensor(klin[:, j, :], K.ps[7][:, j * W:j * W + P], bkv[:, 0:P], ALU.add)
                        i = dve.tensor_tensor(vo[:, j, 0:P], K.ps[7][:, j * W + P:(j + 1) * W], bkv[:, P:2 * P], ALU.add)
                    link(i)
                    dve.tensor_scalar(kmin[:, :, :], klin[:, :, :], 0.0, None, ALU.min).then_inc(kmin_ready, 1)
                    dve.wait_ge(kexp_ready, s + 1)
                    dve.scalar_tensor_tensor(kl[:, :, :], klin[:, :, :], 0.0, kmin[:, :, :], ALU.max, ALU.add)\
                       .then_inc(kl_ready, 1)
                    dve.tensor_tensor(ql[:, :], qmax[:, :], qmin[:, :], ALU.add).then_inc(kl_ready, 1)
                    for g in range(G):
                        dve.wait_ge(qk_ps, s * G + g + 1)
                        bank = K.ps[(1, 6)[g % 2]]
                        dve.tensor_scalar(q4[:, g, :], bank[:, 0:S], f("bq4")[:, g:g + 1], SCALE, ALU.add, ALU.mult)
                        dve.tensor_scalar(k4[:, g, :], bank[:, S:2 * S], f("bk4")[:, g:g + 1], None,
                                          ALU.add).then_inc(qk_ready, 1)
                    dve.wait_ge(v_ps, s + 1)
                    for j in range(TS):
                        dve.tensor_tensor(vw[:, j, :], K.ps[7][:, j * P:(j + 1) * P], f("bvc"), ALU.add)
                    dve.tensor_tensor(vtail[:, :], K.ps[7][0:HALF, 2 * P:3 * P], f("bvc")[0:HALF, :],
                                      ALU.add).then_inc(v_ready, 1)

                    for i in range(STEPS):
                        if i < H:
                            dve.wait_ge(sc_ps, s * H + i + 1)
                            if i >= 2:
                                dve.wait_ge(exp_ready, s * H + i - 1)
                            dve.sem_inc(hold, 1)
                            for t in range(TS):
                                k = dve.tensor_tensor_reduce(
                                    sc[:, i % 2, t, :], K.ps[2 + i % 2][:, t * KW:(t + 1) * KW],
                                    band[:, i, BAND0[t]:BAND0[t] + KW], 1.0, -3e38, ALU.add, ALU.max, mx[:, i, t:t + 1])
                            link(k)
                            dve.tensor_scalar(nmx[:, i, :], mx[:, i, :], -1.0, None, ALU.mult).then_inc(max_ready, 1)
                        if i == 4:
                            dve.wait_ge(kvs_ps, s + 1)
                            dve.tensor_copy(kvs[:, :], K.ps[0][:, 0:2 * P]).then_inc(kvs_ready, 1)
                        if i == 8:
                            dve.wait_ge(lin_ps, s + 1)
                            link(dve.tensor_scalar(den[:, :], K.ps[0][:, S:2 * S], 1e-6, None, ALU.add))
                            link(dve.reciprocal(dinv[:, :], den[:, :]))
                            dve.tensor_tensor(lint[:, :], K.ps[0][:, 0:S], dinv[:, :], ALU.mult).then_inc(lin_ready, 1)
                    dve.wait_ge(exp_ready, s * H + H)
                    link(dve.reciprocal(rinv[:, :, :], rsum[:, :, :]))
                    dve.wait_ge(o_ps, s * H + H)
                    for j in range(TS):
                        i = dve.tensor_tensor(win[:, j, :].rearrange("p (h d) -> p h d", h=H),
                                              K.ps[6][:, j * P:(j + 1) * P].rearrange("p (h d) -> p h d", h=H),
                                              rinv[:, j, :].unsqueeze(2).broadcast_to([P, H, DH]), ALU.mult)
                    i.then_inc(win_ready, 1)
                    dve.wait_ge(wint_ps, s + 1)
                    dve.tensor_copy(wint[:, :], K.ps[7][:, 0:S]).then_inc(wint_ready, 1)
                    dve.wait_ge(wint_ready, s + 1)
                    link(dve.tensor_tensor(diff[:, :], lint[:, :], wint[:, :], ALU.subtract))
                    dve.wait_ge(gate_ready, s + 1)
                    link(dve.tensor_tensor(gd[:, :], gate[:, :], diff[:, :], ALU.mult))
                    dve.tensor_tensor(ot[:, :], gd[:, :], wint[:, :], ALU.add).then_inc(ot_ready, 1)
                    xs = K.x[:, bass.ds(s * W, W)]
                    link(dve.tensor_tensor(xs, xs, N.out[:, :], ALU.add))
                    for j in range(TS):
                        xj = K.x[:, bass.ds(s * W + j * P, P)]
                        i = dve.tensor_tensor(xj, xj, f("bo"), ALU.add)
                    link(i)
                    dve.wait_ge(y_ps, s + 1)
                    dve.tensor_tensor(xs, K.ps[0][:, 0:W], xs, ALU.add).then_inc(done, 1)

            @block.gpsimd
            def _(pool):
                pool.wait_ge(K.loaded["a2"], 16)
                pool.affine_select(out=band, in_=band, compare_op=ALU.is_ge, fill=-1e30, base=0,
                                   pattern=[[0, H], [1, BW]], channel_multiplier=-1).then_inc(masked, 1)
                pool.wait_ge(masked, 1)
                pool.affine_select(out=band, in_=band, compare_op=ALU.is_ge, fill=-1e30, base=2 * HALF,
                                   pattern=[[0, H], [-1, BW]], channel_multiplier=1).then_inc(masked, 1)
                with pool.Fori(0, B) as s:
                    norm_pool(K, N, pool, s)
                    norm_pool(K, M, pool, s)

            @block.scalar
            def _(act):
                act.wait_ge(K.loaded["a2"], 16)
                with act.Fori(0, B) as s:
                    act.wait_ge(M.xt, s + 1)
                    act.activation(ht[:, :], K.ps[0][:, 0:W], ACT.Identity, bias=f("lnb"), scale=f("lng")).then_inc(ht_ready, 1)
                    act.wait_ge(qmin_ready, s + 1)
                    act.activation(qmin[:, :], qmin[:, :], ACT.Exp)
                    act.wait_ge(kmin_ready, s + 1)
                    act.activation(kmin[:, :, :], kmin[:, :, :], ACT.Exp).then_inc(kexp_ready, 1)
                    for i in range(STEPS):
                        if i < H:
                            act.wait_ge(max_ready, s * H + i + 1)
                            if i >= 3:
                                act.wait_ge(pt_ps, s * H + i - 2)
                            for t in range(TS):
                                k = act.activation(pr[:, i % 3, t, :], sc[:, i % 2, t, :], ACT.Exp,
                                                   bias=nmx[:, i, t:t + 1], accum_out=rsum[:, t, i:i + 1])
                            k.then_inc(exp_ready, 1)
                        if 2 <= i < H + 2:
                            h = i - 2
                            act.wait_ge(pt_ps, s * H + h + 1)
                            if h >= 2:
                                act.wait_ge(o_ps, s * H + h - 1)
                            act.activation(pt[:, h % 2, 0, :], K.ps[4 + h % 2][:, 0:W], ACT.Copy)
                            act.activation(pt[0:HALF, h % 2, 1, :], K.ps[4 + h % 2][0:HALF, W:2 * W],
                                           ACT.Copy).then_inc(pt_ready, 1)
                    act.wait_ge(g1_ps, s + 1)
                    act.activation(g1[:, :], K.ps[7][:, S:2 * S], ACT.Relu, bias=f("bg1")).then_inc(g1_ready, 1)
                    act.wait_ge(g2_ps, s + 1)
                    act.activation(gate[:, :], K.ps[1][:, 0:S], ACT.Sigmoid, bias=f("bg2")).then_inc(gate_ready, 1)

            @block.tensor
            def _(pe):
                pe.wait_ge(K.consts_ready, K.N_CONST)
                pe.wait_ge(K.loaded["a2"], 16)
                with pe.Fori(0, B) as s:
                    norm_tensor(K, M, pe, s, K.ps[0])
                    pe.wait_ge(ht_ready, s + 1)
                    pe.wait_ge(done, s + 1)
                    pe.matmul(K.ps[1][:, 0:S], f("wql"), ht[:, :], start=True, stop=True).then_inc(ql_ps, 1)
                    for j in range(TS):
                        i = pe.matmul(K.ps[7][:, j * W:(j + 1) * W], ht[:, j * P:(j + 1) * P], wkv, start=True, stop=True)
                    i.then_inc(kv_ps, 1)
                    for g in range(G):
                        bank = K.ps[(1, 6)[g % 2]]
                        if g == 0:
                            pe.wait_ge(kmin_ready, s + 1)
                        if g >= 2:
                            pe.wait_ge(qk_ready, s * G + g - 1)
                        pe.matmul(bank[:, 0:S], f("wq4")[:, g * P:(g + 1) * P], ht[:, :], start=True, stop=True)
                        pe.matmul(bank[:, S:2 * S], f("wk4")[:, g * P:(g + 1) * P], ht[:, :],
                                  start=True, stop=True).then_inc(qk_ps, 1)
                    for j in range(TS):
                        pe.matmul(K.ps[7][:, j * P:(j + 1) * P], ht[:, j * P:(j + 1) * P], f("wvc"), start=True, stop=True)
                    pe.matmul(K.ps[7][0:HALF, 2 * P:3 * P], ht[:, P - HALF:P], f("wvc"),
                              start=True, stop=True).then_inc(v_ps, 1)
                    pe.wait_ge(kl_ready, 2 * (s + 1))
                    for j in range(TS):
                        i = pe.matmul(K.ps[0][:, 0:2 * P], kl[:, j, :], vo[:, j, :], start=(j == 0), stop=(j == TS - 1))
                    i.then_inc(kvs_ps, 1)
                    pe.wait_ge(v_ready, s + 1)
                    pe.wait_ge(qk_ready, s * G + G)
                    for i in range(STEPS):
                        if i < H:
                            g, r = i // 4, 32 * (i % 4)
                            if i >= 2:
                                pe.wait_ge(max_ready, s * H + i - 1)
                            for t in range(TS):
                                k = pe.matmul(K.ps[2 + i % 2][:, t * KW:(t + 1) * KW],
                                              q4[r:r + 32, g, t * P:(t + 1) * P], k4[r:r + 32, g, KEY0[t]:KEY0[t] + KW],
                                              start=True, stop=True)
                            k.then_inc(sc_ps, 1)
                        if i == 6:
                            pe.wait_ge(kvs_ready, s + 1)
                            pe.matmul(K.ps[0][:, 0:S], kvs[:, 0:P], ql[:, :], start=True, stop=True)
                            pe.matmul(K.ps[0][:, S:2 * S], kvs[:, P:2 * P], ql[:, :], start=True, stop=True).then_inc(lin_ps, 1)
                        if 2 <= i < H + 2:
                            h = i - 2
                            pe.wait_ge(exp_ready, s * H + h + 1)
                            if h >= 2:
                                pe.wait_ge(pt_ready, s * H + h - 1)
                            bank, pb = K.ps[4 + h % 2], pr[:, h % 3, :, :]
                            pe.transpose(bank[:, 0:P], pb[:, 0, 0:P], K.ident[:, :])
                            pe.transpose(bank[:, P:2 * P], pb[:, 1, HALF:KW], K.ident[:, :])
                            pe.transpose(bank[0:HALF, 2 * P:3 * P], pb[:, 0, P:KW], K.ident[:, :])
                            pe.transpose(bank[0:HALF, 3 * P:4 * P], pb[:, 1, 0:HALF], K.ident[:, :]).then_inc(pt_ps, 1)
                        if 3 <= i:
                            h = i - 3
                            pe.wait_ge(pt_ready, s * H + h + 1)
                            c = slice(h * DH, (h + 1) * DH)
                            for t in range(TS):
                                o = K.ps[6][:, t * P + h * DH:t * P + (h + 1) * DH]
                                pe.matmul(o, pt[:, h % 2, 0, t * P:(t + 1) * P], vw[:, t, c], start=True, stop=False)
                                k = pe.matmul(o, pt[0:HALF, h % 2, 1, t * P:(t + 1) * P],
                                              vw[0:HALF, 1, c] if t == 0 else vtail[:, c], start=False, stop=True)
                            k.then_inc(o_ps, 1)
                    pe.wait_ge(win_ready, s + 1)
                    for j in range(TS):
                        i = pe.transpose(K.ps[7][:, j * P:(j + 1) * P], win[:, j, :], K.ident[:, :])
                    i.then_inc(wint_ps, 1)
                    pe.wait_ge(lin_ready, s + 1)
                    pe.wait_ge(wint_ready, s + 1)
                    for n, src in enumerate((lint, wint, ht)):
                        i = pe.matmul(K.ps[7][:, S:2 * S], f("wg1")[:, n * P:(n + 1) * P], src[:, :],
                                      start=(n == 0), stop=(n == 2))
                    i.then_inc(g1_ps, 1)
                    pe.wait_ge(g1_ready, s + 1)
                    pe.matmul(K.ps[1][:, 0:S], f("wg2"), g1[:, :], start=True, stop=True).then_inc(g2_ps, 1)
                    pe.wait_ge(ot_ready, s + 1)
                    for j in range(TS):
                        i = pe.matmul(K.ps[0][:, j * P:(j + 1) * P], ot[:, j * P:(j + 1) * P], f("wo"), start=True, stop=True)
                    i.then_inc(y_ps, 1)



def stage_quantised_ffn(K, tag):
    nc = K.nc
    NB, U = 3, 4
    with ExitStack() as scope:
        K.scope = scope
        sb = K.sb
        w = sb(f"{tag}_w", [P, 6 * P])
        bn = sb(f"{tag}_bn", [P, U, TS, 6])
        mv = sb(f"{tag}_mv", [P, U, TS, 2])
        rs = sb(f"{tag}_rs", [P, U, TS])
        hcur = sb(f"{tag}_h", [P, U, W])
        hb = sb(f"{tag}_h_bias", [P, U, W])
        ht = sb(f"{tag}_ht", [P, U, W])
        y = sb(f"{tag}_y", [P, U, W])
        yn = sb(f"{tag}_yn", [P, U, W])
        gt = sb(f"{tag}_gelu_t", [P, U, W])
        (dve_s, pool_s, lora_ps, w_ready, stats, rstd, h_ready, ht_ps, ht_ready, y_ps, yn_ready, ynt_ps, gt_ready,
         z_ps, hb_ready, pool_hold, y_sb) = make_sems(
            K, tag, "dve_chain pool_chain lora_product w_ready stats rstd h_ready ht_product ht_ready y_product "
                    "yn_ready ynt_product gelu_ready z_product h_bias_ready pool_hold y_ready")
        f = lambda n: field(K, "f3", n)
        bias = f("bias")
        NL = (NB + 1) * U
        with nc.Block() as block:
            K.start_loads(block, tag)

            @block.vector
            def _(dve):
                dve.wait_ge(K.loaded["f3"], 16)
                dve.wait_ge(K.loaded_q, 16)
                link = chain(dve, dve_s)
                link(dve.tensor_scalar(w[:, :], K.qw[:, :], 7.5, 1.0 / 7.5, ALU.subtract, ALU.mult))
                link(dve.tensor_tensor(w[:, :], w[:, :], f("scale"), ALU.mult))
                dve.wait_ge(lora_ps, 1)
                dve.tensor_tensor(w[:, 0:512], w[:, 0:512], K.ps[0][:, :], ALU.add).then_inc(w_ready, 1)
                dve.tensor_tensor(w[:, 512:768], w[:, 512:768], K.ps[1][:, 0:256], ALU.add).then_inc(w_ready, 1)
                with dve.Fori(0, B // U) as s:
                    link = chain(dve, dve_s)

                    def statistics(u, src):
                        for j in range(TS):
                            i = dve.bn_stats(bn[:, u, j, :], src(j))
                        link(i)
                        for j in range(TS):
                            i = dve.bn_aggr(mv[:, u, j, :], bn[:, u, j, :])
                        i.then_inc(stats, 1)

                    def normalise(u, src, dst):
                        for j in range(TS):
                            i = dve.tensor_scalar(dst[:, u, j * P:(j + 1) * P], src(j), mv[:, u, j, 0:1],
                                                  rs[:, u, j:j + 1], ALU.subtract, ALU.mult)
                        return i

                    xt = lambda u: lambda j: K.x[:, bass.ds((s * U + u) * W + j * P, P)]
                    yt = lambda u: lambda j: y[:, u, j * P:(j + 1) * P]
                    for u in range(U):
                        statistics(u, xt(u))
                    for u in range(U):
                        dve.wait_ge(rstd, s * NL + u + 1)
                        normalise(u, xt(u), hcur).then_inc(h_ready, 1)
                    for b in range(NB):
                        e = s * (NB * U) + b * U
                        for u in range(U):
                            dve.wait_ge(y_ps, e + u + 1)
                            link(dve.tensor_tensor(
                                y[:, u, :].rearrange("p (t o) -> p t o", t=TS),
                                K.ps[2 + u % 2][:, 0:W].rearrange("p (t o) -> p t o", t=TS),
                                bias[:, 2 * b * P:(2 * b + 1) * P].unsqueeze(1).broadcast_to([P, TS, P]), ALU.add))
                            dve.sem_inc(y_sb, 1)
                            statistics(u, yt(u))
                        for u in range(U):
                            dve.wait_ge(rstd, s * NL + (b + 1) * U + u + 1)
                            normalise(u, yt(u), yn).then_inc(yn_ready, 1)
                        for u in range(U):
                            dve.wait_ge(hb_ready, e + u + 1)
                            dve.wait_ge(z_ps, e + u + 1)
                            dve.tensor_tensor(hcur[:, u, :], K.ps[6 + u % 2][:, 0:W], hb[:, u, :],
                                              ALU.add).then_inc(h_ready, 1)
                    for u in range(U):
                        dve.wait_ge(h_ready, s * NL + NB * U + u + 1)
                        xs = K.x[:, bass.ds((s * U + u) * W, W)]
                        link(dve.scalar_tensor_tensor(xs, hcur[:, u, :], 0.5, xs, ALU.mult, ALU.add))

            @block.gpsimd
            def _(pool):
                pool.wait_ge(K.loaded["f3"], 16)
                with pool.Fori(0, B // U) as s:
                    pool.sem_clear(pool_s)
                    count = [0]

                    def rsqrt(u, e):
                        pool.wait_ge(stats, e + 1)
                        pool.sem_inc(pool_hold, 1)
                        pool.tensor_scalar(rs[:, u, :], mv[:, u, :, 1], EPS, None, ALU.add).then_inc(pool_s, 1)
                        count[0] += 1
                        pool.wait_ge(pool_s, count[0])
                        pool.tensor_tensor(rs[:, u, :], rs[:, u, :], K.neg_half[:, 0:TS], ALU.pow).then_inc(rstd, 1)

                    for u in range(U):
                        rsqrt(u, s * NL + u)
                    for b in range(NB):
                        for u in range(U):
                            pool.wait_ge(h_ready, s * NL + b * U + u + 1)
                            for j in range(TS):
                                i = pool.tensor_tensor(hb[:, u, j * P:(j + 1) * P], hcur[:, u, j * P:(j + 1) * P],
                                                       bias[:, (2 * b + 1) * P:(2 * b + 2) * P], ALU.add)
                            i.then_inc(hb_ready, 1)
                        for u in range(U):
                            rsqrt(u, s * NL + (b + 1) * U + u)

            @block.scalar
            def _(act):
                act.wait_ge(K.loaded["f3"], 16)
                with act.Fori(0, B // U) as s:
                    for b in range(NB):
                        e = s * (NB * U) + b * U
                        for u in range(U):
                            act.wait_ge(ht_ps, e + u + 1)
                            act.activation(ht[:, u, :], K.ps[0 + u % 2][:, 0:W], ACT.Copy).then_inc(ht_ready, 1)
                        for u in range(U):
                            act.wait_ge(ynt_ps, e + u + 1)
                            act.activation(gt[:, u, :], K.ps[4 + u % 2][:, 0:W], ACT.Gelu, bias=f("bet")[:, b:b + 1],
                                           scale=f("gam")[:, b:b + 1]).then_inc(gt_ready, 1)

            @block.tensor
            def _(pe):
                pe.wait_ge(K.consts_ready, K.N_CONST)
                pe.wait_ge(K.loaded["f3"], 16)
                for i in range(6):
                    k = pe.matmul(K.ps[i // 4][:, (i % 4) * P:(i % 4 + 1) * P], f("la")[0:32, i * P:(i + 1) * P],
                                  f("lb")[0:32, i * P:(i + 1) * P], start=True, stop=True)
                k.then_inc(lora_ps, 1)
                pe.wait_ge(w_ready, 2)
                with pe.Fori(0, B // U) as s:
                    for b in range(NB):
                        e = s * (NB * U) + b * U
                        for u in range(U):
                            pe.wait_ge(h_ready, s * NL + b * U + u + 1)
                            if u >= 2 or b > 0:
                                pe.wait_ge(ht_ready, e + u - 1)
                            for j in range(TS):
                                i = pe.transpose(K.ps[0 + u % 2][:, j * P:(j + 1) * P], hcur[:, u, j * P:(j + 1) * P],
                                                 K.ident[:, :])
                            i.then_inc(ht_ps, 1)
                        for u in range(U):
                            pe.wait_ge(ht_ready, e + u + 1)
                            if u >= 2 or b > 0:
                                pe.wait_ge(y_sb, e + u - 1)
                            for j in range(TS):
                                i = pe.matmul(K.ps[2 + u % 2][:, j * P:(j + 1) * P], ht[:, u, j * P:(j + 1) * P],
                                              w[:, 2 * b * P:(2 * b + 1) * P], start=True, stop=True)
                            i.then_inc(y_ps, 1)
                        for u in range(U):
                            pe.wait_ge(yn_ready, e + u + 1)
                            if u >= 2 or b > 0:
                                pe.wait_ge(gt_ready, e + u - 1)
                            for j in range(TS):
                                i = pe.transpose(K.ps[4 + u % 2][:, j * P:(j + 1) * P], yn[:, u, j * P:(j + 1) * P],
                                                 K.ident[:, :])
                            i.then_inc(ynt_ps, 1)
                        for u in range(U):
                            pe.wait_ge(gt_ready, e + u + 1)
                            if u >= 2 or b > 0:
                                pe.wait_ge(h_ready, s * NL + (b + 1) * U + u - 1)
                            for j in range(TS):
                                i = pe.matmul(K.ps[6 + u % 2][:, j * P:(j + 1) * P], gt[:, u, j * P:(j + 1) * P],
                                              w[:, (2 * b + 1) * P:(2 * b + 2) * P], start=True, stop=True)
                            i.then_inc(z_ps, 1)



def stage_squared_relu_attention(K, tag):
    nc = K.nc
    H, DK, DV = 16, 16, 64
    G = 4
    TINY = 1e-24
    with ExitStack() as scope:
        K.scope = scope
        sb = K.sb
        N = Norm(K, tag)
        xnt = sb(f"{tag}_xnt", [P, W])
        q4 = sb(f"{tag}_q4", [P, G, S])
        k4 = sb(f"{tag}_k4", [P, G, S])
        sq = sb(f"{tag}_qk_squares", [P, 2, 2 * S])
        v = sb(f"{tag}_v", [P, TS, H * DV])
        vsq = sb(f"{tag}_v_squares", [P, 2, 512])
        gt = sb(f"{tag}_gates", [P, TS, H * DV])
        ss = sb(f"{tag}_sums", [P, 3, TS, H])
        ssc = sb(f"{tag}_sums_guarded", [P, 3, TS, H])
        nrm = sb(f"{tag}_norms", [P, 2, TS, H])
        rinv = sb(f"{tag}_norms_inverse", [P, 3, TS, H])
        rel = sb(f"{tag}_relu", [P, 3, TS, S])
        at = sb(f"{tag}_attention", [P, 3, TS, S])
        osq = sb(f"{tag}_out_squares", [P, 2, 512])
        og = sb(f"{tag}_out_gated", [P, TS, H * DV])
        on = sb(f"{tag}_out_norm", [P, TS, H])
        onn = sb(f"{tag}_out_norm_root", [P, TS, H])
        n2 = sb(f"{tag}_n", [P, TS, H])
        nmaxed = sb(f"{tag}_n_guarded", [P, TS, H])
        ninv = sb(f"{tag}_n_inverse", [P, TS, H])
        th = sb(f"{tag}_tanh_n", [P, TS, H])
        fac = sb(f"{tag}_factor", [P, TS, H])
        outt = sb(f"{tag}_outt", [P, 8, S])
        (dve_s, xnt_ready, qk_ps, qk_sq, qk_sb, nrm_ps, v_ps, v_sq, v_sb, g_ps, g_ready, guarded, roots, inv_ready,
         sc_ps, rel_ready, at_ready, o_ps, o_sq, on_ready, oroot, n_ready, th_ready, og_ready, ot_ps, ot_ready,
         y_ps, done, silu_ready, sq_used) = make_sems(
            K, tag, "dve_chain xnt_ready qk_product qk_squares qk_ready norm_product v_product v_squares v_ready "
                    "gate_product gate_ready sums_guarded roots_ready inverse_ready scores_product relu_ready "
                    "attention_ready out_product out_squares out_norm_ready out_root_ready n_ready tanh_ready "
                    "gated_ready outt_product outt_ready y_product seq_done silu_ready squares_used")
        f = lambda n: field(K, "a3", n)
        with nc.Block() as block:
            K.start_loads(block, tag)

            @block.vector
            def _(dve):
                dve.sem_inc(done, 1)
                with dve.Fori(0, B) as s:
                    link = chain(dve, dve_s)
                    norm_vector(K, N, dve, link, lambda j: K.x[:, bass.ds(s * W + j * P, P)], s)
                    dve.wait_ge(N.xt, s + 1)
                    dve.tensor_copy(xnt[:, :], K.ps[0][:, 0:W]).then_inc(xnt_ready, 1)
                    for g in range(G):
                        dve.wait_ge(qk_sq, s * G + g + 1)
                        bank = K.ps[1 + g % 2]
                        dve.tensor_copy(q4[:, g, :], bank[:, 0:S])
                        dve.tensor_copy(k4[:, g, :], bank[:, S:2 * S]).then_inc(qk_sb, 1)
                    for n in range(4):
                        j, c = n // 2, n % 2
                        dve.wait_ge(v_sq, s * 4 + n + 1)
                        dve.tensor_copy(v[:, j, c * 512:(c + 1) * 512], K.ps[4 + n % 2][:, :]).then_inc(v_sb, 1)
                        link(dve.tensor_reduce(ss[:, 2, j, c * 8:(c + 1) * 8],
                                               vsq[:, n % 2, :].rearrange("p (h d) -> p h d", h=8), AX_X, ALU.add))
                    dve.wait_ge(nrm_ps, s + 1)
                    link(dve.tensor_copy(ss[:, 0:2, :, :], K.ps[3][:, 0:64].rearrange("p (a t h) -> p a t h", a=2, t=TS)))
                    dve.tensor_scalar(ssc[:, :, :, :], ss[:, :, :, :], TINY, None, ALU.max).then_inc(guarded, 1)
                    dve.wait_ge(roots, s + 1)
                    dve.reciprocal(rinv[:, 0, :, :], ssc[:, 0, :, :])
                    dve.reciprocal(rinv[:, 1:3, :, :], nrm[:, :, :, :]).then_inc(inv_ready, 1)
                    dve.wait_ge(inv_ready, s + 1)
                    for h in range(H):
                        dve.wait_ge(rel_ready, s * H + h + 1)
                        if h >= 3:
                            dve.wait_ge(o_ps, s * H + h - 2)
                        for j in range(TS):
                            i = dve.scalar_tensor_tensor(at[:, h % 3, j, :], rel[:, h % 3, j, :],
                                                         rinv[:, 2, j, h:h + 1], rel[:, h % 3, j, :], ALU.mult, ALU.mult)
                        i.then_inc(at_ready, 1)
                    for n in range(4):
                        a, j = n // 2, n % 2
                        dve.wait_ge(o_sq, s * 4 + n + 1)
                        dve.tensor_reduce(on[:, j, a * 8:(a + 1) * 8],
                                          osq[:, n % 2, :].rearrange("p (h d) -> p h d", h=8), AX_X,
                                          ALU.add).then_inc(on_ready, 1)
                    dve.wait_ge(oroot, s + 1)
                    dve.tensor_tensor(n2[:, :, :], onn[:, :, :], rinv[:, 0, :, :], ALU.mult).then_inc(n_ready, 1)
                    dve.wait_ge(n_ready, s + 1)
                    link(dve.tensor_scalar(nmaxed[:, :, :], n2[:, :, :], 1e-12, None, ALU.max))
                    link(dve.reciprocal(ninv[:, :, :], nmaxed[:, :, :]))
                    link(dve.tensor_tensor(ninv[:, :, :], ninv[:, :, :], rinv[:, 0, :, :], ALU.mult))
                    dve.wait_ge(th_ready, s + 1)
                    link(dve.tensor_tensor(fac[:, :, :], th[:, :, :], ninv[:, :, :], ALU.mult))
                    for n in range(4):
                        a, j = n // 2, n % 2
                        hh = slice(a * 8, (a + 1) * 8)
                        cols = og[:, j, a * 512:(a + 1) * 512]
                        link(dve.tensor_tensor(cols, K.ps[4 + n][:, :], gt[:, j, a * 512:(a + 1) * 512], ALU.mult))
                        dve.tensor_tensor(cols.rearrange("p (h d) -> p h d", h=8), cols.rearrange("p (h d) -> p h d", h=8),
                                          fac[:, j, hh].unsqueeze(2).broadcast_to([P, 8, DV]), ALU.mult).then_inc(og_ready, 1)
                    dve.wait_ge(y_ps, s + 1)
                    xs = K.x[:, bass.ds(s * W, W)]
                    dve.tensor_tensor(xs, K.ps[0][:, 0:W], xs, ALU.add).then_inc(done, 1)

            @block.gpsimd
            def _(pool):
                with pool.Fori(0, B) as s:
                    norm_pool(K, N, pool, s)

            @block.scalar
            def _(act):
                with act.Fori(0, B) as s:
                    act.wait_ge(done, s + 1)
                    for g in range(G):
                        act.wait_ge(qk_ps, s * G + g + 1)
                        if g >= 2:
                            act.wait_ge(sq_used, s * G + g - 1)
                        act.activation(sq[:, g % 2, :], K.ps[1 + g % 2][:, :], ACT.Square).then_inc(qk_sq, 1)
                    for n in range(4):
                        act.wait_ge(v_ps, s * 4 + n + 1)
                        if n >= 2:
                            act.wait_ge(v_sb, s * 4 + n)
                        act.activation(vsq[:, n % 2, :], K.ps[4 + n % 2][:, :], ACT.Square).then_inc(v_sq, 1)
                    for n in range(4):
                        act.wait_ge(g_ps, s * 4 + n + 1)
                        act.activation(gt[:, n // 2, (n % 2) * 512:(n % 2 + 1) * 512], K.ps[(0, 6)[n % 2]][:, :],
                                       ACT.Silu).then_inc(silu_ready, 1)
                    act.wait_ge(silu_ready, s * 4 + 4)
                    act.activation(gt[:, :, :], gt[:, :, :], ACT.Tanh).then_inc(g_ready, 1)
                    act.wait_ge(guarded, s + 1)
                    act.activation(nrm[:, :, :, :], ssc[:, 1:3, :, :], ACT.Sqrt).then_inc(roots, 1)
                    act.wait_ge(inv_ready, s + 1)
                    for h in range(H):
                        act.wait_ge(sc_ps, s * H + h + 1)
                        if h >= 3:
                            act.wait_ge(at_ready, s * H + h - 2)
                        for j in range(TS):
                            i = act.activation(rel[:, h % 3, j, :], K.ps[2 + h % 2][:, j * S:(j + 1) * S], ACT.Relu,
                                               scale=rinv[:, 1, j, h:h + 1])
                        i.then_inc(rel_ready, 1)
                    for n in range(4):
                        act.wait_ge(o_ps, s * H + 8 * (n // 2) + 8)
                        if n >= 2:
                            act.wait_ge(on_ready, s * 4 + n - 1)
                        act.activation(osq[:, n % 2, :], K.ps[4 + n][:, :], ACT.Square).then_inc(o_sq, 1)
                    act.wait_ge(on_ready, s * 4 + 4)
                    act.activation(onn[:, :, :], on[:, :, :], ACT.Sqrt).then_inc(oroot, 1)
                    act.wait_ge(n_ready, s + 1)
                    act.activation(th[:, :, :], n2[:, :, :], ACT.Tanh).then_inc(th_ready, 1)
                    for n in range(4):
                        act.wait_ge(ot_ps, s * 4 + n + 1)
                        act.activation(outt[:, 2 * n:2 * n + 2, :].rearrange("p c t -> p (c t)"), K.ps[2 + n % 2][:, :],
                                       ACT.Copy).then_inc(ot_ready, 1)

            @block.tensor
            def _(pe):
                pe.wait_ge(K.consts_ready, K.N_CONST)
                pe.wait_ge(K.loaded["a3"], 16)
                with pe.Fori(0, B) as s:
                    norm_tensor(K, N, pe, s, K.ps[0])
                    pe.wait_ge(xnt_ready, s + 1)
                    pe.wait_ge(done, s + 1)

                    def norms(g):
                        pe.wait_ge(qk_sq, s * G + g + 1)
                        for a in range(2):
                            for j in range(TS):
                                i = pe.matmul(K.ps[3][:, (a * TS + j) * H + 4 * g:(a * TS + j) * H + 4 * g + 4],
                                              sq[:, g % 2, a * S + j * P:a * S + (j + 1) * P], K.quad[:, :],
                                              start=True, stop=True)
                        i.then_inc(sq_used, 1)
                        if g == G - 1:
                            pe.wait_ge(sq_used, s * G + G)
                            pe.sem_inc(nrm_ps, 1)

                    for g in range(G):
                        if g >= 2:
                            pe.wait_ge(qk_sb, s * G + g - 1)
                        bank = K.ps[1 + g % 2]
                        pe.matmul(bank[:, 0:S], f("wq4")[:, g * P:(g + 1) * P], xnt[:, :], start=True, stop=True)
                        pe.matmul(bank[:, S:2 * S], f("wk4")[:, g * P:(g + 1) * P], xnt[:, :],
                                  start=True, stop=True).then_inc(qk_ps, 1)
                        if g >= 1:
                            norms(g - 1)
                    norms(G - 1)
                    for n in range(4):
                        j, c = n // 2, n % 2
                        if n >= 2:
                            pe.wait_ge(v_sb, s * 4 + n - 1)
                        pe.matmul(K.ps[4 + n % 2][:, :], xnt[:, j * P:(j + 1) * P], f("wv")[:, c * 512:(c + 1) * 512],
                                  start=True, stop=True).then_inc(v_ps, 1)
                    for n in range(4):
                        j, c = n // 2, n % 2
                        if n >= 2:
                            pe.wait_ge(silu_ready, s * 4 + n - 1)
                        pe.matmul(K.ps[(0, 6)[n % 2]][:, :], xnt[:, j * P:(j + 1) * P],
                                  f("wg")[:, c * 512:(c + 1) * 512], start=True, stop=True).then_inc(g_ps, 1)
                    pe.wait_ge(guarded, s + 1)
                    pe.wait_ge(silu_ready, s * 4 + 4)
                    for i in range(H + 2):
                        if i < H:
                            g, r = i // 4, 32 * (i % 4)
                            if i >= 2:
                                pe.wait_ge(rel_ready, s * H + i - 1)
                            for j in range(TS):
                                k = pe.matmul(K.ps[2 + i % 2][:, j * S:(j + 1) * S], k4[r:r + 32, g, j * P:(j + 1) * P],
                                              q4[r:r + 32, g, :], start=True, stop=True)
                            k.then_inc(sc_ps, 1)
                        if i >= 2:
                            h = i - 2
                            pe.wait_ge(at_ready, s * H + h + 1)
                            for t in range(TS):
                                for j in range(TS):
                                    k = pe.matmul(K.ps[4 + 2 * (h // 8) + t][:, (h % 8) * DV:(h % 8 + 1) * DV],
                                                  at[:, h % 3, j, t * P:(t + 1) * P], v[:, j, h * DV:(h + 1) * DV],
                                                  start=(j == 0), stop=(j == TS - 1))
                            k.then_inc(o_ps, 1)
                    for n in range(4):
                        if n >= 2:
                            pe.wait_ge(ot_ready, s * 4 + n - 1)
                        pe.wait_ge(og_ready, s * 4 + (2 if n < 2 else 4))
                        for c in range(2):
                            for t in range(TS):
                                i = pe.transpose(K.ps[2 + n % 2][:, c * S + t * P:c * S + (t + 1) * P],
                                                 og[:, t, (2 * n + c) * P:(2 * n + c + 1) * P], K.ident[:, :])
                        i.then_inc(ot_ps, 1)
                    for t in range(TS):
                        for c in range(8):
                            if t == 0 and c % 2 == 0:
                                pe.wait_ge(ot_ready, s * 4 + c // 2 + 1)
                            i = pe.matmul(K.ps[0][:, t * P:(t + 1) * P], outt[:, c, t * P:(t + 1) * P],
                                          f("wo")[:, c * P:(c + 1) * P], start=(c == 0), stop=(c == 7))
                    i.then_inc(y_ps, 1)



STAGES = {
    "f0a": (stage_signed_ffn,), "at0": (stage_softmax_attention,), "f0b": (stage_signed_ffn,),
    "m1a": (stage_gated_experts,), "mam": (stage_state_space,), "m1b": (stage_gated_experts,),
    "m2a": (stage_gelu_experts,), "at2": (stage_window_linear_attention,), "m2b": (stage_gelu_experts,),
    "f3a": (stage_quantised_ffn,), "at3": (stage_squared_relu_attention,), "f3b": (stage_quantised_ffn,),
}
REGION = {"a0": "r0", "mb": "r0", "a2": "r0", "a3": "r0", "m1": "r1", "m2": "r2", "f3": "r3"}
LOAD_AT = {"mb": "m1a", "a2": "m1b", "a3": "f3a"}


def build(nc, aps, out, stages=tuple(STAGES)):
    K = Core()
    K.nc = nc
    needs = {"f0a": "a0", "at0": "a0", "f0b": "a0", "m1a": "m1", "mam": "mb", "m1b": "m1", "m2a": "m2",
             "at2": "a2", "m2b": "m2", "f3a": "f3", "at3": "a3", "f3b": "f3"}
    used = [p for p in PACKS if p in {needs[s] for s in stages}]
    with ExitStack() as ctx:
        K.sem_scope = ctx.enter_context(ExitStack())
        K.live_sems = []
        K.scope = ctx
        K.sb = lambda name, shape, dt=F32: K.scope.enter_context(nc.sbuf_tensor(name, shape, dt))
        K.ps = [ctx.enter_context(nc.psum_tensor(f"bank{i}", [P, 512], F32)) for i in range(8)]
        K.x = K.sb("x", [P, B * W])
        K.ident = K.sb("identity", [P, P])
        K.neg_half = K.sb("neg_half", [P, 8])
        K.neg_one = K.sb("neg_one", [P, 1])
        K.ones = K.sb("ones", [P, P])
        K.quad = K.sb("quadrant_ones", [P, 4])
        K.iota16 = K.sb("iota16", [P, E])
        K.sel64 = K.sb("select_64", [PARTS, E * 64], BF16)
        K.sel = K.sb("select", [96, 32 * P], BF16)
        K.qw = K.sb("qweights", [P, 6 * P], I32)
        region = {}
        for p in used:
            r = REGION[p]
            region[r] = max(region.get(r, 0), pack_width(p))
        region = {r: K.sb(f"weights_{r}", [P, n]) for r, n in region.items()}
        K.pack = {p: region[REGION[p]] for p in used}
        K.loaded = {p: ctx.enter_context(nc.semaphore(f"loaded_{p}")) for p in used}
        K.loaded_x, K.loaded_q, K.consts_ready, K.const_chain, K.stored = (
            ctx.enter_context(nc.semaphore(n)) for n in
            ("loaded_x", "loaded_q", "consts_ready", "const_chain", "stored"))
        K.N_CONST = 1

        def start_loads(block, tag):
            due = [p for p in used if LOAD_AT.get(p) == tag]
            if due:
                @block.sync
                def _(sp):
                    for p in due:
                        sp.dma_start(K.pack[p][:, 0:pack_width(p)], aps[p]).then_inc(K.loaded[p], 16)
        K.start_loads = start_loads

        with nc.Block() as block:
            @block.sync
            def _(sp):
                sp.dma_start(K.x[:, :], aps["x"]).then_inc(K.loaded_x, 16)
                for p in used:
                    if LOAD_AT.get(p) not in stages:
                        sp.dma_start(K.pack[p][:, 0:pack_width(p)], aps[p]).then_inc(K.loaded[p], 16)
                sp.dma_start(K.qw[:, :], aps["q"]).then_inc(K.loaded_q, 16)
                sp.wait_ge(K.loaded_x, 16)

            @block.gpsimd
            def _(pool):
                n = 0

                def link(ins):
                    nonlocal n
                    n += 1
                    ins.then_inc(K.const_chain, 1)
                    pool.wait_ge(K.const_chain, n)
                pool.memset(K.neg_half[:, :], -0.5)
                pool.memset(K.ones[:, :], 1.0)
                pool.memset(K.neg_one[:, :], -1.0)
                pool.iota(K.iota16[:, :], [[1, E]], base=0, channel_multiplier=0,
                          allow_small_or_imprecise_dtypes=True)
                pool.memset(K.sel64[:, :], 0.0)
                pool.memset(K.sel[:, :], 0.0)
                link(pool.memset(K.ident[:, :], 0.0))
                link(pool.affine_select(out=K.ident[:, :], in_=K.ident[:, :], compare_op=ALU.not_equal, fill=1.0,
                                        base=0, pattern=[[-1, P]], channel_multiplier=1))
                link(pool.memset(K.quad[:, :], 1.0))
                link(pool.affine_select(out=K.quad[:, :], in_=K.quad[:, :], compare_op=ALU.is_ge, fill=0.0, base=0,
                                        pattern=[[-32, 4]], channel_multiplier=1))
                link(pool.affine_select(out=K.quad[:, :], in_=K.quad[:, :], compare_op=ALU.is_ge, fill=0.0, base=31,
                                        pattern=[[32, 4]], channel_multiplier=-1))
                for sel, rows, wide in ((K.sel64, E, 64), (K.sel, 32, P)):
                    for base in (HI, MID, LO):
                        v = sel[:, :].rearrange("p (e c) -> p e c", e=rows)
                        link(pool.affine_select(out=v, in_=v, compare_op=ALU.not_equal, fill=1.0, base=-base,
                                                pattern=[[-1, rows], [0, wide]], channel_multiplier=1))
                pool.sem_inc(K.consts_ready, 1)
        for tag in stages:
            STAGES[tag][0](K, tag)
            clear_sems(K)
        with nc.Block() as block:
            @block.sync
            def _(sp):
                sp.dma_start(out, K.x[:, :]).then_inc(K.stored, 16)
                sp.wait_ge(K.stored, 16)


def host_arrays(i):
    rows = lambda v: np.broadcast_to(np.asarray(v).reshape(1, -1), (P, np.asarray(v).size))
    cols = lambda v, n: np.asarray(v).reshape(n, P).T
    kpm = lambda w: w.reshape(-1, P, w.shape[-1]).transpose(1, 0, 2).reshape(P, -1)

    def pad(a):
        out = np.zeros((P, a.shape[1]), a.dtype)
        out[:a.shape[0]] = a
        return out

    def by_four(w, d):
        out = np.zeros((w.shape[0], 16, 32), w.dtype)
        out[:, :, :d] = w.reshape(w.shape[0], 16, d)
        return out.reshape(w.shape[0], 512)

    g = {}
    Ww, Wb = i["L0_attn_W_w"], i["L0_attn_W_b"]
    g["a0"] = dict(ffn=i["L0_ffn_weight"].T, wq=Ww[:1024].T, wk=Ww[1024:2048].T, wv=Ww[2048:].T,
                   wo=kpm(i["L0_attn_out_w"].T), bq=cols(Wb[:1024], 8), bk=cols(Wb[1024:2048], 8),
                   bv=rows(Wb[2048:]), bo=rows(i["L0_attn_out_b"]))
    g["m1"] = dict(rw=i["L1_ffn_router_w"].T, rb=np.tile(rows(i["L1_ffn_router_bias"]), (1, 2)),
                   up=i["L1_ffn_up_proj"].transpose(1, 0, 2).reshape(P, -1),
                   gate=i["L1_ffn_gate_proj"].transpose(1, 0, 2).reshape(P, -1),
                   down=kpm(i["L1_ffn_down_proj"].reshape(1024, P)), shg=i["L1_ffn_sh_gate"].T,
                   shu=i["L1_ffn_sh_up"].T, shd=i["L1_ffn_sh_down"].T)
    mb = {}
    for l in range(4):
        a = {k[8:]: v[l] for k, v in i.items() if k.startswith("L1_attn_") and "fnorm" not in k}
        bc = a["x_proj_w"][8:40].T
        xp = np.concatenate([bc, bc, bc, a["x_proj_w"][:8].T], axis=1)
        dtw = np.zeros((P, 256), np.float32)
        dtw[96:104] = a["dt_proj_w"].T
        mb.update({f"{k}{l}": v for k, v in dict(
            taps=rows(a["conv_w"][:, 0, :].T), inx=a["in_proj_w"][:256].T, inz=a["in_proj_w"][256:].T,
            cb=cols(a["conv_b"], 2), xp=kpm(xp), dtw=dtw, dtb=cols(a["dt_proj_b"], 2),
            alog=kpm(a["A_log"]), dsk=cols(a["D_skip"], 2), outw=kpm(a["out_proj_w"].T),
            lnw=a["ln_w"][:, None], lnb=a["ln_b"][:, None]).items()})
    g["mb"] = mb
    g["m2"] = dict(rw=i["L2_ffn_router_w"], rb=np.tile(rows(i["L2_ffn_router_b"]), (1, 2)),
                   w1=i["L2_ffn_w1"].transpose(1, 0, 2).reshape(P, -1), b1=cols(i["L2_ffn_b1"], 32),
                   w2=kpm(i["L2_ffn_w2"].reshape(-1, P)), b2=pad(i["L2_ffn_b2"]))
    a = {k[8:]: v for k, v in i.items() if k.startswith("L2_attn_")}
    at = np.clip(np.arange(192)[None, :] + 32 - np.arange(P)[:, None], 0, 128)
    g["a2"] = dict(wql=a["wq_lin"], wkl=a["wk_lin"], wvl=a["wv_lin"], bql=a["bq_lin"][:, None],
                   bkl=rows(a["bk_lin"]), bvl=rows(a["bv_lin"]), wq4=by_four(a["wq_loc"], 8),
                   wk4=by_four(a["wk_loc"], 8), bq4=cols(by_four(rows(a["bq_loc"])[:1], 8), 4),
                   bk4=cols(by_four(rows(a["bk_loc"])[:1], 8), 4), wvc=a["wv_loc"], bvc=rows(a["bv_loc"]),
                   wo=a["wo"], bo=rows(a["bo"]), wg1=kpm(a["wg1"]), bg1=a["bg1"][:, None], wg2=a["wg2"],
                   bg2=a["bg2"][:, None], lng=a["ln_g"][:, None], lnb=a["ln_b"][:, None],
                   band=a["rel_bias"][at].transpose(0, 2, 1).reshape(P, -1))
    g["f3"] = dict(scale=np.repeat(i["L3_ffn_scales"].transpose(2, 0, 1), 16, axis=0).reshape(P, -1),
                   bias=rows(i["L3_ffn_biases"]), la=pad(i["L3_ffn_lora_a"].transpose(1, 0, 2).reshape(32, -1)),
                   lb=pad(i["L3_ffn_lora_b"].transpose(2, 0, 1).reshape(32, -1)),
                   gam=i["L3_ffn_ln_gamma"].T, bet=i["L3_ffn_ln_beta"].T)
    qg, kv = (i[n].reshape(P, 16, 80) for n in ("L3_attn_Wqg", "L3_attn_Wkv"))
    g["a3"] = dict(wq4=by_four(qg[:, :, :16].reshape(P, -1), 16), wk4=by_four(kv[:, :, :16].reshape(P, -1), 16),
                   wg=qg[:, :, 16:].reshape(P, -1), wv=kv[:, :, 16:].reshape(P, -1), wo=kpm(i["L3_attn_Wout"]))
    arrays = {}
    for p, fields in PACKS.items():
        for n, c in fields.items():
            assert g[p][n].shape == (P, c), (p, n, g[p][n].shape, c)
        arrays[p] = np.ascontiguousarray(np.concatenate([g[p][n] for n in fields], axis=1))
    arrays["q"] = np.ascontiguousarray(i["L3_ffn_qweights"].transpose(2, 0, 1).reshape(P, -1))
    arrays["x"] = np.ascontiguousarray(i["L0_attn_x"].reshape(B * TS, P, P).transpose(1, 0, 2).reshape(P, -1))
    return arrays


def kernel(**inputs):
    from concourse import bacc
    from concourse.bass_utils import run_bass_kernel_spmd

    arrays = host_arrays({k: np.asarray(v) for k, v in inputs.items()})
    nc = bacc.Bacc("TRN2", target_bir_lowering=False, num_devices=1)
    aps = {n: nc.dram_tensor(f"in_{n}", a.shape, mybir.dt.from_np(a.dtype), kind="ExternalInput").ap()
           for n, a in arrays.items()}
    out = nc.dram_tensor("out_x", (P, B * W), F32, kind="ExternalOutput").ap()
    build(nc, aps, out)
    r = run_bass_kernel_spmd(nc, [{f"in_{n}": a for n, a in arrays.items()}], core_ids=[0])
    y = r.results[0]["out_x"]
    return np.ascontiguousarray(y.reshape(P, B * TS, P).transpose(1, 0, 2)).reshape(B, S, P)
```

```python
from contextlib import ExitStack

import numpy as np

import concourse.bass as bass
from concourse import mybir

F32 = mybir.dt.float32
BF16 = mybir.dt.bfloat16
I32 = mybir.dt.int32
U32 = mybir.dt.uint32
ALU = mybir.AluOpType
ACT = mybir.ActivationFunctionType
AX_X = mybir.AxisListType.X

P = 128
B, S = 8, 256
TS = S // P
W = TS * P
EPS = 1e-5

PACKS = {
    "a0": dict(ffn=128, wq=1024, wk=1024, wv=1024, wo=1024, bq=8, bk=8, bv=1024, bo=128),
    "m1": dict(rw=16, rb=32, up=1024, gate=1024, down=1024, shg=128, shu=128, shd=128),
    "mb": {f"{n}{l}": c for l in range(4) for n, c in dict(
        taps=1024, inx=256, inz=256, cb=2, xp=208, dtw=256, dtb=2, alog=32, dsk=2,
        outw=256, lnw=1, lnb=1).items()},
    "m2": dict(rw=16, rb=32, w1=4096, b1=32, w2=4096, b2=128),
    "a2": dict(wql=128, wkl=128, wvl=128, bql=1, bkl=128, bvl=128, wq4=512, wk4=512, bq4=4, bk4=4,
               wvc=128, bvc=128, wo=128, bo=128, wg1=384, bg1=1, wg2=128, bg2=1, lng=1, lnb=1,
               band=16 * 192),
    "f3": dict(scale=768, bias=768, la=768, lb=768, gam=3, bet=3),
    "a3": dict(wq4=512, wk4=512, wg=1024, wv=1024, wo=1024),
}


def pack_width(name):
    return sum(PACKS[name].values())


def pack_offset(name, field):
    at = 0
    for f, n in PACKS[name].items():
        if f == field:
            return at, n
        at += n
    raise KeyError(field)


class Core:
    pass


def make_sems(K, stage, names):
    sems = [K.sem_scope.enter_context(K.nc.semaphore(f"{stage}_{n}")) for n in names.split()]
    K.live_sems += sems
    return sems


def clear_sems(K):
    with K.nc.Block() as block:
        @block.sync
        def _(sp):
            for sem in K.live_sems:
                sp.sem_clear(sem)
    K.live_sems = []
    K.sem_scope.close()


def field(K, pack, name):
    at, n = pack_offset(pack, name)
    return K.pack[pack][:, at:at + n]


def chain(eng, sem):
    count = [0]
    eng.sem_clear(sem)

    def link(ins):
        count[0] += 1
        ins.then_inc(sem, 1)
        eng.wait_ge(sem, count[0])
    return link



class Norm:
    def __init__(self, K, stage):
        self.stats, self.rstd, self.xn, self.xt, self.pool = make_sems(
            K, stage, "ln_stats ln_rstd ln_xn ln_transposed ln_pool_chain")
        sb = K.sb
        self.bn = sb(f"{stage}_ln_bn", [P, TS, 6])
        self.mv = sb(f"{stage}_ln_mv", [P, TS, 2])
        self.rs = sb(f"{stage}_ln_rs", [P, TS])
        self.out = sb(f"{stage}_ln_xn", [P, W])


def norm_vector(K, N, dve, link, src, n, before=None):
    for j in range(TS):
        i = dve.bn_stats(N.bn[:, j, :], src(j))
    link(i)
    for j in range(TS):
        i = dve.bn_aggr(N.mv[:, j, :], N.bn[:, j, :])
    i.then_inc(N.stats, 1)
    dve.wait_ge(N.rstd, n + 1)
    for j in range(TS):
        i = dve.tensor_scalar(N.out[:, j * P:(j + 1) * P], src(j), N.mv[:, j, 0:1], N.rs[:, j:j + 1],
                              ALU.subtract, ALU.mult)
    i.then_inc(N.xn, 1)


def norm_pool(K, N, pool, n):
    pool.wait_ge(N.stats, n + 1)
    pool.sem_inc(N.pool, 1)
    pool.tensor_scalar(N.rs[:, :], N.mv[:, :, 1], EPS, None, ALU.add).then_inc(N.pool, 1)
    pool.wait_ge(N.pool, 2 * (n + 1))
    pool.tensor_tensor(N.rs[:, :], N.rs[:, :], K.neg_half[:, 0:TS], ALU.pow).then_inc(N.rstd, 1)


def norm_tensor(K, N, pe, n, dst):
    pe.wait_ge(N.xn, n + 1)
    for j in range(TS):
        i = pe.transpose(dst[:, j * P:(j + 1) * P], N.out[:, j * P:(j + 1) * P], K.ident[:, :])
    i.then_inc(N.xt, 1)



def stage_signed_ffn(K, tag):
    nc = K.nc
    with ExitStack() as scope:
        K.scope = scope
        N = Norm(K, tag)
        xnt = K.sb(f"{tag}_xnt", [P, W])
        sgn = K.sb(f"{tag}_sign", [P, P])
        neg = K.sb(f"{tag}_negative", [P, P])
        link_s, xnt_ready, prod, done = make_sems(K, tag, "dve_chain xnt_ready product_ready seq_done")
        with nc.Block() as block:
            K.start_loads(block, tag)

            @block.vector
            def _(dve):
                dve.sem_inc(done, 1)
                link = chain(dve, link_s)
                dve.wait_ge(K.loaded["a0"], 16)
                w = field(K, "a0", "ffn")
                link(dve.tensor_scalar(neg[:, :], w, 0.0, None, ALU.is_lt))
                link(dve.scalar_tensor_tensor(sgn[:, :], w, 0.0, neg[:, :], ALU.is_gt, ALU.subtract))
                with dve.Fori(0, B) as s:
                    link = chain(dve, link_s)
                    norm_vector(K, N, dve, link, lambda j: K.x[:, bass.ds(s * W + j * P, P)], s)
                    dve.wait_ge(N.xt, s + 1)
                    dve.tensor_copy(xnt[:, :], K.ps[0][:, 0:W]).then_inc(xnt_ready, 1)
                    dve.wait_ge(prod, s + 1)
                    xs = K.x[:, bass.ds(s * W, W)]
                    dve.scalar_tensor_tensor(xs, K.ps[1][:, 0:W], 0.5, xs, ALU.mult, ALU.add).then_inc(done, 1)

            @block.gpsimd
            def _(pool):
                with pool.Fori(0, B) as s:
                    norm_pool(K, N, pool, s)

            @block.tensor
            def _(pe):
                pe.wait_ge(K.consts_ready, K.N_CONST)
                with pe.Fori(0, B) as s:
                    norm_tensor(K, N, pe, s, K.ps[0])
                    pe.wait_ge(xnt_ready, s + 1)
                    pe.wait_ge(done, s + 1)
                    for j in range(TS):
                        i = pe.matmul(K.ps[1][:, j * P:(j + 1) * P], xnt[:, j * P:(j + 1) * P], sgn[:, :],
                                      start=True, stop=True)
                    i.then_inc(prod, 1)



def stage_softmax_attention(K, tag):
    nc = K.nc
    H, DH = 16, 64
    G = H // 2
    with ExitStack() as scope:
        K.scope = scope
        sb = K.sb
        N = Norm(K, tag)
        xnt = sb(f"{tag}_xnt", [P, W])
        v = sb(f"{tag}_v", [P, TS, H * DH])
        qt = sb(f"{tag}_qt", [P, 2, S])
        kt = sb(f"{tag}_kt", [P, 2, S])
        nmax = sb(f"{tag}_nmax", [P, H, TS])
        rsum = sb(f"{tag}_rsum", [P, H, TS])
        rinv = sb(f"{tag}_rinv", [P, H, TS])
        probs = sb(f"{tag}_probs", [P, 3, TS, S])
        probst = sb(f"{tag}_probst", [P, 2, TS * S])
        outt = sb(f"{tag}_outt", [P, G, S])
        (link_s, xnt_ready, v_ps, v_ready, qk_ps, qk_ready, sc_ready, max_ready, exp_ready,
         inv_ready, norm_ready, pt_ps, pt_ready, o_ps, o_ready, y_ps, done, pool_step) = make_sems(
            K, tag, "dve_chain xnt_ready v_product v_ready qk_product qk_ready scores_ready max_ready "
                    "exp_ready inv_ready probs_ready probst_product probst_ready out_product out_ready "
                    "y_product seq_done pool_step")
        wq, wk, wv, wo = (field(K, "a0", n) for n in ("wq", "wk", "wv", "wo"))
        bq, bk, bv, bo = (field(K, "a0", n) for n in ("bq", "bk", "bv", "bo"))
        STEPS = H + 3
        with nc.Block() as block:
            K.start_loads(block, tag)

            @block.vector
            def _(dve):
                dve.sem_inc(done, 1)
                dve.wait_ge(K.loaded["a0"], 16)
                with dve.Fori(0, B) as s:
                    link = chain(dve, link_s)
                    norm_vector(K, N, dve, link, lambda j: K.x[:, bass.ds(s * W + j * P, P)], s)
                    dve.wait_ge(N.xt, s + 1)
                    dve.tensor_copy(xnt[:, :], K.ps[0][:, 0:W]).then_inc(xnt_ready, 1)
                    for n in range(4):
                        j, c = n // 2, n % 2
                        dve.wait_ge(v_ps, s * 4 + n + 1)
                        dve.tensor_tensor(v[:, j, c * 512:(c + 1) * 512], K.ps[(1, 7)[n % 2]][:, :],
                                          bv[:, c * 512:(c + 1) * 512], ALU.add).then_inc(v_ready, 1)

                    def queries_keys(g):
                        dve.wait_ge(qk_ps, s * G + g + 1)
                        dve.tensor_scalar(qt[:, g % 2, :], K.ps[0][:, 0:S], bq[:, g:g + 1], DH ** -0.5,
                                          ALU.add, ALU.mult)
                        dve.tensor_scalar(kt[:, g % 2, :], K.ps[0][:, S:2 * S], bk[:, g:g + 1], None,
                                          ALU.add).then_inc(qk_ready, 1)

                    queries_keys(0)
                    for i in range(STEPS):
                        if i < H:
                            dve.wait_ge(sc_ready, s * H + i + 1)
                            dve.tensor_reduce(nmax[:, i, :], K.ps[2 + i % 2][:, :].rearrange("p (t k) -> p t k", t=TS),
                                              AX_X, ALU.max, negate=True).then_inc(max_ready, 1)
                        if i % 2 == 0 and i + 2 < H:
                            queries_keys(i // 2 + 1)
                        if 1 <= i <= H:
                            dve.wait_ge(exp_ready, s * H + i)
                            dve.reciprocal(rinv[:, i - 1, :], rsum[:, i - 1, :]).then_inc(inv_ready, 1)
                        if i >= 4 and i % 2 == 0:
                            g = (i - 4) // 2
                            dve.wait_ge(o_ps, s * H + 2 * g + 2)
                            dve.tensor_copy(outt[:, g, :], K.ps[6 + g % 2][:, 0:S]).then_inc(o_ready, 1)
                    xs = K.x[:, bass.ds(s * W, W)]
                    for j in range(TS):
                        xj = K.x[:, bass.ds(s * W + j * P, P)]
                        i = dve.tensor_tensor(xj, xj, bo, ALU.add)
                    link(i)
                    dve.wait_ge(y_ps, s + 1)
                    dve.tensor_tensor(xs, K.ps[1][:, 0:W], xs, ALU.add).then_inc(done, 1)

            @block.gpsimd
            def _(pool):
                with pool.Fori(0, B) as s:
                    norm_pool(K, N, pool, s)
                    for h in range(H):
                        pool.wait_ge(inv_ready, s * H + h + 1)
                        pool.sem_inc(pool_step, 1)
                        for t in range(TS):
                            i = pool.tensor_scalar(probs[:, h % 3, t, :], probs[:, h % 3, t, :],
                                                   rinv[:, h, t:t + 1], None, ALU.mult)
                        i.then_inc(norm_ready, 1)

            @block.scalar
            def _(act):
                act.wait_ge(K.loaded["a0"], 16)
                with act.Fori(0, B) as s:
                    act.wait_ge(done, s + 1)
                    for i in range(STEPS):
                        if i < H:
                            act.wait_ge(max_ready, s * H + i + 1)
                            if i >= 3:
                                act.wait_ge(pt_ps, s * H + i - 2)
                            for t in range(TS):
                                k = act.activation(probs[:, i % 3, t, :], K.ps[2 + i % 2][:, t * S:(t + 1) * S],
                                                   ACT.Exp, bias=nmax[:, i, t:t + 1],
                                                   accum_out=rsum[:, i, t:t + 1])
                            k.then_inc(exp_ready, 1)
                        if 2 <= i < H + 2:
                            h = i - 2
                            act.wait_ge(pt_ps, s * H + h + 1)
                            if h >= 2:
                                act.wait_ge(o_ps, s * H + h - 1)
                            act.activation(probst[:, h % 2, :], K.ps[4 + h % 2][:, :],
                                           ACT.Copy).then_inc(pt_ready, 1)

            @block.tensor
            def _(pe):
                pe.wait_ge(K.consts_ready, K.N_CONST)
                pe.wait_ge(K.loaded["a0"], 16)
                with pe.Fori(0, B) as s:
                    norm_tensor(K, N, pe, s, K.ps[0])
                    pe.wait_ge(xnt_ready, s + 1)
                    pe.wait_ge(done, s + 1)
                    for n in range(4):
                        j, c = n // 2, n % 2
                        if n >= 2:
                            pe.wait_ge(v_ready, s * 4 + n - 1)
                        pe.matmul(K.ps[(1, 7)[n % 2]][:, :], xnt[:, j * P:(j + 1) * P],
                                  wv[:, c * 512:(c + 1) * 512], start=True, stop=True).then_inc(v_ps, 1)

                    def project(g):
                        if g >= 1:
                            pe.wait_ge(qk_ready, s * G + g)
                        pe.matmul(K.ps[0][:, 0:S], wq[:, g * P:(g + 1) * P], xnt[:, :], start=True, stop=True)
                        pe.matmul(K.ps[0][:, S:2 * S], wk[:, g * P:(g + 1) * P], xnt[:, :],
                                  start=True, stop=True).then_inc(qk_ps, 1)

                    project(0)
                    pe.wait_ge(v_ready, s * 4 + 4)
                    for i in range(STEPS):
                        if i < H:
                            g, r = i // 2, 64 * (i % 2)
                            pe.wait_ge(qk_ready, s * G + g + 1)
                            if i >= 2:
                                pe.wait_ge(exp_ready, s * H + i - 1)
                            for t in range(TS):
                                k = pe.matmul(K.ps[2 + i % 2][:, t * S:(t + 1) * S],
                                              qt[r:r + 64, g % 2, t * P:(t + 1) * P], kt[r:r + 64, g % 2, :],
                                              start=True, stop=True)
                            k.then_inc(sc_ready, 1)
                            if i % 2 == 0 and g + 1 < G:
                                project(g + 1)
                        if 2 <= i < H + 2:
                            h = i - 2
                            pe.wait_ge(norm_ready, s * H + h + 1)
                            if h >= 2:
                                pe.wait_ge(pt_ready, s * H + h - 1)
                            for c in range(TS):
                                for t in range(TS):
                                    k = pe.transpose(K.ps[4 + h % 2][:, c * S + t * P:c * S + (t + 1) * P],
                                                     probs[:, h % 3, t, c * P:(c + 1) * P], K.ident[:, :])
                            k.then_inc(pt_ps, 1)
                        if 3 <= i:
                            h = i - 3
                            g, r = h // 2, 64 * (h % 2)
                            pe.wait_ge(pt_ready, s * H + h + 1)
                            if h % 2 == 0 and g >= 2:
                                pe.wait_ge(o_ready, s * G + g - 1)
                            for c in range(TS):
                                k = pe.matmul(K.ps[6 + g % 2][r:r + 64, 0:S], v[:, c, h * DH:(h + 1) * DH],
                                              probst[:, h % 2, c * S:(c + 1) * S], start=(c == 0), stop=(c == 1))
                            k.then_inc(o_ps, 1)
                    for j in range(TS):
                        for g in range(G):
                            if j == 0:
                                pe.wait_ge(o_ready, s * G + g + 1)
                            k = pe.matmul(K.ps[1][:, j * P:(j + 1) * P], outt[:, g, j * P:(j + 1) * P],
                                          wo[:, g * P:(g + 1) * P], start=(g == 0), stop=(g == G - 1))
                    k.then_inc(y_ps, 1)



E = 16
HI, MID, LO = 0, 32, 64
PARTS = LO + E


class Router:
    def __init__(self, K, stage, topk):
        sb = K.sb
        self.topk = topk
        self.lg_ps, self.top, self.wexp, self.comb, self.combt_ps, self.parts = make_sems(
            K, stage, "logits_product top_ready weights_exp comb_ready combt_product parts_ready")
        self.lg = sb(f"{stage}_logits", [P, TS, E])
        self.top8 = sb(f"{stage}_top8", [P, TS, 8])
        self.idx = sb(f"{stage}_idx", [P, TS, 8], U32)
        self.idxf = sb(f"{stage}_idxf", [P, TS, 8])
        self.negm = sb(f"{stage}_negmax", [P, TS])
        self.wexps = sb(f"{stage}_wexp", [P, TS, topk])
        self.wsum = sb(f"{stage}_wsum", [P, TS])
        self.winv = sb(f"{stage}_winv", [P, TS])
        self.hot = sb(f"{stage}_onehot", [P, TS, topk, E])
        self.raw = sb(f"{stage}_comb_raw", [P, TS, E])
        self.out = sb(f"{stage}_comb", [P, TS, E])
        self.t32 = sb(f"{stage}_combt", [E, W])
        self.rest = sb(f"{stage}_comb_rest", [E, W])
        self.mid = sb(f"{stage}_comb_mid", [E, W], BF16)
        self.part = sb(f"{stage}_comb_parts", [PARTS, W], BF16)


def route_tensor_logits(K, R, pe, xnt, rw):
    for j in range(TS):
        i = pe.matmul(K.ps[1][:, j * E:(j + 1) * E], xnt[:, j * P:(j + 1) * P], rw, start=True, stop=True)
    i.then_inc(R.lg_ps, 1)


def route_vector(K, R, dve, link, s, rb):
    dve.wait_ge(R.lg_ps, s + 1)
    link(dve.tensor_tensor(R.lg[:, :, :].rearrange("p t e -> p (t e)"), K.ps[1][:, 0:TS * E], rb, ALU.add))
    for j in range(TS):
        i = dve.max(R.top8[:, j, :], R.lg[:, j, :])
    link(i)
    dve.tensor_scalar(R.negm[:, :], R.top8[:, :, 0], -1.0, None, ALU.mult).then_inc(R.top, 1)
    for j in range(TS):
        i = dve.max_index(R.idx[:, j, :], R.top8[:, j, :], R.lg[:, j, :])
    link(i)
    link(dve.tensor_copy(R.idxf[:, :, :], R.idx[:, :, :]))
    dve.wait_ge(R.wexp, s + 1)
    dve.tensor_reduce(R.wsum[:, :], R.wexps[:, :, :], AX_X, ALU.add)
    for j in range(TS):
        for k in range(R.topk):
            i = dve.tensor_scalar(R.hot[:, j, k, :], K.iota16[:, :], R.idxf[:, j, k:k + 1],
                                  R.wexps[:, j, k:k + 1], ALU.is_equal, ALU.mult)
    link(i)
    dve.reciprocal(R.winv[:, :], R.wsum[:, :])
    for j in range(TS):
        i = dve.tensor_reduce(R.raw[:, j, :], R.hot[:, j, :, :].rearrange("p k e -> p e k"), AX_X, ALU.add)
    link(i)
    for j in range(TS):
        i = dve.tensor_scalar(R.out[:, j, :], R.raw[:, j, :], R.winv[:, j:j + 1], None, ALU.mult)
    i.then_inc(R.comb, 1)


def route_scalar(K, R, act, s):
    act.wait_ge(R.top, s + 1)
    for j in range(TS):
        i = act.activation(R.wexps[:, j, :], R.top8[:, j, 0:R.topk], ACT.Exp, bias=R.negm[:, j:j + 1])
    i.then_inc(R.wexp, 1)


def route_tensor_transpose(K, R, pe, s):
    pe.wait_ge(R.comb, s + 1)
    for j in range(TS):
        i = pe.transpose(K.ps[1][0:E, W + j * P:W + (j + 1) * P], R.out[:, j, :], K.ident[:, :])
    i.then_inc(R.combt_ps, 1)


def route_vector_parts(K, R, dve, link, s):
    dve.wait_ge(R.combt_ps, s + 1)
    link(dve.tensor_copy(R.t32[:, :], K.ps[1][0:E, W:2 * W]))
    link(dve.tensor_copy(R.part[HI:HI + E, :], R.t32[:, :]))
    link(dve.tensor_tensor(R.rest[:, :], R.t32[:, :], R.part[HI:HI + E, :], ALU.subtract))
    link(dve.tensor_copy(R.mid[:, :], R.rest[:, :]))
    dve.tensor_copy(R.part[MID:MID + E, :], R.mid[:, :])
    dve.tensor_tensor(R.part[LO:LO + E, :], R.rest[:, :], R.mid[:, :], ALU.subtract).then_inc(R.parts, 1)



def stage_gated_experts(K, tag):
    nc = K.nc
    G = E // 2
    with ExitStack() as scope:
        K.scope = scope
        sb = K.sb
        N = Norm(K, tag)
        R = Router(K, tag, 2)
        xnt = sb(f"{tag}_xnt", [P, W])
        act_g = sb(f"{tag}_silu", [P, 2, W])
        gated = sb(f"{tag}_gated", [P, 2, W])
        hid = sb(f"{tag}_hidden", [P, 3, W])
        (link_s, xnt_ready, gu_ps, silu_ready, c_ps, gated_ready, hid_ready, y_ps, done, down_done, zeroed) = make_sems(
            K, tag, "dve_chain xnt_ready gate_up_product silu_ready comb_product gated_ready hidden_ready "
                    "y_product seq_done down_issued parts_zeroed")
        f = lambda n: field(K, "m1", n)
        GATE = [f("gate")[:, g * P:(g + 1) * P] for g in range(G)] + [f("shg")]
        UP = [f("up")[:, g * P:(g + 1) * P] for g in range(G)] + [f("shu")]
        DOWN = [f("down")[:, g * P:(g + 1) * P] for g in range(G)] + [f("shd")]
        ORDER = [G] + list(range(G))
        NG = G + 1
        with nc.Block() as block:
            K.start_loads(block, tag)

            @block.vector
            def _(dve):
                dve.sem_inc(done, 1)
                dve.wait_ge(K.consts_ready, K.N_CONST)
                dve.wait_ge(K.loaded["m1"], 16)
                link = chain(dve, link_s)
                link(dve.memset(R.part[:, :], 0.0))
                with dve.Fori(0, B) as s:
                    link = chain(dve, link_s)
                    norm_vector(K, N, dve, link, lambda j: K.x[:, bass.ds(s * W + j * P, P)], s)
                    dve.wait_ge(N.xt, s + 1)
                    dve.tensor_copy(xnt[:, :], K.ps[0][:, 0:W]).then_inc(xnt_ready, 1)
                    route_vector(K, R, dve, link, s, f("rb"))
                    route_vector_parts(K, R, dve, link, s)
                    for n, g in enumerate(ORDER):
                        dve.wait_ge(silu_ready, s * NG + n + 1)
                        if n >= 3:
                            dve.wait_ge(down_done, s * NG + n - 2)
                        dst = hid[:, n % 3, :] if g == G else gated[:, n % 2, :]
                        i = dve.tensor_tensor(dst, act_g[:, n % 2, :], K.ps[2 + n % 2][:, W:2 * W], ALU.mult)
                        if g == G:
                            link(i)
                            dve.sem_inc(gated_ready, 1)
                            dve.sem_inc(hid_ready, 1)
                        else:
                            i.then_inc(gated_ready, 1)
                            dve.wait_ge(gated_ready, s * NG + n + 1)
                            dve.wait_ge(c_ps, s * G + n)
                            dve.tensor_tensor(hid[:, n % 3, :], gated[:, n % 2, :], K.ps[4 + n % 2][:, 0:W],
                                              ALU.mult).then_inc(hid_ready, 1)
                    dve.wait_ge(y_ps, s + 1)
                    for j in range(TS):
                        xj = K.x[:, bass.ds(s * W + j * P, P)]
                        i = dve.scalar_tensor_tensor(xj, K.ps[6 + j][:, 0:P], 0.5, xj, ALU.mult, ALU.add)
                    i.then_inc(done, 1)

            @block.gpsimd
            def _(pool):
                with pool.Fori(0, B) as s:
                    norm_pool(K, N, pool, s)

            @block.scalar
            def _(act):
                with act.Fori(0, B) as s:
                    route_scalar(K, R, act, s)
                    for n in range(NG):
                        act.wait_ge(gu_ps, s * NG + n + 1)
                        if n >= 2:
                            act.wait_ge(gated_ready, s * NG + n - 1)
                        act.activation(act_g[:, n % 2, :], K.ps[2 + n % 2][:, 0:W], ACT.Silu).then_inc(silu_ready, 1)

            @block.tensor
            def _(pe):
                pe.wait_ge(K.consts_ready, K.N_CONST)
                pe.wait_ge(K.loaded["m1"], 16)
                with pe.Fori(0, B) as s:
                    norm_tensor(K, N, pe, s, K.ps[0])
                    pe.wait_ge(xnt_ready, s + 1)
                    pe.wait_ge(done, s + 1)
                    route_tensor_logits(K, R, pe, xnt, f("rw"))

                    def gate_up(n):
                        if n >= 2:
                            pe.wait_ge(gated_ready, s * NG + n - 1)
                        pe.matmul(K.ps[2 + n % 2][:, 0:W], GATE[ORDER[n]], xnt[:, :], start=True, stop=True)
                        pe.matmul(K.ps[2 + n % 2][:, W:2 * W], UP[ORDER[n]], xnt[:, :],
                                  start=True, stop=True).then_inc(gu_ps, 1)

                    def spread(n):
                        g = ORDER[n]
                        if n >= 3:
                            pe.wait_ge(hid_ready, s * NG + n - 1)
                        pe.matmul(K.ps[4 + n % 2][:, 0:W], K.sel64[:, 2 * g * 64:(2 * g + 2) * 64],
                                  R.part[:, :], start=True, stop=True).then_inc(c_ps, 1)

                    gate_up(0)
                    gate_up(1)
                    route_tensor_transpose(K, R, pe, s)
                    pe.wait_ge(R.parts, s + 1)
                    for n in range(NG):
                        if n >= 1 and n + 1 < NG:
                            gate_up(n + 1)
                        if n + 1 < NG:
                            spread(n + 1)
                        pe.wait_ge(hid_ready, s * NG + n + 1)
                        for j in range(TS):
                            i = pe.matmul(K.ps[6 + j][:, 0:P], hid[:, n % 3, j * P:(j + 1) * P], DOWN[ORDER[n]],
                                          start=(n == 0), stop=(n == NG - 1))
                        i.then_inc(down_done, 1)
                        if n == NG - 1:
                            pe.wait_ge(down_done, s * NG + NG)
                            pe.sem_inc(y_ps, 1)



def stage_gelu_experts(K, tag):
    nc = K.nc
    with ExitStack() as scope:
        K.scope = scope
        sb = K.sb
        N = Norm(K, tag)
        R = Router(K, tag, 4)
        xnt = sb(f"{tag}_xnt", [P, W])
        gelu = sb(f"{tag}_gelu", [P, 2, 2, W])
        hid = sb(f"{tag}_hidden", [P, 3, 2, W])
        (link_s, xnt_ready, h_ps, gelu_ready, c_ps, hid_ready, y_ps, done, down_done) = make_sems(
            K, tag, "dve_chain xnt_ready hidden_product gelu_ready comb_product hidden_ready "
                    "y_product seq_done down_issued")
        f = lambda n: field(K, "m2", n)
        w1, b1, w2 = f("w1"), f("b1"), f("w2")
        with nc.Block() as block:
            K.start_loads(block, tag)

            @block.vector
            def _(dve):
                dve.sem_inc(done, 1)
                dve.wait_ge(K.consts_ready, K.N_CONST)
                dve.wait_ge(K.loaded["m2"], 16)
                link = chain(dve, link_s)
                link(dve.memset(R.part[:, :], 0.0))
                with dve.Fori(0, B) as s:
                    link = chain(dve, link_s)
                    norm_vector(K, N, dve, link, lambda j: K.x[:, bass.ds(s * W + j * P, P)], s)
                    dve.wait_ge(N.xt, s + 1)
                    dve.tensor_copy(xnt[:, :], K.ps[0][:, 0:W]).then_inc(xnt_ready, 1)
                    route_vector(K, R, dve, link, s, f("rb"))
                    route_vector_parts(K, R, dve, link, s)
                    for e in range(E):
                        dve.wait_ge(gelu_ready, s * E + e + 1)
                        dve.wait_ge(c_ps, s * E + e + 1)
                        if e >= 3:
                            dve.wait_ge(down_done, s * E + e - 2)
                        for c in range(2):
                            i = dve.tensor_tensor(hid[:, e % 3, c, :], gelu[:, e % 2, c, :], K.ps[4 + e % 2][:, 0:W],
                                                  ALU.mult)
                        i.then_inc(hid_ready, 1)
                    dve.wait_ge(y_ps, s + 1)
                    for j in range(TS):
                        xj = K.x[:, bass.ds(s * W + j * P, P)]
                        i = dve.scalar_tensor_tensor(xj, K.ps[6 + j][:, 0:P], 0.5, xj, ALU.mult, ALU.add)
                    i.then_inc(done, 1)

            @block.gpsimd
            def _(pool):
                with pool.Fori(0, B) as s:
                    norm_pool(K, N, pool, s)

            @block.scalar
            def _(act):
                act.wait_ge(K.loaded["m2"], 16)
                with act.Fori(0, B) as s:
                    route_scalar(K, R, act, s)
                    for e in range(E):
                        act.wait_ge(h_ps, s * E + e + 1)
                        if e >= 2:
                            act.wait_ge(hid_ready, s * E + e - 1)
                        for c in range(2):
                            i = act.activation(gelu[:, e % 2, c, :], K.ps[2 + e % 2][:, c * W:(c + 1) * W], ACT.Gelu,
                                               bias=b1[:, 2 * e + c:2 * e + c + 1])
                        i.then_inc(gelu_ready, 1)

            @block.tensor
            def _(pe):
                pe.wait_ge(K.consts_ready, K.N_CONST)
                pe.wait_ge(K.loaded["m2"], 16)
                with pe.Fori(0, B) as s:
                    norm_tensor(K, N, pe, s, K.ps[0])
                    pe.wait_ge(xnt_ready, s + 1)
                    pe.wait_ge(done, s + 1)
                    route_tensor_logits(K, R, pe, xnt, f("rw"))

                    def hidden(e):
                        if e >= 2:
                            pe.wait_ge(gelu_ready, s * E + e - 1)
                        for c in range(2):
                            i = pe.matmul(K.ps[2 + e % 2][:, c * W:(c + 1) * W],
                                          w1[:, e * 256 + c * P:e * 256 + (c + 1) * P], xnt[:, :],
                                          start=True, stop=True)
                        i.then_inc(h_ps, 1)

                    def spread(e):
                        if e >= 2:
                            pe.wait_ge(hid_ready, s * E + e - 1)
                        pe.matmul(K.ps[4 + e % 2][:, 0:W], K.sel[0:PARTS, e * P:(e + 1) * P], R.part[:, :],
                                  start=True, stop=True).then_inc(c_ps, 1)

                    hidden(0)
                    hidden(1)
                    route_tensor_transpose(K, R, pe, s)
                    pe.wait_ge(R.parts, s + 1)
                    for j in range(TS):
                        pe.matmul(K.ps[6 + j][:, 0:P], R.t32[:, j * P:(j + 1) * P], f("b2")[0:E, :],
                                  start=True, stop=False)
                    spread(0)
                    spread(1)
                    for e in range(E):
                        pe.wait_ge(hid_ready, s * E + e + 1)
                        if e + 2 < E:
                            hidden(e + 2)
                            spread(e + 2)
                        for c in range(2):
                            for j in range(TS):
                                i = pe.matmul(K.ps[6 + j][:, 0:P], hid[:, e % 3, c, j * P:(j + 1) * P],
                                              w2[:, (2 * e + c) * P:(2 * e + c + 1) * P],
                                              start=False, stop=(e == E - 1 and c == 1))
                        i.then_inc(down_done, 1)
                    pe.wait_ge(down_done, s * E + E)
                    pe.sem_inc(y_ps, 1)



def stage_state_space(K, tag):
    nc = K.nc
    L, NS, KC = 4, 16, 4
    C = 2
    R = 4
    with ExitStack() as scope:
        K.scope = scope
        sb = K.sb
        xm = sb(f"{tag}_xm", [P, B * W])
        aneg = sb(f"{tag}_a_neg", [P, L, C * NS])
        xpad = sb(f"{tag}_xn_padded", [P, KC - 1 + S])
        xc = sb(f"{tag}_conv", [P, 2, C, S])
        zs = sb(f"{tag}_gate", [P, 2, C, S])
        dt = sb(f"{tag}_dt", [P, 2, C, S])
        du = sb(f"{tag}_dt_u", [P, 2, C, S])
        part = sb(f"{tag}_bc_parts", [96, 2, S], BF16)
        rest = sb(f"{tag}_bc_rest", [96, S])
        mid = sb(f"{tag}_bc_mid", [96, S], BF16)
        dtr = sb(f"{tag}_dt_rank", [P, S])
        v = sb(f"{tag}_dt_positive", [P, C, S])
        va = sb(f"{tag}_dt_abs", [P, C, S])
        ve = sb(f"{tag}_dt_exp", [P, C, S])
        vl = sb(f"{tag}_dt_ln", [P, C, S])
        vu = sb(f"{tag}_dt_one_plus", [P, C, S])
        vw = sb(f"{tag}_dt_correction", [P, C, S])
        da = sb(f"{tag}_decay", [P, R, C, S])
        csb = sb(f"{tag}_c_spread", [P, R, S])
        dbu = sb(f"{tag}_dbu", [P, R, C, S])
        h = sb(f"{tag}_state", [P, R, C, S])
        hc = sb(f"{tag}_state_c", [P, R, C, S])
        yf = sb(f"{tag}_y", [P, C, S])
        yg = sb(f"{tag}_y_gated", [P, C, S])

        N0 = Norm(K, f"{tag}_in")
        dve_s, exp_s, fold_s = make_sems(K, f"{tag}_in", "dve_chain a_exp folded")
        with nc.Block() as block:
            K.start_loads(block, tag)

            @block.vector
            def _(dve):
                link = chain(dve, dve_s)
                link(dve.memset(xpad[:, :], 0.0))
                link(dve.memset(da[:, :, 1, 0:1], 0.0))
                with dve.Fori(0, B) as s:
                    link = chain(dve, dve_s)
                    for j in range(TS):
                        i = dve.bn_stats(N0.bn[:, j, :], K.x[:, bass.ds(s * W + j * P, P)])
                    link(i)
                    for j in range(TS):
                        i = dve.bn_aggr(N0.mv[:, j, :], N0.bn[:, j, :])
                    i.then_inc(N0.stats, 1)
                    dve.wait_ge(N0.rstd, s + 1)
                    for j in range(TS):
                        dve.tensor_scalar(xm[:, bass.ds(s * W + j * P, P)], K.x[:, bass.ds(s * W + j * P, P)],
                                          N0.mv[:, j, 0:1], N0.rs[:, j:j + 1], ALU.subtract, ALU.mult)
                dve.wait_ge(exp_s, L)
                dve.tensor_scalar(aneg[:, :, :], aneg[:, :, :], -1.0, None, ALU.mult)

            @block.gpsimd
            def _(pool):
                with pool.Fori(0, B) as s:
                    norm_pool(K, N0, pool, s)
                pool.wait_ge(K.loaded["mb"], 16)
                for l in range(L):
                    taps, inx = field(K, "mb", f"taps{l}"), field(K, "mb", f"inx{l}")
                    for k in range(KC):
                        t = taps[:, k * 256:(k + 1) * 256]
                        pool.tensor_tensor(t, t, inx, ALU.mult).then_inc(fold_s, 1)

            @block.scalar
            def _(act):
                act.wait_ge(K.loaded["mb"], 16)
                for l in range(L):
                    act.activation(aneg[:, l, :], field(K, "mb", f"alog{l}"), ACT.Exp).then_inc(exp_s, 1)

        clear_sems(K)
        state_space_layers(K, tag, dict(locals()))
        clear_sems(K)
        add_s, = make_sems(K, tag, "added")
        with nc.Block() as block:
            @block.vector
            def _(dve):
                dve.tensor_tensor(K.x[:, :], K.x[:, :], xm[:, :], ALU.add).then_inc(add_s, 1)
                dve.wait_ge(add_s, 1)


AT = dict(dve_stats=0, dve_norm=1, pool_rstd=0, pe_in=0, act_in=1, pe_conv0=1, pe_conv1=2, pe_gate=3, act_conv=5,
          act_gate=6, pe_bc=4, act_bc=7, dve_bc=7, pe_dt=6, act_exp=9, act_ln=10, dve_ln=10, pool_dt=11,
          dve_y=2, pe_out=1, dve_add=5)


def state_space_layers(K, tag, m):
    nc = K.nc
    L, NS, KC, C, R = m["L"], m["NS"], m["KC"], m["C"], m["R"]
    (xm, aneg, xpad, xc, zs, dt, du, part, rest, mid, dtr, v, va, ve, vl, vu, vw, da, csb, dbu, h, hc, yf, yg) = (
        m[n] for n in "xm aneg xpad xc zs dt du part rest mid dtr v va ve vl vu vw da csb dbu h hc yf yg".split())
    flat = lambda a: a.rearrange("p c t -> p (c t)")
    halves = lambda a: a.unsqueeze(1).broadcast_to([P, C, S])
    with ExitStack() as scope:
        K.scope = scope
        N = Norm(K, tag)
        (dve_s, act_s, xn_ready, xin_ps, z_ps, xc_ready, z_ready, bc_ps, part_ready, dtr_ready, dt_ps,
         vu_ready, ln_ready, vw_ready, dt_ready, du_ready, b_ps, c_ps, c_ready, da_ready, h_ready, hc_ready, sum_done,
         yg_ready, out_ps, done, b_used) = make_sems(
            K, tag, "dve_chain act_chain xn_ready conv_product gate_product conv_ready gate_ready "
                    "bc_product parts_ready dt_rank_ready dt_product one_plus_ready ln_ready correction_ready dt_ready "
                    "dtu_ready b_spread c_spread c_ready decay_ready state_ready state_c_ready sum_issued "
                    "y_gated_ready out_product unit_done b_used")
        f = lambda l, n: field(K, "mb", f"{n}{l}")

        def over_units(eng, main):
            for l in range(L):
                main(l, 0, 0, (l - 1, B - 1) if l > 0 else None, (l, 1))
                with eng.Fori(0, (B - 2) // 2) as pair:
                    for d in (1, 2):
                        main(l, pair * 2 + d, d % 2, (l, pair * 2 + (d - 1)), (l, pair * 2 + (d + 1)))
                main(l, B - 1, 1, (l, B - 2), (l + 1, 0) if l + 1 < L else None)

        with nc.Block() as block:
            @block.vector
            def _(dve):
                dve.sem_inc(b_used, 2)
                dve.sem_inc(h_ready, R)
                dve.sem_inc(done, 2)

                def prepare(l, s, q, n):
                    u = s + l * B
                    xs = lambda j: xm[:, bass.ds(s * W + j * P, P)]
                    if n == AT["dve_stats"]:
                        link = chain(dve, dve_s)
                        if l > 0:
                            dve.wait_ge(done, u - B + 3)
                        for j in range(TS):
                            i = dve.bn_stats(N.bn[:, j, :], xs(j))
                        link(i)
                        for j in range(TS):
                            i = dve.bn_aggr(N.mv[:, j, :], N.bn[:, j, :])
                        i.then_inc(N.stats, 1)
                    if n == AT["dve_norm"]:
                        dve.wait_ge(N.rstd, u + 1)
                        for j in range(TS):
                            i = dve.tensor_scalar(N.out[:, j * P:(j + 1) * P], xs(j), N.mv[:, j, 0:1],
                                                  N.rs[:, j:j + 1], ALU.subtract, ALU.mult)
                        i.then_inc(N.xn, 1)
                    if n == AT["dve_bc"]:
                        link = chain(dve, dve_s)
                        dve.wait_ge(bc_ps, u + 1)
                        link(dve.tensor_copy(part[:, q, :], K.ps[0][0:96, 0:S]))
                        link(dve.tensor_tensor(rest[:, :], K.ps[0][0:96, 0:S], part[:, q, :], ALU.subtract))
                        link(dve.tensor_copy(mid[:, :], rest[:, :]))
                        dve.tensor_copy(part[32:64, q, :], mid[32:64, :]).then_inc(part_ready, 1)
                        dve.tensor_tensor(part[64:96, q, :], rest[64:96, :], mid[64:96, :],
                                          ALU.subtract).then_inc(part_ready, 1)
                    if n == AT["dve_ln"]:
                        link = chain(dve, dve_s)
                        dve.wait_ge(vu_ready, u + 1)
                        link(dve.scalar_tensor_tensor(vw[:, :, :], vu[:, :, :], -1.0, ve[:, :, :], ALU.add,
                                                      ALU.subtract))
                        dve.tensor_tensor(vw[:, :, :], vw[:, :, :], v[:, :, :], ALU.subtract).then_inc(vw_ready, 1)

                def end(l, s, q, n):
                    u = s + l * B
                    if n == AT["dve_y"]:
                        link = chain(dve, dve_s)
                        dve.wait_ge(sum_done, (u + 1) * NS + R)
                        for c in range(C):
                            i = dve.scalar_tensor_tensor(yf[:, c, :], xc[:, q, c, :], f(l, "dsk")[:, c:c + 1],
                                                         K.ps[6 + q][:, c * S:(c + 1) * S], ALU.mult, ALU.add)
                        link(i)
                        dve.tensor_tensor(yg[:, :, :], yf[:, :, :], zs[:, q, :, :], ALU.mult).then_inc(yg_ready, 1)
                    if n == AT["dve_add"]:
                        dve.wait_ge(out_ps, u + 1)
                        xs = xm[:, bass.ds(s * W, W)]
                        dve.tensor_tensor(xs, K.ps[6 + q][:, 0:W], xs, ALU.add).then_inc(done, 1)

                def input_term(g, q, n):
                    dve.wait_ge(h_ready, g + 1)
                    dve.wait_ge(b_ps, g + 1)
                    dve.tensor_tensor(dbu[:, n % R, :, :], du[:, q, :, :], halves(K.ps[2 + n % 2][:, 0:S]),
                                      ALU.mult).then_inc(b_used, 1)

                def main(l, s, q, last, nxt):
                    u = s + l * B
                    for n in range(NS):
                        g = u * NS + n
                        if n + 1 < NS:
                            input_term(g + 1, q, n + 1)
                        elif nxt:
                            dve.wait_ge(du_ready, u + 2)
                            input_term(g + 1, 1 - q, 0)
                        dve.wait_ge(b_used, g + 3)
                        dve.wait_ge(hc_ready, g + 1)
                        dve.wait_ge(da_ready, g + 1)
                        dve.tensor_tensor_scan(flat(h[:, n % R, :, :]), flat(da[:, n % R, :, :]),
                                               flat(dbu[:, n % R, :, :]), 0.0, ALU.mult,
                                               ALU.add).then_inc(h_ready, 1)
                        if last:
                            end(*last, 1 - q, n)
                        if nxt:
                            prepare(*nxt, 1 - q, n)
                for n in range(NS):
                    prepare(0, 0, 0, n)
                dve.wait_ge(du_ready, 1)
                input_term(0, 0, 0)
                over_units(dve, main)
                for n in range(NS):
                    end(L - 1, B - 1, 1, n)

            @block.gpsimd
            def _(pool):
                pool.sem_inc(hc_ready, R)

                def prepare(l, s, q, n):
                    u = s + l * B
                    if n == AT["pool_rstd"]:
                        norm_pool(K, N, pool, u)
                    if n == AT["pool_dt"]:
                        pool.wait_ge(ln_ready, u + 1)
                        pool.wait_ge(vw_ready, u + 1)
                        pool.tensor_tensor(dt[:, q, :, :], vl[:, :, :], vw[:, :, :],
                                           ALU.subtract).then_inc(dt_ready, 1)
                        pool.wait_ge(dt_ready, u + 1)
                        pool.tensor_tensor(du[:, q, :, :], dt[:, q, :, :], xc[:, q, :, :], ALU.mult).then_inc(du_ready, 1)

                def main(l, s, q, last, nxt):
                    for n in range(NS):
                        g = (s + l * B) * NS + n
                        pool.wait_ge(c_ready, g + 3)
                        pool.wait_ge(sum_done, g + 1)
                        pool.wait_ge(h_ready, g + 1 + R)
                        pool.tensor_tensor(hc[:, n % R, :, :], h[:, n % R, :, :], halves(csb[:, n % R, :]),
                                           ALU.mult).then_inc(hc_ready, 1)
                        if nxt:
                            prepare(*nxt, 1 - q, n)
                for n in range(NS):
                    prepare(0, 0, 0, n)
                over_units(pool, main)

            @block.scalar
            def _(act):
                act.sem_inc(c_ready, 2)

                def prepare(l, s, q, n):
                    u = s + l * B
                    if n == AT["act_in"]:
                        act.wait_ge(N.xt, u + 1)
                        act.activation(xpad[:, KC - 1:KC - 1 + S], K.ps[0][:, 0:S], ACT.Identity,
                                       bias=f(l, "lnb"), scale=f(l, "lnw")).then_inc(xn_ready, 1)
                    if n == AT["act_conv"]:
                        act.wait_ge(xin_ps, u + 1)
                        for c in range(C):
                            i = act.activation(xc[:, q, c, :], K.ps[0][:, c * S:(c + 1) * S], ACT.Silu,
                                               bias=f(l, "cb")[:, c:c + 1])
                        i.then_inc(xc_ready, 1)
                        act.wait_ge(z_ps, u + 1)
                        act.activation(flat(zs[:, q, :, :]), K.ps[1][:, :], ACT.Silu).then_inc(z_ready, 1)
                    if n == AT["act_bc"]:
                        act.wait_ge(bc_ps, u + 1)
                        act.activation(dtr[96:104, :], K.ps[0][96:104, 0:S], ACT.Copy).then_inc(dtr_ready, 1)
                    if n == AT["act_exp"]:
                        act.sem_clear(act_s)
                        act.wait_ge(dt_ps, u + 1)
                        for c in range(C):
                            i = act.activation(va[:, c, :], K.ps[1][:, c * S:(c + 1) * S], ACT.Abs,
                                               bias=f(l, "dtb")[:, c:c + 1])
                        i.then_inc(act_s, 1)
                        for c in range(C):
                            act.activation(v[:, c, :], K.ps[1][:, c * S:(c + 1) * S], ACT.Relu,
                                           bias=f(l, "dtb")[:, c:c + 1])
                        act.wait_ge(act_s, 1)
                        act.activation(ve[:, :, :], va[:, :, :], ACT.Exp, scale=-1.0).then_inc(act_s, 1)
                    if n == AT["act_ln"]:
                        act.wait_ge(act_s, 2)
                        act.activation(vu[:, :, :], ve[:, :, :], ACT.Identity, bias=K.ones[:, 0:1]).then_inc(vu_ready, 1)
                        act.wait_ge(vu_ready, u + 1)
                        act.activation(vl[:, :, :], vu[:, :, :], ACT.Ln).then_inc(ln_ready, 1)

                def main(l, s, q, last, nxt):
                    u = s + l * B
                    act.wait_ge(du_ready, u + 1)
                    for n in range(NS):
                        g = u * NS + n
                        act.wait_ge(h_ready, g + 1)
                        for c in range(C):
                            i = act.activation(da[:, n % R, c, c:S], dt[:, q, c, c:S], ACT.Exp,
                                               scale=aneg[:, l, c * NS + n:c * NS + n + 1])
                        i.then_inc(da_ready, 1)
                        act.wait_ge(c_ps, g + 1)
                        act.wait_ge(hc_ready, g + 1)
                        act.activation(csb[:, n % R, :], K.ps[4 + n % 2][:, 0:S], ACT.Copy).then_inc(c_ready, 1)
                        if nxt:
                            prepare(*nxt, 1 - q, n)
                for n in range(NS):
                    prepare(0, 0, 0, n)
                over_units(act, main)

            @block.tensor
            def _(pe):
                pe.sem_inc(sum_done, R)

                def convolve(l, c):
                    for k in range(KC):
                        i = pe.matmul(K.ps[0][:, c * S:(c + 1) * S],
                                      f(l, "taps")[:, k * 256 + c * P:k * 256 + (c + 1) * P],
                                      xpad[:, k:k + S], start=(k == 0), stop=(k == KC - 1))
                    return i

                def prepare(l, s, q, n):
                    u = s + l * B
                    if n == AT["pe_in"]:
                        norm_tensor(K, N, pe, u, K.ps[0])
                    if n == AT["pe_conv0"]:
                        pe.wait_ge(xn_ready, u + 1)
                        convolve(l, 0)
                    if n == AT["pe_conv1"]:
                        convolve(l, 1).then_inc(xin_ps, 1)
                    if n == AT["pe_gate"]:
                        for c in range(C):
                            i = pe.matmul(K.ps[1][:, c * S:(c + 1) * S], f(l, "inz")[:, c * P:(c + 1) * P],
                                          xpad[:, KC - 1:KC - 1 + S], start=True, stop=True)
                        i.then_inc(z_ps, 1)
                    if n == AT["pe_bc"]:
                        pe.wait_ge(xc_ready, u + 1)
                        for c in range(C):
                            i = pe.matmul(K.ps[0][0:104, 0:S], f(l, "xp")[:, c * 104:(c + 1) * 104],
                                          xc[:, q, c, :], start=(c == 0), stop=(c == C - 1))
                        i.then_inc(bc_ps, 1)
                    if n == AT["pe_dt"]:
                        pe.wait_ge(dtr_ready, u + 1)
                        pe.wait_ge(z_ready, u + 1)
                        for c in range(C):
                            i = pe.matmul(K.ps[1][:, c * S:(c + 1) * S], f(l, "dtw")[96:104, c * P:(c + 1) * P],
                                          dtr[96:104, :], start=True, stop=True)
                        i.then_inc(dt_ps, 1)

                def spread(g, q, n):
                    pe.wait_ge(b_used, g + 1)
                    pe.matmul(K.ps[2 + n % 2][:, 0:S], K.sel[:, n * P:(n + 1) * P], part[:, q, :],
                              start=True, stop=True).then_inc(b_ps, 1)
                    pe.wait_ge(c_ready, g + 1)
                    pe.matmul(K.ps[4 + n % 2][:, 0:S], K.sel[:, (NS + n) * P:(NS + n + 1) * P], part[:, q, :],
                              start=True, stop=True).then_inc(c_ps, 1)

                def out_product(l, s, q):
                    pe.wait_ge(yg_ready, s + l * B + 1)
                    for j in range(TS):
                        for c in range(C):
                            i = pe.matmul(K.ps[6 + q][:, j * P:(j + 1) * P], yg[:, c, j * P:(j + 1) * P],
                                          f(l, "outw")[:, c * P:(c + 1) * P], start=(c == 0), stop=(c == C - 1))
                    i.then_inc(out_ps, 1)

                AHEAD = 3
                def main(l, s, q, last, nxt):
                    u = s + l * B
                    for n in range(NS):
                        g = u * NS + n
                        if n + AHEAD < NS:
                            spread(g + AHEAD, q, n + AHEAD)
                        elif nxt:
                            if n + AHEAD == NS:
                                pe.wait_ge(part_ready, 2 * (u + 2))
                            spread(g + AHEAD, 1 - q, n + AHEAD - NS)
                        if n == 0:
                            pe.wait_ge(done, u + 1)
                        pe.wait_ge(hc_ready, g + 1 + R)
                        pe.matmul(K.ps[6 + q][:, :], K.ident[:, :], flat(hc[:, n % R, :, :]),
                                  start=(n == 0), stop=(n == NS - 1)).then_inc(sum_done, 1)
                        if last and n == AT["pe_out"]:
                            out_product(*last, 1 - q)
                        if nxt:
                            prepare(*nxt, 1 - q, n)
                for n in range(NS):
                    prepare(0, 0, 0, n)
                pe.wait_ge(part_ready, 2)
                for n in range(AHEAD):
                    spread(n, 0, n)
                over_units(pe, main)
                out_product(L - 1, B - 1, 1)



def stage_window_linear_attention(K, tag):
    nc = K.nc
    H, DH, HALF = 16, 8, 32
    G, KW = 4, 160
    KEY0 = (0, S - KW)
    BAND0 = (HALF, 0)
    BW = P + 2 * HALF
    SCALE = float(np.float32(1.0 / np.sqrt(DH)))
    with ExitStack() as scope:
        K.scope = scope
        sb = K.sb
        N = Norm(K, f"{tag}_a")
        M = Norm(K, f"{tag}_b")
        ht = sb(f"{tag}_ht", [P, W])
        band = field(K, "a2", "band").rearrange("p (h j) -> p h j", h=H)
        qmin = sb(f"{tag}_qmin", [P, S])
        qmax = sb(f"{tag}_qmax", [P, S])
        ql = sb(f"{tag}_ql", [P, S])
        klin = sb(f"{tag}_klin", [P, TS, P])
        kmin = sb(f"{tag}_kmin", [P, TS, P])
        kl = sb(f"{tag}_kl", [P, TS, P])
        vo = sb(f"{tag}_v_ones", [P, TS, 2 * P])
        kvs = sb(f"{tag}_kv_ksum", [P, 2 * P])
        den = sb(f"{tag}_den", [P, S])
        dinv = sb(f"{tag}_dinv", [P, S])
        lint = sb(f"{tag}_lin_t", [P, S])
        q4 = sb(f"{tag}_q4", [P, G, S])
        k4 = sb(f"{tag}_k4", [P, G, S])
        vw = sb(f"{tag}_v_window", [P, TS, P])
        vtail = sb(f"{tag}_v_tail", [HALF, P])
        sc = sb(f"{tag}_scores", [P, 2, TS, KW])
        mx = sb(f"{tag}_max", [P, H, TS])
        nmx = sb(f"{tag}_nmax", [P, H, TS])
        rsum = sb(f"{tag}_rsum", [P, TS, H])
        rinv = sb(f"{tag}_rinv", [P, TS, H])
        pr = sb(f"{tag}_probs", [P, 3, TS, KW])
        pt = sb(f"{tag}_probst", [P, 2, 2, TS * P])
        win = sb(f"{tag}_win", [P, TS, P])
        wint = sb(f"{tag}_win_t", [P, S])
        g1 = sb(f"{tag}_gate1", [P, S])
        gate = sb(f"{tag}_gate", [P, S])
        diff = sb(f"{tag}_diff", [P, S])
        gd = sb(f"{tag}_gate_diff", [P, S])
        ot = sb(f"{tag}_out_t", [P, S])
        (dve_s, masked, ht_ready, ql_ps, qmin_ready, qexp_ready, kv_ps, kmin_ready, kexp_ready, kl_ready, kvs_ps,
         kvs_ready, lin_ps, lin_ready, qk_ps, qk_ready, v_ps, v_ready, sc_ps, max_ready, exp_ready, pt_ps, pt_ready,
         o_ps, win_ready, wint_ps, wint_ready, g1_ps, g1_ready, g2_ps, gate_ready, ot_ready, y_ps, done,
         hold) = make_sems(
            K, tag, "dve_chain band_masked ht_ready ql_product qmin_ready qexp_ready kv_product kmin_ready "
                    "kexp_ready kl_ready kv_sum_product kv_sum_ready lin_product lin_ready qk_product qk_ready "
                    "v_product v_ready scores_product max_ready exp_ready probst_product probst_ready out_product "
                    "win_ready wint_product wint_ready gate1_product gate1_ready gate2_product gate_ready "
                    "mix_ready y_product seq_done hold")
        f = lambda n: field(K, "a2", n)
        STEPS = H + 3
        at, _ = pack_offset("a2", "wkl")
        wkv = K.pack["a2"][:, at:at + 2 * P]
        at, _ = pack_offset("a2", "bkl")
        bkv = K.pack["a2"][:, at:at + 2 * P]
        with nc.Block() as block:
            K.start_loads(block, tag)

            @block.vector
            def _(dve):
                dve.sem_inc(done, 1)
                dve.wait_ge(K.loaded["a2"], 16)
                link = chain(dve, dve_s)
                link(dve.memset(vo[:, :, :], 1.0))
                dve.wait_ge(masked, 2)
                with dve.Fori(0, B) as s:
                    link = chain(dve, dve_s)
                    norm_vector(K, N, dve, link, lambda j: K.x[:, bass.ds(s * W + j * P, P)], s)
                    dve.wait_ge(N.xn, s + 1)
                    norm_vector(K, M, dve, link, lambda j: N.out[:, j * P:(j + 1) * P], s)
                    dve.wait_ge(ql_ps, s + 1)
                    dve.tensor_scalar(qmin[:, :], K.ps[1][:, 0:S], f("bql"), 0.0, ALU.add, ALU.min).then_inc(qmin_ready, 1)
                    link(dve.tensor_scalar(qmax[:, :], K.ps[1][:, 0:S], f("bql"), 0.0, ALU.add, ALU.max))
                    dve.wait_ge(kv_ps, s + 1)
                    for j in range(TS):
                        dve.tensor_tensor(klin[:, j, :], K.ps[7][:, j * W:j * W + P], bkv[:, 0:P], ALU.add)
                        i = dve.tensor_tensor(vo[:, j, 0:P], K.ps[7][:, j * W + P:(j + 1) * W], bkv[:, P:2 * P], ALU.add)
                    link(i)
                    dve.tensor_scalar(kmin[:, :, :], klin[:, :, :], 0.0, None, ALU.min).then_inc(kmin_ready, 1)
                    dve.wait_ge(kexp_ready, s + 1)
                    dve.scalar_tensor_tensor(kl[:, :, :], klin[:, :, :], 0.0, kmin[:, :, :], ALU.max, ALU.add)\
                       .then_inc(kl_ready, 1)
                    dve.tensor_tensor(ql[:, :], qmax[:, :], qmin[:, :], ALU.add).then_inc(kl_ready, 1)
                    for g in range(G):
                        dve.wait_ge(qk_ps, s * G + g + 1)
                        bank = K.ps[(1, 6)[g % 2]]
                        dve.tensor_scalar(q4[:, g, :], bank[:, 0:S], f("bq4")[:, g:g + 1], SCALE, ALU.add, ALU.mult)
                        dve.tensor_scalar(k4[:, g, :], bank[:, S:2 * S], f("bk4")[:, g:g + 1], None,
                                          ALU.add).then_inc(qk_ready, 1)
                    dve.wait_ge(v_ps, s + 1)
                    for j in range(TS):
                        dve.tensor_tensor(vw[:, j, :], K.ps[7][:, j * P:(j + 1) * P], f("bvc"), ALU.add)
                    dve.tensor_tensor(vtail[:, :], K.ps[7][0:HALF, 2 * P:3 * P], f("bvc")[0:HALF, :],
                                      ALU.add).then_inc(v_ready, 1)

                    for i in range(STEPS):
                        if i < H:
                            dve.wait_ge(sc_ps, s * H + i + 1)
                            if i >= 2:
                                dve.wait_ge(exp_ready, s * H + i - 1)
                            dve.sem_inc(hold, 1)
                            for t in range(TS):
                                k = dve.tensor_tensor_reduce(
                                    sc[:, i % 2, t, :], K.ps[2 + i % 2][:, t * KW:(t + 1) * KW],
                                    band[:, i, BAND0[t]:BAND0[t] + KW], 1.0, -3e38, ALU.add, ALU.max, mx[:, i, t:t + 1])
                            link(k)
                            dve.tensor_scalar(nmx[:, i, :], mx[:, i, :], -1.0, None, ALU.mult).then_inc(max_ready, 1)
                        if i == 4:
                            dve.wait_ge(kvs_ps, s + 1)
                            dve.tensor_copy(kvs[:, :], K.ps[0][:, 0:2 * P]).then_inc(kvs_ready, 1)
                        if i == 8:
                            dve.wait_ge(lin_ps, s + 1)
                            link(dve.tensor_scalar(den[:, :], K.ps[0][:, S:2 * S], 1e-6, None, ALU.add))
                            link(dve.reciprocal(dinv[:, :], den[:, :]))
                            dve.tensor_tensor(lint[:, :], K.ps[0][:, 0:S], dinv[:, :], ALU.mult).then_inc(lin_ready, 1)
                    dve.wait_ge(exp_ready, s * H + H)
                    link(dve.reciprocal(rinv[:, :, :], rsum[:, :, :]))
                    dve.wait_ge(o_ps, s * H + H)
                    for j in range(TS):
                        i = dve.tensor_tensor(win[:, j, :].rearrange("p (h d) -> p h d", h=H),
                                              K.ps[6][:, j * P:(j + 1) * P].rearrange("p (h d) -> p h d", h=H),
                                              rinv[:, j, :].unsqueeze(2).broadcast_to([P, H, DH]), ALU.mult)
                    i.then_inc(win_ready, 1)
                    dve.wait_ge(wint_ps, s + 1)
                    dve.tensor_copy(wint[:, :], K.ps[7][:, 0:S]).then_inc(wint_ready, 1)
                    dve.wait_ge(wint_ready, s + 1)
                    link(dve.tensor_tensor(diff[:, :], lint[:, :], wint[:, :], ALU.subtract))
                    dve.wait_ge(gate_ready, s + 1)
                    link(dve.tensor_tensor(gd[:, :], gate[:, :], diff[:, :], ALU.mult))
                    dve.tensor_tensor(ot[:, :], gd[:, :], wint[:, :], ALU.add).then_inc(ot_ready, 1)
                    xs = K.x[:, bass.ds(s * W, W)]
                    link(dve.tensor_tensor(xs, xs, N.out[:, :], ALU.add))
                    for j in range(TS):
                        xj = K.x[:, bass.ds(s * W + j * P, P)]
                        i = dve.tensor_tensor(xj, xj, f("bo"), ALU.add)
                    link(i)
                    dve.wait_ge(y_ps, s + 1)
                    dve.tensor_tensor(xs, K.ps[0][:, 0:W], xs, ALU.add).then_inc(done, 1)

            @block.gpsimd
            def _(pool):
                pool.wait_ge(K.loaded["a2"], 16)
                pool.affine_select(out=band, in_=band, compare_op=ALU.is_ge, fill=-1e30, base=0,
                                   pattern=[[0, H], [1, BW]], channel_multiplier=-1).then_inc(masked, 1)
                pool.wait_ge(masked, 1)
                pool.affine_select(out=band, in_=band, compare_op=ALU.is_ge, fill=-1e30, base=2 * HALF,
                                   pattern=[[0, H], [-1, BW]], channel_multiplier=1).then_inc(masked, 1)
                with pool.Fori(0, B) as s:
                    norm_pool(K, N, pool, s)
                    norm_pool(K, M, pool, s)

            @block.scalar
            def _(act):
                act.wait_ge(K.loaded["a2"], 16)
                with act.Fori(0, B) as s:
                    act.wait_ge(M.xt, s + 1)
                    act.activation(ht[:, :], K.ps[0][:, 0:W], ACT.Identity, bias=f("lnb"), scale=f("lng")).then_inc(ht_ready, 1)
                    act.wait_ge(qmin_ready, s + 1)
                    act.activation(qmin[:, :], qmin[:, :], ACT.Exp)
                    act.wait_ge(kmin_ready, s + 1)
                    act.activation(kmin[:, :, :], kmin[:, :, :], ACT.Exp).then_inc(kexp_ready, 1)
                    for i in range(STEPS):
                        if i < H:
                            act.wait_ge(max_ready, s * H + i + 1)
                            if i >= 3:
                                act.wait_ge(pt_ps, s * H + i - 2)
                            for t in range(TS):
                                k = act.activation(pr[:, i % 3, t, :], sc[:, i % 2, t, :], ACT.Exp,
                                                   bias=nmx[:, i, t:t + 1], accum_out=rsum[:, t, i:i + 1])
                            k.then_inc(exp_ready, 1)
                        if 2 <= i < H + 2:
                            h = i - 2
                            act.wait_ge(pt_ps, s * H + h + 1)
                            if h >= 2:
                                act.wait_ge(o_ps, s * H + h - 1)
                            act.activation(pt[:, h % 2, 0, :], K.ps[4 + h % 2][:, 0:W], ACT.Copy)
                            act.activation(pt[0:HALF, h % 2, 1, :], K.ps[4 + h % 2][0:HALF, W:2 * W],
                                           ACT.Copy).then_inc(pt_ready, 1)
                    act.wait_ge(g1_ps, s + 1)
                    act.activation(g1[:, :], K.ps[7][:, S:2 * S], ACT.Relu, bias=f("bg1")).then_inc(g1_ready, 1)
                    act.wait_ge(g2_ps, s + 1)
                    act.activation(gate[:, :], K.ps[1][:, 0:S], ACT.Sigmoid, bias=f("bg2")).then_inc(gate_ready, 1)

            @block.tensor
            def _(pe):
                pe.wait_ge(K.consts_ready, K.N_CONST)
                pe.wait_ge(K.loaded["a2"], 16)
                with pe.Fori(0, B) as s:
                    norm_tensor(K, M, pe, s, K.ps[0])
                    pe.wait_ge(ht_ready, s + 1)
                    pe.wait_ge(done, s + 1)
                    pe.matmul(K.ps[1][:, 0:S], f("wql"), ht[:, :], start=True, stop=True).then_inc(ql_ps, 1)
                    for j in range(TS):
                        i = pe.matmul(K.ps[7][:, j * W:(j + 1) * W], ht[:, j * P:(j + 1) * P], wkv, start=True, stop=True)
                    i.then_inc(kv_ps, 1)
                    for g in range(G):
                        bank = K.ps[(1, 6)[g % 2]]
                        if g == 0:
                            pe.wait_ge(kmin_ready, s + 1)
                        if g >= 2:
                            pe.wait_ge(qk_ready, s * G + g - 1)
                        pe.matmul(bank[:, 0:S], f("wq4")[:, g * P:(g + 1) * P], ht[:, :], start=True, stop=True)
                        pe.matmul(bank[:, S:2 * S], f("wk4")[:, g * P:(g + 1) * P], ht[:, :],
                                  start=True, stop=True).then_inc(qk_ps, 1)
                    for j in range(TS):
                        pe.matmul(K.ps[7][:, j * P:(j + 1) * P], ht[:, j * P:(j + 1) * P], f("wvc"), start=True, stop=True)
                    pe.matmul(K.ps[7][0:HALF, 2 * P:3 * P], ht[:, P - HALF:P], f("wvc"),
                              start=True, stop=True).then_inc(v_ps, 1)
                    pe.wait_ge(kl_ready, 2 * (s + 1))
                    for j in range(TS):
                        i = pe.matmul(K.ps[0][:, 0:2 * P], kl[:, j, :], vo[:, j, :], start=(j == 0), stop=(j == TS - 1))
                    i.then_inc(kvs_ps, 1)
                    pe.wait_ge(v_ready, s + 1)
                    pe.wait_ge(qk_ready, s * G + G)
                    for i in range(STEPS):
                        if i < H:
                            g, r = i // 4, 32 * (i % 4)
                            if i >= 2:
                                pe.wait_ge(max_ready, s * H + i - 1)
                            for t in range(TS):
                                k = pe.matmul(K.ps[2 + i % 2][:, t * KW:(t + 1) * KW],
                                              q4[r:r + 32, g, t * P:(t + 1) * P], k4[r:r + 32, g, KEY0[t]:KEY0[t] + KW],
                                              start=True, stop=True)
                            k.then_inc(sc_ps, 1)
                        if i == 6:
                            pe.wait_ge(kvs_ready, s + 1)
                            pe.matmul(K.ps[0][:, 0:S], kvs[:, 0:P], ql[:, :], start=True, stop=True)
                            pe.matmul(K.ps[0][:, S:2 * S], kvs[:, P:2 * P], ql[:, :], start=True, stop=True).then_inc(lin_ps, 1)
                        if 2 <= i < H + 2:
                            h = i - 2
                            pe.wait_ge(exp_ready, s * H + h + 1)
                            if h >= 2:
                                pe.wait_ge(pt_ready, s * H + h - 1)
                            bank, pb = K.ps[4 + h % 2], pr[:, h % 3, :, :]
                            pe.transpose(bank[:, 0:P], pb[:, 0, 0:P], K.ident[:, :])
                            pe.transpose(bank[:, P:2 * P], pb[:, 1, HALF:KW], K.ident[:, :])
                            pe.transpose(bank[0:HALF, 2 * P:3 * P], pb[:, 0, P:KW], K.ident[:, :])
                            pe.transpose(bank[0:HALF, 3 * P:4 * P], pb[:, 1, 0:HALF], K.ident[:, :]).then_inc(pt_ps, 1)
                        if 3 <= i:
                            h = i - 3
                            pe.wait_ge(pt_ready, s * H + h + 1)
                            c = slice(h * DH, (h + 1) * DH)
                            for t in range(TS):
                                o = K.ps[6][:, t * P + h * DH:t * P + (h + 1) * DH]
                                pe.matmul(o, pt[:, h % 2, 0, t * P:(t + 1) * P], vw[:, t, c], start=True, stop=False)
                                k = pe.matmul(o, pt[0:HALF, h % 2, 1, t * P:(t + 1) * P],
                                              vw[0:HALF, 1, c] if t == 0 else vtail[:, c], start=False, stop=True)
                            k.then_inc(o_ps, 1)
                    pe.wait_ge(win_ready, s + 1)
                    for j in range(TS):
                        i = pe.transpose(K.ps[7][:, j * P:(j + 1) * P], win[:, j, :], K.ident[:, :])
                    i.then_inc(wint_ps, 1)
                    pe.wait_ge(lin_ready, s + 1)
                    pe.wait_ge(wint_ready, s + 1)
                    for n, src in enumerate((lint, wint, ht)):
                        i = pe.matmul(K.ps[7][:, S:2 * S], f("wg1")[:, n * P:(n + 1) * P], src[:, :],
                                      start=(n == 0), stop=(n == 2))
                    i.then_inc(g1_ps, 1)
                    pe.wait_ge(g1_ready, s + 1)
                    pe.matmul(K.ps[1][:, 0:S], f("wg2"), g1[:, :], start=True, stop=True).then_inc(g2_ps, 1)
                    pe.wait_ge(ot_ready, s + 1)
                    for j in range(TS):
                        i = pe.matmul(K.ps[0][:, j * P:(j + 1) * P], ot[:, j * P:(j + 1) * P], f("wo"), start=True, stop=True)
                    i.then_inc(y_ps, 1)



def stage_quantised_ffn(K, tag):
    nc = K.nc
    NB, U = 3, 4
    with ExitStack() as scope:
        K.scope = scope
        sb = K.sb
        w = sb(f"{tag}_w", [P, 6 * P])
        bn = sb(f"{tag}_bn", [P, U, TS, 6])
        mv = sb(f"{tag}_mv", [P, U, TS, 2])
        rs = sb(f"{tag}_rs", [P, U, TS])
        hcur = sb(f"{tag}_h", [P, U, W])
        hb = sb(f"{tag}_h_bias", [P, U, W])
        ht = sb(f"{tag}_ht", [P, U, W])
        y = sb(f"{tag}_y", [P, U, W])
        yn = sb(f"{tag}_yn", [P, U, W])
        gt = sb(f"{tag}_gelu_t", [P, U, W])
        (dve_s, pool_s, lora_ps, w_ready, stats, rstd, h_ready, ht_ps, ht_ready, y_ps, yn_ready, ynt_ps, gt_ready,
         z_ps, hb_ready, pool_hold, y_sb) = make_sems(
            K, tag, "dve_chain pool_chain lora_product w_ready stats rstd h_ready ht_product ht_ready y_product "
                    "yn_ready ynt_product gelu_ready z_product h_bias_ready pool_hold y_ready")
        f = lambda n: field(K, "f3", n)
        bias = f("bias")
        NL = (NB + 1) * U
        with nc.Block() as block:
            K.start_loads(block, tag)

            @block.vector
            def _(dve):
                dve.wait_ge(K.loaded["f3"], 16)
                dve.wait_ge(K.loaded_q, 16)
                link = chain(dve, dve_s)
                link(dve.tensor_scalar(w[:, :], K.qw[:, :], 7.5, 1.0 / 7.5, ALU.subtract, ALU.mult))
                link(dve.tensor_tensor(w[:, :], w[:, :], f("scale"), ALU.mult))
                dve.wait_ge(lora_ps, 1)
                dve.tensor_tensor(w[:, 0:512], w[:, 0:512], K.ps[0][:, :], ALU.add).then_inc(w_ready, 1)
                dve.tensor_tensor(w[:, 512:768], w[:, 512:768], K.ps[1][:, 0:256], ALU.add).then_inc(w_ready, 1)
                with dve.Fori(0, B // U) as s:
                    link = chain(dve, dve_s)

                    def statistics(u, src):
                        for j in range(TS):
                            i = dve.bn_stats(bn[:, u, j, :], src(j))
                        link(i)
                        for j in range(TS):
                            i = dve.bn_aggr(mv[:, u, j, :], bn[:, u, j, :])
                        i.then_inc(stats, 1)

                    def normalise(u, src, dst):
                        for j in range(TS):
                            i = dve.tensor_scalar(dst[:, u, j * P:(j + 1) * P], src(j), mv[:, u, j, 0:1],
                                                  rs[:, u, j:j + 1], ALU.subtract, ALU.mult)
                        return i

                    xt = lambda u: lambda j: K.x[:, bass.ds((s * U + u) * W + j * P, P)]
                    yt = lambda u: lambda j: y[:, u, j * P:(j + 1) * P]
                    for u in range(U):
                        statistics(u, xt(u))
                    for u in range(U):
                        dve.wait_ge(rstd, s * NL + u + 1)
                        normalise(u, xt(u), hcur).then_inc(h_ready, 1)
                    for b in range(NB):
                        e = s * (NB * U) + b * U
                        for u in range(U):
                            dve.wait_ge(y_ps, e + u + 1)
                            link(dve.tensor_tensor(
                                y[:, u, :].rearrange("p (t o) -> p t o", t=TS),
                                K.ps[2 + u % 2][:, 0:W].rearrange("p (t o) -> p t o", t=TS),
                                bias[:, 2 * b * P:(2 * b + 1) * P].unsqueeze(1).broadcast_to([P, TS, P]), ALU.add))
                            dve.sem_inc(y_sb, 1)
                            statistics(u, yt(u))
                        for u in range(U):
                            dve.wait_ge(rstd, s * NL + (b + 1) * U + u + 1)
                            normalise(u, yt(u), yn).then_inc(yn_ready, 1)
                        for u in range(U):
                            dve.wait_ge(hb_ready, e + u + 1)
                            dve.wait_ge(z_ps, e + u + 1)
                            dve.tensor_tensor(hcur[:, u, :], K.ps[6 + u % 2][:, 0:W], hb[:, u, :],
                                              ALU.add).then_inc(h_ready, 1)
                    for u in range(U):
                        dve.wait_ge(h_ready, s * NL + NB * U + u + 1)
                        xs = K.x[:, bass.ds((s * U + u) * W, W)]
                        link(dve.scalar_tensor_tensor(xs, hcur[:, u, :], 0.5, xs, ALU.mult, ALU.add))

            @block.gpsimd
            def _(pool):
                pool.wait_ge(K.loaded["f3"], 16)
                with pool.Fori(0, B // U) as s:
                    pool.sem_clear(pool_s)
                    count = [0]

                    def rsqrt(u, e):
                        pool.wait_ge(stats, e + 1)
                        pool.sem_inc(pool_hold, 1)
                        pool.tensor_scalar(rs[:, u, :], mv[:, u, :, 1], EPS, None, ALU.add).then_inc(pool_s, 1)
                        count[0] += 1
                        pool.wait_ge(pool_s, count[0])
                        pool.tensor_tensor(rs[:, u, :], rs[:, u, :], K.neg_half[:, 0:TS], ALU.pow).then_inc(rstd, 1)

                    for u in range(U):
                        rsqrt(u, s * NL + u)
                    for b in range(NB):
                        for u in range(U):
                            pool.wait_ge(h_ready, s * NL + b * U + u + 1)
                            for j in range(TS):
                                i = pool.tensor_tensor(hb[:, u, j * P:(j + 1) * P], hcur[:, u, j * P:(j + 1) * P],
                                                       bias[:, (2 * b + 1) * P:(2 * b + 2) * P], ALU.add)
                            i.then_inc(hb_ready, 1)
                        for u in range(U):
                            rsqrt(u, s * NL + (b + 1) * U + u)

            @block.scalar
            def _(act):
                act.wait_ge(K.loaded["f3"], 16)
                with act.Fori(0, B // U) as s:
                    for b in range(NB):
                        e = s * (NB * U) + b * U
                        for u in range(U):
                            act.wait_ge(ht_ps, e + u + 1)
                            act.activation(ht[:, u, :], K.ps[0 + u % 2][:, 0:W], ACT.Copy).then_inc(ht_ready, 1)
                        for u in range(U):
                            act.wait_ge(ynt_ps, e + u + 1)
                            act.activation(gt[:, u, :], K.ps[4 + u % 2][:, 0:W], ACT.Gelu, bias=f("bet")[:, b:b + 1],
                                           scale=f("gam")[:, b:b + 1]).then_inc(gt_ready, 1)

            @block.tensor
            def _(pe):
                pe.wait_ge(K.consts_ready, K.N_CONST)
                pe.wait_ge(K.loaded["f3"], 16)
                for i in range(6):
                    k = pe.matmul(K.ps[i // 4][:, (i % 4) * P:(i % 4 + 1) * P], f("la")[0:32, i * P:(i + 1) * P],
                                  f("lb")[0:32, i * P:(i + 1) * P], start=True, stop=True)
                k.then_inc(lora_ps, 1)
                pe.wait_ge(w_ready, 2)
                with pe.Fori(0, B // U) as s:
                    for b in range(NB):
                        e = s * (NB * U) + b * U
                        for u in range(U):
                            pe.wait_ge(h_ready, s * NL + b * U + u + 1)
                            if u >= 2 or b > 0:
                                pe.wait_ge(ht_ready, e + u - 1)
                            for j in range(TS):
                                i = pe.transpose(K.ps[0 + u % 2][:, j * P:(j + 1) * P], hcur[:, u, j * P:(j + 1) * P],
                                                 K.ident[:, :])
                            i.then_inc(ht_ps, 1)
                        for u in range(U):
                            pe.wait_ge(ht_ready, e + u + 1)
                            if u >= 2 or b > 0:
                                pe.wait_ge(y_sb, e + u - 1)
                            for j in range(TS):
                                i = pe.matmul(K.ps[2 + u % 2][:, j * P:(j + 1) * P], ht[:, u, j * P:(j + 1) * P],
                                              w[:, 2 * b * P:(2 * b + 1) * P], start=True, stop=True)
                            i.then_inc(y_ps, 1)
                        for u in range(U):
                            pe.wait_ge(yn_ready, e + u + 1)
                            if u >= 2 or b > 0:
                                pe.wait_ge(gt_ready, e + u - 1)
                            for j in range(TS):
                                i = pe.transpose(K.ps[4 + u % 2][:, j * P:(j + 1) * P], yn[:, u, j * P:(j + 1) * P],
                                                 K.ident[:, :])
                            i.then_inc(ynt_ps, 1)
                        for u in range(U):
                            pe.wait_ge(gt_ready, e + u + 1)
                            if u >= 2 or b > 0:
                                pe.wait_ge(h_ready, s * NL + (b + 1) * U + u - 1)
                            for j in range(TS):
                                i = pe.matmul(K.ps[6 + u % 2][:, j * P:(j + 1) * P], gt[:, u, j * P:(j + 1) * P],
                                              w[:, (2 * b + 1) * P:(2 * b + 2) * P], start=True, stop=True)
                            i.then_inc(z_ps, 1)



def stage_squared_relu_attention(K, tag):
    nc = K.nc
    H, DK, DV = 16, 16, 64
    G = 4
    TINY = 1e-24
    with ExitStack() as scope:
        K.scope = scope
        sb = K.sb
        N = Norm(K, tag)
        xnt = sb(f"{tag}_xnt", [P, W])
        q4 = sb(f"{tag}_q4", [P, G, S])
        k4 = sb(f"{tag}_k4", [P, G, S])
        sq = sb(f"{tag}_qk_squares", [P, 2, 2 * S])
        v = sb(f"{tag}_v", [P, TS, H * DV])
        vsq = sb(f"{tag}_v_squares", [P, 2, 512])
        gt = sb(f"{tag}_gates", [P, TS, H * DV])
        ss = sb(f"{tag}_sums", [P, 3, TS, H])
        ssc = sb(f"{tag}_sums_guarded", [P, 3, TS, H])
        nrm = sb(f"{tag}_norms", [P, 2, TS, H])
        rinv = sb(f"{tag}_norms_inverse", [P, 3, TS, H])
        rel = sb(f"{tag}_relu", [P, 3, TS, S])
        at = sb(f"{tag}_attention", [P, 3, TS, S])
        osq = sb(f"{tag}_out_squares", [P, 2, 512])
        og = sb(f"{tag}_out_gated", [P, TS, H * DV])
        on = sb(f"{tag}_out_norm", [P, TS, H])
        onn = sb(f"{tag}_out_norm_root", [P, TS, H])
        n2 = sb(f"{tag}_n", [P, TS, H])
        nmaxed = sb(f"{tag}_n_guarded", [P, TS, H])
        ninv = sb(f"{tag}_n_inverse", [P, TS, H])
        th = sb(f"{tag}_tanh_n", [P, TS, H])
        fac = sb(f"{tag}_factor", [P, TS, H])
        outt = sb(f"{tag}_outt", [P, 8, S])
        (dve_s, xnt_ready, qk_ps, qk_sq, qk_sb, nrm_ps, v_ps, v_sq, v_sb, g_ps, g_ready, guarded, roots, inv_ready,
         sc_ps, rel_ready, at_ready, o_ps, o_sq, on_ready, oroot, n_ready, th_ready, og_ready, ot_ps, ot_ready,
         y_ps, done, silu_ready, sq_used) = make_sems(
            K, tag, "dve_chain xnt_ready qk_product qk_squares qk_ready norm_product v_product v_squares v_ready "
                    "gate_product gate_ready sums_guarded roots_ready inverse_ready scores_product relu_ready "
                    "attention_ready out_product out_squares out_norm_ready out_root_ready n_ready tanh_ready "
                    "gated_ready outt_product outt_ready y_product seq_done silu_ready squares_used")
        f = lambda n: field(K, "a3", n)
        with nc.Block() as block:
            K.start_loads(block, tag)

            @block.vector
            def _(dve):
                dve.sem_inc(done, 1)
                with dve.Fori(0, B) as s:
                    link = chain(dve, dve_s)
                    norm_vector(K, N, dve, link, lambda j: K.x[:, bass.ds(s * W + j * P, P)], s)
                    dve.wait_ge(N.xt, s + 1)
                    dve.tensor_copy(xnt[:, :], K.ps[0][:, 0:W]).then_inc(xnt_ready, 1)
                    for g in range(G):
                        dve.wait_ge(qk_sq, s * G + g + 1)
                        bank = K.ps[1 + g % 2]
                        dve.tensor_copy(q4[:, g, :], bank[:, 0:S])
                        dve.tensor_copy(k4[:, g, :], bank[:, S:2 * S]).then_inc(qk_sb, 1)
                    for n in range(4):
                        j, c = n // 2, n % 2
                        dve.wait_ge(v_sq, s * 4 + n + 1)
                        dve.tensor_copy(v[:, j, c * 512:(c + 1) * 512], K.ps[4 + n % 2][:, :]).then_inc(v_sb, 1)
                        link(dve.tensor_reduce(ss[:, 2, j, c * 8:(c + 1) * 8],
                                               vsq[:, n % 2, :].rearrange("p (h d) -> p h d", h=8), AX_X, ALU.add))
                    dve.wait_ge(nrm_ps, s + 1)
                    link(dve.tensor_copy(ss[:, 0:2, :, :], K.ps[3][:, 0:64].rearrange("p (a t h) -> p a t h", a=2, t=TS)))
                    dve.tensor_scalar(ssc[:, :, :, :], ss[:, :, :, :], TINY, None, ALU.max).then_inc(guarded, 1)
                    dve.wait_ge(roots, s + 1)
                    dve.reciprocal(rinv[:, 0, :, :], ssc[:, 0, :, :])
                    dve.reciprocal(rinv[:, 1:3, :, :], nrm[:, :, :, :]).then_inc(inv_ready, 1)
                    dve.wait_ge(inv_ready, s + 1)
                    for h in range(H):
                        dve.wait_ge(rel_ready, s * H + h + 1)
                        if h >= 3:
                            dve.wait_ge(o_ps, s * H + h - 2)
                        for j in range(TS):
                            i = dve.scalar_tensor_tensor(at[:, h % 3, j, :], rel[:, h % 3, j, :],
                                                         rinv[:, 2, j, h:h + 1], rel[:, h % 3, j, :], ALU.mult, ALU.mult)
                        i.then_inc(at_ready, 1)
                    for n in range(4):
                        a, j = n // 2, n % 2
                        dve.wait_ge(o_sq, s * 4 + n + 1)
                        dve.tensor_reduce(on[:, j, a * 8:(a + 1) * 8],
                                          osq[:, n % 2, :].rearrange("p (h d) -> p h d", h=8), AX_X,
                                          ALU.add).then_inc(on_ready, 1)
                    dve.wait_ge(oroot, s + 1)
                    dve.tensor_tensor(n2[:, :, :], onn[:, :, :], rinv[:, 0, :, :], ALU.mult).then_inc(n_ready, 1)
                    dve.wait_ge(n_ready, s + 1)
                    link(dve.tensor_scalar(nmaxed[:, :, :], n2[:, :, :], 1e-12, None, ALU.max))
                    link(dve.reciprocal(ninv[:, :, :], nmaxed[:, :, :]))
                    link(dve.tensor_tensor(ninv[:, :, :], ninv[:, :, :], rinv[:, 0, :, :], ALU.mult))
                    dve.wait_ge(th_ready, s + 1)
                    link(dve.tensor_tensor(fac[:, :, :], th[:, :, :], ninv[:, :, :], ALU.mult))
                    for n in range(4):
                        a, j = n // 2, n % 2
                        hh = slice(a * 8, (a + 1) * 8)
                        cols = og[:, j, a * 512:(a + 1) * 512]
                        link(dve.tensor_tensor(cols, K.ps[4 + n][:, :], gt[:, j, a * 512:(a + 1) * 512], ALU.mult))
                        dve.tensor_tensor(cols.rearrange("p (h d) -> p h d", h=8), cols.rearrange("p (h d) -> p h d", h=8),
                                          fac[:, j, hh].unsqueeze(2).broadcast_to([P, 8, DV]), ALU.mult).then_inc(og_ready, 1)
                    dve.wait_ge(y_ps, s + 1)
                    xs = K.x[:, bass.ds(s * W, W)]
                    dve.tensor_tensor(xs, K.ps[0][:, 0:W], xs, ALU.add).then_inc(done, 1)

            @block.gpsimd
            def _(pool):
                with pool.Fori(0, B) as s:
                    norm_pool(K, N, pool, s)

            @block.scalar
            def _(act):
                with act.Fori(0, B) as s:
                    act.wait_ge(done, s + 1)
                    for g in range(G):
                        act.wait_ge(qk_ps, s * G + g + 1)
                        if g >= 2:
                            act.wait_ge(sq_used, s * G + g - 1)
                        act.activation(sq[:, g % 2, :], K.ps[1 + g % 2][:, :], ACT.Square).then_inc(qk_sq, 1)
                    for n in range(4):
                        act.wait_ge(v_ps, s * 4 + n + 1)
                        if n >= 2:
                            act.wait_ge(v_sb, s * 4 + n)
                        act.activation(vsq[:, n % 2, :], K.ps[4 + n % 2][:, :], ACT.Square).then_inc(v_sq, 1)
                    for n in range(4):
                        act.wait_ge(g_ps, s * 4 + n + 1)
                        act.activation(gt[:, n // 2, (n % 2) * 512:(n % 2 + 1) * 512], K.ps[(0, 6)[n % 2]][:, :],
                                       ACT.Silu).then_inc(silu_ready, 1)
                    act.wait_ge(silu_ready, s * 4 + 4)
                    act.activation(gt[:, :, :], gt[:, :, :], ACT.Tanh).then_inc(g_ready, 1)
                    act.wait_ge(guarded, s + 1)
                    act.activation(nrm[:, :, :, :], ssc[:, 1:3, :, :], ACT.Sqrt).then_inc(roots, 1)
                    act.wait_ge(inv_ready, s + 1)
                    for h in range(H):
                        act.wait_ge(sc_ps, s * H + h + 1)
                        if h >= 3:
                            act.wait_ge(at_ready, s * H + h - 2)
                        for j in range(TS):
                            i = act.activation(rel[:, h % 3, j, :], K.ps[2 + h % 2][:, j * S:(j + 1) * S], ACT.Relu,
                                               scale=rinv[:, 1, j, h:h + 1])
                        i.then_inc(rel_ready, 1)
                    for n in range(4):
                        act.wait_ge(o_ps, s * H + 8 * (n // 2) + 8)
                        if n >= 2:
                            act.wait_ge(on_ready, s * 4 + n - 1)
                        act.activation(osq[:, n % 2, :], K.ps[4 + n][:, :], ACT.Square).then_inc(o_sq, 1)
                    act.wait_ge(on_ready, s * 4 + 4)
                    act.activation(onn[:, :, :], on[:, :, :], ACT.Sqrt).then_inc(oroot, 1)
                    act.wait_ge(n_ready, s + 1)
                    act.activation(th[:, :, :], n2[:, :, :], ACT.Tanh).then_inc(th_ready, 1)
                    for n in range(4):
                        act.wait_ge(ot_ps, s * 4 + n + 1)
                        act.activation(outt[:, 2 * n:2 * n + 2, :].rearrange("p c t -> p (c t)"), K.ps[2 + n % 2][:, :],
                                       ACT.Copy).then_inc(ot_ready, 1)

            @block.tensor
            def _(pe):
                pe.wait_ge(K.consts_ready, K.N_CONST)
                pe.wait_ge(K.loaded["a3"], 16)
                with pe.Fori(0, B) as s:
                    norm_tensor(K, N, pe, s, K.ps[0])
                    pe.wait_ge(xnt_ready, s + 1)
                    pe.wait_ge(done, s + 1)

                    def norms(g):
                        pe.wait_ge(qk_sq, s * G + g + 1)
                        for a in range(2):
                            for j in range(TS):
                                i = pe.matmul(K.ps[3][:, (a * TS + j) * H + 4 * g:(a * TS + j) * H + 4 * g + 4],
                                              sq[:, g % 2, a * S + j * P:a * S + (j + 1) * P], K.quad[:, :],
                                              start=True, stop=True)
                        i.then_inc(sq_used, 1)
                        if g == G - 1:
                            pe.wait_ge(sq_used, s * G + G)
                            pe.sem_inc(nrm_ps, 1)

                    for g in range(G):
                        if g >= 2:
                            pe.wait_ge(qk_sb, s * G + g - 1)
                        bank = K.ps[1 + g % 2]
                        pe.matmul(bank[:, 0:S], f("wq4")[:, g * P:(g + 1) * P], xnt[:, :], start=True, stop=True)
                        pe.matmul(bank[:, S:2 * S], f("wk4")[:, g * P:(g + 1) * P], xnt[:, :],
                                  start=True, stop=True).then_inc(qk_ps, 1)
                        if g >= 1:
                            norms(g - 1)
                    norms(G - 1)
                    for n in range(4):
                        j, c = n // 2, n % 2
                        if n >= 2:
                            pe.wait_ge(v_sb, s * 4 + n - 1)
                        pe.matmul(K.ps[4 + n % 2][:, :], xnt[:, j * P:(j + 1) * P], f("wv")[:, c * 512:(c + 1) * 512],
                                  start=True, stop=True).then_inc(v_ps, 1)
                    for n in range(4):
                        j, c = n // 2, n % 2
                        if n >= 2:
                            pe.wait_ge(silu_ready, s * 4 + n - 1)
                        pe.matmul(K.ps[(0, 6)[n % 2]][:, :], xnt[:, j * P:(j + 1) * P],
                                  f("wg")[:, c * 512:(c + 1) * 512], start=True, stop=True).then_inc(g_ps, 1)
                    pe.wait_ge(guarded, s + 1)
                    pe.wait_ge(silu_ready, s * 4 + 4)
                    for i in range(H + 2):
                        if i < H:
                            g, r = i // 4, 32 * (i % 4)
                            if i >= 2:
                                pe.wait_ge(rel_ready, s * H + i - 1)
                            for j in range(TS):
                                k = pe.matmul(K.ps[2 + i % 2][:, j * S:(j + 1) * S], k4[r:r + 32, g, j * P:(j + 1) * P],
                                              q4[r:r + 32, g, :], start=True, stop=True)
                            k.then_inc(sc_ps, 1)
                        if i >= 2:
                            h = i - 2
                            pe.wait_ge(at_ready, s * H + h + 1)
                            for t in range(TS):
                                for j in range(TS):
                                    k = pe.matmul(K.ps[4 + 2 * (h // 8) + t][:, (h % 8) * DV:(h % 8 + 1) * DV],
                                                  at[:, h % 3, j, t * P:(t + 1) * P], v[:, j, h * DV:(h + 1) * DV],
                                                  start=(j == 0), stop=(j == TS - 1))
                            k.then_inc(o_ps, 1)
                    for n in range(4):
                        if n >= 2:
                            pe.wait_ge(ot_ready, s * 4 + n - 1)
                        pe.wait_ge(og_ready, s * 4 + (2 if n < 2 else 4))
                        for c in range(2):
                            for t in range(TS):
                                i = pe.transpose(K.ps[2 + n % 2][:, c * S + t * P:c * S + (t + 1) * P],
                                                 og[:, t, (2 * n + c) * P:(2 * n + c + 1) * P], K.ident[:, :])
                        i.then_inc(ot_ps, 1)
                    for t in range(TS):
                        for c in range(8):
                            if t == 0 and c % 2 == 0:
                                pe.wait_ge(ot_ready, s * 4 + c // 2 + 1)
                            i = pe.matmul(K.ps[0][:, t * P:(t + 1) * P], outt[:, c, t * P:(t + 1) * P],
                                          f("wo")[:, c * P:(c + 1) * P], start=(c == 0), stop=(c == 7))
                    i.then_inc(y_ps, 1)



STAGES = {
    "f0a": (stage_signed_ffn,), "at0": (stage_softmax_attention,), "f0b": (stage_signed_ffn,),
    "m1a": (stage_gated_experts,), "mam": (stage_state_space,), "m1b": (stage_gated_experts,),
    "m2a": (stage_gelu_experts,), "at2": (stage_window_linear_attention,), "m2b": (stage_gelu_experts,),
    "f3a": (stage_quantised_ffn,), "at3": (stage_squared_relu_attention,), "f3b": (stage_quantised_ffn,),
}
REGION = {"a0": "r0", "mb": "r0", "a2": "r0", "a3": "r0", "m1": "r1", "m2": "r2", "f3": "r3"}
LOAD_AT = {"mb": "m1a", "a2": "m1b", "a3": "f3a"}


def build(nc, aps, out, stages=tuple(STAGES)):
    K = Core()
    K.nc = nc
    needs = {"f0a": "a0", "at0": "a0", "f0b": "a0", "m1a": "m1", "mam": "mb", "m1b": "m1", "m2a": "m2",
             "at2": "a2", "m2b": "m2", "f3a": "f3", "at3": "a3", "f3b": "f3"}
    used = [p for p in PACKS if p in {needs[s] for s in stages}]
    with ExitStack() as ctx:
        K.sem_scope = ctx.enter_context(ExitStack())
        K.live_sems = []
        K.scope = ctx
        K.sb = lambda name, shape, dt=F32: K.scope.enter_context(nc.sbuf_tensor(name, shape, dt))
        K.ps = [ctx.enter_context(nc.psum_tensor(f"bank{i}", [P, 512], F32)) for i in range(8)]
        K.x = K.sb("x", [P, B * W])
        K.ident = K.sb("identity", [P, P])
        K.neg_half = K.sb("neg_half", [P, 8])
        K.neg_one = K.sb("neg_one", [P, 1])
        K.ones = K.sb("ones", [P, P])
        K.quad = K.sb("quadrant_ones", [P, 4])
        K.iota16 = K.sb("iota16", [P, E])
        K.sel64 = K.sb("select_64", [PARTS, E * 64], BF16)
        K.sel = K.sb("select", [96, 32 * P], BF16)
        K.qw = K.sb("qweights", [P, 6 * P], I32)
        region = {}
        for p in used:
            r = REGION[p]
            region[r] = max(region.get(r, 0), pack_width(p))
        region = {r: K.sb(f"weights_{r}", [P, n]) for r, n in region.items()}
        K.pack = {p: region[REGION[p]] for p in used}
        K.loaded = {p: ctx.enter_context(nc.semaphore(f"loaded_{p}")) for p in used}
        K.loaded_x, K.loaded_q, K.consts_ready, K.const_chain, K.stored = (
            ctx.enter_context(nc.semaphore(n)) for n in
            ("loaded_x", "loaded_q", "consts_ready", "const_chain", "stored"))
        K.N_CONST = 1

        def start_loads(block, tag):
            due = [p for p in used if LOAD_AT.get(p) == tag]
            if due:
                @block.sync
                def _(sp):
                    for p in due:
                        sp.dma_start(K.pack[p][:, 0:pack_width(p)], aps[p]).then_inc(K.loaded[p], 16)
        K.start_loads = start_loads

        with nc.Block() as block:
            @block.sync
            def _(sp):
                sp.dma_start(K.x[:, :], aps["x"]).then_inc(K.loaded_x, 16)
                for p in used:
                    if LOAD_AT.get(p) not in stages:
                        sp.dma_start(K.pack[p][:, 0:pack_width(p)], aps[p]).then_inc(K.loaded[p], 16)
                sp.dma_start(K.qw[:, :], aps["q"]).then_inc(K.loaded_q, 16)
                sp.wait_ge(K.loaded_x, 16)

            @block.gpsimd
            def _(pool):
                n = 0

                def link(ins):
                    nonlocal n
                    n += 1
                    ins.then_inc(K.const_chain, 1)
                    pool.wait_ge(K.const_chain, n)
                pool.memset(K.neg_half[:, :], -0.5)
                pool.memset(K.ones[:, :], 1.0)
                pool.memset(K.neg_one[:, :], -1.0)
                pool.iota(K.iota16[:, :], [[1, E]], base=0, channel_multiplier=0,
                          allow_small_or_imprecise_dtypes=True)
                pool.memset(K.sel64[:, :], 0.0)
                pool.memset(K.sel[:, :], 0.0)
                link(pool.memset(K.ident[:, :], 0.0))
                link(pool.affine_select(out=K.ident[:, :], in_=K.ident[:, :], compare_op=ALU.not_equal, fill=1.0,
                                        base=0, pattern=[[-1, P]], channel_multiplier=1))
                link(pool.memset(K.quad[:, :], 1.0))
                link(pool.affine_select(out=K.quad[:, :], in_=K.quad[:, :], compare_op=ALU.is_ge, fill=0.0, base=0,
                                        pattern=[[-32, 4]], channel_multiplier=1))
                link(pool.affine_select(out=K.quad[:, :], in_=K.quad[:, :], compare_op=ALU.is_ge, fill=0.0, base=31,
                                        pattern=[[32, 4]], channel_multiplier=-1))
                for sel, rows, wide in ((K.sel64, E, 64), (K.sel, 32, P)):
                    for base in (HI, MID, LO):
                        v = sel[:, :].rearrange("p (e c) -> p e c", e=rows)
                        link(pool.affine_select(out=v, in_=v, compare_op=ALU.not_equal, fill=1.0, base=-base,
                                                pattern=[[-1, rows], [0, wide]], channel_multiplier=1))
                pool.sem_inc(K.consts_ready, 1)
        for tag in stages:
            STAGES[tag][0](K, tag)
            clear_sems(K)
        with nc.Block() as block:
            @block.sync
            def _(sp):
                sp.dma_start(out, K.x[:, :]).then_inc(K.stored, 16)
                sp.wait_ge(K.stored, 16)


def host_arrays(i):
    rows = lambda v: np.broadcast_to(np.asarray(v).reshape(1, -1), (P, np.asarray(v).size))
    cols = lambda v, n: np.asarray(v).reshape(n, P).T
    kpm = lambda w: w.reshape(-1, P, w.shape[-1]).transpose(1, 0, 2).reshape(P, -1)

    def pad(a):
        out = np.zeros((P, a.shape[1]), a.dtype)
        out[:a.shape[0]] = a
        return out

    def by_four(w, d):
        out = np.zeros((w.shape[0], 16, 32), w.dtype)
        out[:, :, :d] = w.reshape(w.shape[0], 16, d)
        return out.reshape(w.shape[0], 512)

    g = {}
    Ww, Wb = i["L0_attn_W_w"], i["L0_attn_W_b"]
    g["a0"] = dict(ffn=i["L0_ffn_weight"].T, wq=Ww[:1024].T, wk=Ww[1024:2048].T, wv=Ww[2048:].T,
                   wo=kpm(i["L0_attn_out_w"].T), bq=cols(Wb[:1024], 8), bk=cols(Wb[1024:2048], 8),
                   bv=rows(Wb[2048:]), bo=rows(i["L0_attn_out_b"]))
    g["m1"] = dict(rw=i["L1_ffn_router_w"].T, rb=np.tile(rows(i["L1_ffn_router_bias"]), (1, 2)),
                   up=i["L1_ffn_up_proj"].transpose(1, 0, 2).reshape(P, -1),
                   gate=i["L1_ffn_gate_proj"].transpose(1, 0, 2).reshape(P, -1),
                   down=kpm(i["L1_ffn_down_proj"].reshape(1024, P)), shg=i["L1_ffn_sh_gate"].T,
                   shu=i["L1_ffn_sh_up"].T, shd=i["L1_ffn_sh_down"].T)
    mb = {}
    for l in range(4):
        a = {k[8:]: v[l] for k, v in i.items() if k.startswith("L1_attn_") and "fnorm" not in k}
        bc = a["x_proj_w"][8:40].T
        xp = np.concatenate([bc, bc, bc, a["x_proj_w"][:8].T], axis=1)
        dtw = np.zeros((P, 256), np.float32)
        dtw[96:104] = a["dt_proj_w"].T
        mb.update({f"{k}{l}": v for k, v in dict(
            taps=rows(a["conv_w"][:, 0, :].T), inx=a["in_proj_w"][:256].T, inz=a["in_proj_w"][256:].T,
            cb=cols(a["conv_b"], 2), xp=kpm(xp), dtw=dtw, dtb=cols(a["dt_proj_b"], 2),
            alog=kpm(a["A_log"]), dsk=cols(a["D_skip"], 2), outw=kpm(a["out_proj_w"].T),
            lnw=a["ln_w"][:, None], lnb=a["ln_b"][:, None]).items()})
    g["mb"] = mb
    g["m2"] = dict(rw=i["L2_ffn_router_w"], rb=np.tile(rows(i["L2_ffn_router_b"]), (1, 2)),
                   w1=i["L2_ffn_w1"].transpose(1, 0, 2).reshape(P, -1), b1=cols(i["L2_ffn_b1"], 32),
                   w2=kpm(i["L2_ffn_w2"].reshape(-1, P)), b2=pad(i["L2_ffn_b2"]))
    a = {k[8:]: v for k, v in i.items() if k.startswith("L2_attn_")}
    at = np.clip(np.arange(192)[None, :] + 32 - np.arange(P)[:, None], 0, 128)
    g["a2"] = dict(wql=a["wq_lin"], wkl=a["wk_lin"], wvl=a["wv_lin"], bql=a["bq_lin"][:, None],
                   bkl=rows(a["bk_lin"]), bvl=rows(a["bv_lin"]), wq4=by_four(a["wq_loc"], 8),
                   wk4=by_four(a["wk_loc"], 8), bq4=cols(by_four(rows(a["bq_loc"])[:1], 8), 4),
                   bk4=cols(by_four(rows(a["bk_loc"])[:1], 8), 4), wvc=a["wv_loc"], bvc=rows(a["bv_loc"]),
                   wo=a["wo"], bo=rows(a["bo"]), wg1=kpm(a["wg1"]), bg1=a["bg1"][:, None], wg2=a["wg2"],
                   bg2=a["bg2"][:, None], lng=a["ln_g"][:, None], lnb=a["ln_b"][:, None],
                   band=a["rel_bias"][at].transpose(0, 2, 1).reshape(P, -1))
    g["f3"] = dict(scale=np.repeat(i["L3_ffn_scales"].transpose(2, 0, 1), 16, axis=0).reshape(P, -1),
                   bias=rows(i["L3_ffn_biases"]), la=pad(i["L3_ffn_lora_a"].transpose(1, 0, 2).reshape(32, -1)),
                   lb=pad(i["L3_ffn_lora_b"].transpose(2, 0, 1).reshape(32, -1)),
                   gam=i["L3_ffn_ln_gamma"].T, bet=i["L3_ffn_ln_beta"].T)
    qg, kv = (i[n].reshape(P, 16, 80) for n in ("L3_attn_Wqg", "L3_attn_Wkv"))
    g["a3"] = dict(wq4=by_four(qg[:, :, :16].reshape(P, -1), 16), wk4=by_four(kv[:, :, :16].reshape(P, -1), 16),
                   wg=qg[:, :, 16:].reshape(P, -1), wv=kv[:, :, 16:].reshape(P, -1), wo=kpm(i["L3_attn_Wout"]))
    arrays = {}
    for p, fields in PACKS.items():
        for n, c in fields.items():
            assert g[p][n].shape == (P, c), (p, n, g[p][n].shape, c)
        arrays[p] = np.ascontiguousarray(np.concatenate([g[p][n] for n in fields], axis=1))
    arrays["q"] = np.ascontiguousarray(i["L3_ffn_qweights"].transpose(2, 0, 1).reshape(P, -1))
    arrays["x"] = np.ascontiguousarray(i["L0_attn_x"].reshape(B * TS, P, P).transpose(1, 0, 2).reshape(P, -1))
    return arrays


def kernel(**inputs):
    from concourse import bacc
    from concourse.bass_utils import run_bass_kernel_spmd

    arrays = host_arrays({k: np.asarray(v) for k, v in inputs.items()})
    nc = bacc.Bacc("TRN2", target_bir_lowering=False, num_devices=1)
    aps = {n: nc.dram_tensor(f"in_{n}", a.shape, mybir.dt.from_np(a.dtype), kind="ExternalInput").ap()
           for n, a in arrays.items()}
    out = nc.dram_tensor("out_x", (P, B * W), F32, kind="ExternalOutput").ap()
    build(nc, aps, out)
    r = run_bass_kernel_spmd(nc, [{f"in_{n}": a for n, a in arrays.items()}], core_ids=[0])
    y = r.results[0]["out_x"]
    return np.ascontiguousarray(y.reshape(P, B * TS, P).transpose(1, 0, 2)).reshape(B, S, P)
```

```python
from contextlib import ExitStack

import numpy as np

import concourse.bass as bass
from concourse import mybir

F32 = mybir.dt.float32
BF16 = mybir.dt.bfloat16
I32 = mybir.dt.int32
U32 = mybir.dt.uint32
ALU = mybir.AluOpType
ACT = mybir.ActivationFunctionType
AX_X = mybir.AxisListType.X

P = 128
B, S = 8, 256
TS = S // P
W = TS * P
EPS = 1e-5

PACKS = {
    "a0": dict(ffn=128, wq=1024, wk=1024, wv=1024, wo=1024, bq=8, bk=8, bv=1024, bo=128),
    "m1": dict(rw=16, rb=32, up=1024, gate=1024, down=1024, shg=128, shu=128, shd=128),
    "mb": {f"{n}{l}": c for l in range(4) for n, c in dict(
        taps=1024, inx=256, inz=256, cb=2, xp=208, dtw=256, dtb=2, alog=32, dsk=2,
        outw=256, lnw=1, lnb=1).items()},
    "m2": dict(rw=16, rb=32, w1=4096, b1=32, w2=4096, b2=128),
    "a2": dict(wql=128, wkl=128, wvl=128, bql=1, bkl=128, bvl=128, wq4=512, wk4=512, bq4=4, bk4=4,
               wvc=128, bvc=128, wo=128, bo=128, wg1=384, bg1=1, wg2=128, bg2=1, lng=1, lnb=1,
               band=16 * 192),
    "f3": dict(scale=768, bias=768, la=768, lb=768, gam=3, bet=3),
    "a3": dict(wq4=512, wk4=512, wg=1024, wv=1024, wo=1024),
}


def pack_width(name):
    return sum(PACKS[name].values())


def pack_offset(name, field):
    at = 0
    for f, n in PACKS[name].items():
        if f == field:
            return at, n
        at += n
    raise KeyError(field)


class Core:
    pass


def make_sems(K, stage, names):
    sems = [K.sem_scope.enter_context(K.nc.semaphore(f"{stage}_{n}")) for n in names.split()]
    K.live_sems += sems
    return sems


def clear_sems(K):
    with K.nc.Block() as block:
        @block.sync
        def _(sp):
            for sem in K.live_sems:
                sp.sem_clear(sem)
    K.live_sems = []
    K.sem_scope.close()


def field(K, pack, name):
    at, n = pack_offset(pack, name)
    return K.pack[pack][:, at:at + n]


def chain(eng, sem):
    count = [0]
    eng.sem_clear(sem)

    def link(ins):
        count[0] += 1
        ins.then_inc(sem, 1)
        eng.wait_ge(sem, count[0])
    return link



class Norm:
    def __init__(self, K, stage):
        self.stats, self.rstd, self.xn, self.xt, self.pool, self.own = make_sems(
            K, stage, "ln_stats ln_rstd ln_xn ln_transposed ln_pool_chain ln_dve_chain")
        sb = K.sb
        self.bn = sb(f"{stage}_ln_bn", [P, TS, 6])
        self.mv = sb(f"{stage}_ln_mv", [P, TS, 2])
        self.rs = sb(f"{stage}_ln_rs", [P, TS])
        self.out = sb(f"{stage}_ln_xn", [P, W])


def norm_vector(K, N, dve, link, src, n, before=None):
    for j in range(TS):
        i = dve.bn_stats(N.bn[:, j, :], src(j))
    link(i)
    for j in range(TS):
        i = dve.bn_aggr(N.mv[:, j, :], N.bn[:, j, :])
    i.then_inc(N.stats, 1)
    dve.wait_ge(N.rstd, n + 1)
    for j in range(TS):
        i = dve.tensor_scalar(N.out[:, j * P:(j + 1) * P], src(j), N.mv[:, j, 0:1], N.rs[:, j:j + 1],
                              ALU.subtract, ALU.mult)
    i.then_inc(N.xn, 1)


def norm_stats(N, dve, src):
    for j in range(TS):
        i = dve.bn_stats(N.bn[:, j, :], src(j)).then_inc(N.own, 1)
    dve.wait_ge(N.own, TS)
    dve.sem_clear(N.own)
    for j in range(TS):
        i = dve.bn_aggr(N.mv[:, j, :], N.bn[:, j, :])
    i.then_inc(N.stats, 1)


def norm_apply(N, dve, src, n):
    dve.wait_ge(N.rstd, n + 1)
    for j in range(TS):
        i = dve.tensor_scalar(N.out[:, j * P:(j + 1) * P], src(j), N.mv[:, j, 0:1], N.rs[:, j:j + 1],
                              ALU.subtract, ALU.mult)
    i.then_inc(N.xn, 1)


def norm_pool(K, N, pool, n):
    pool.wait_ge(N.stats, n + 1)
    pool.sem_inc(N.pool, 1)
    pool.tensor_scalar(N.rs[:, :], N.mv[:, :, 1], EPS, None, ALU.add).then_inc(N.pool, 1)
    pool.wait_ge(N.pool, 2 * (n + 1))
    pool.tensor_tensor(N.rs[:, :], N.rs[:, :], K.neg_half[:, 0:TS], ALU.pow).then_inc(N.rstd, 1)


def norm_tensor(K, N, pe, n, dst):
    pe.wait_ge(N.xn, n + 1)
    for j in range(TS):
        i = pe.transpose(dst[:, j * P:(j + 1) * P], N.out[:, j * P:(j + 1) * P], K.ident[:, :])
    i.then_inc(N.xt, 1)



def stage_signed_ffn(K, tag):
    nc = K.nc
    with ExitStack() as scope:
        K.scope = scope
        N = Norm(K, tag)
        xnt = K.sb(f"{tag}_xnt", [P, W])
        sgn = K.sb(f"{tag}_sign", [P, P])
        neg = K.sb(f"{tag}_negative", [P, P])
        link_s, xnt_ready, prod, done = make_sems(K, tag, "dve_chain xnt_ready product_ready seq_done")
        with nc.Block() as block:
            K.start_loads(block, tag)

            @block.vector
            def _(dve):
                dve.sem_inc(done, 1)
                link = chain(dve, link_s)
                dve.wait_ge(K.loaded["a0"], 16)
                w = field(K, "a0", "ffn")
                link(dve.tensor_scalar(neg[:, :], w, 0.0, None, ALU.is_lt))
                link(dve.scalar_tensor_tensor(sgn[:, :], w, 0.0, neg[:, :], ALU.is_gt, ALU.subtract))
                with dve.Fori(0, B) as s:
                    link = chain(dve, link_s)
                    norm_vector(K, N, dve, link, lambda j: K.x[:, bass.ds(s * W + j * P, P)], s)
                    dve.wait_ge(N.xt, s + 1)
                    dve.tensor_copy(xnt[:, :], K.ps[0][:, 0:W]).then_inc(xnt_ready, 1)
                    dve.wait_ge(prod, s + 1)
                    xs = K.x[:, bass.ds(s * W, W)]
                    dve.scalar_tensor_tensor(xs, K.ps[1][:, 0:W], 0.5, xs, ALU.mult, ALU.add).then_inc(done, 1)

            @block.gpsimd
            def _(pool):
                with pool.Fori(0, B) as s:
                    norm_pool(K, N, pool, s)

            @block.tensor
            def _(pe):
                pe.wait_ge(K.consts_ready, K.N_CONST)
                with pe.Fori(0, B) as s:
                    norm_tensor(K, N, pe, s, K.ps[0])
                    pe.wait_ge(xnt_ready, s + 1)
                    pe.wait_ge(done, s + 1)
                    for j in range(TS):
                        i = pe.matmul(K.ps[1][:, j * P:(j + 1) * P], xnt[:, j * P:(j + 1) * P], sgn[:, :],
                                      start=True, stop=True)
                    i.then_inc(prod, 1)



def over_sequences(eng, slot, slots, tail):
    def main(now, last, nxt):
        for i in range(slots):
            slot(i, now, last, nxt)
    main((0, 0), None, (1, 1))
    with eng.Fori(0, (B - 2) // 2) as pair:
        for d in (1, 2):
            main((pair * 2 + d, d % 2), (pair * 2 + (d - 1), 1 - d % 2), (pair * 2 + (d + 1), 1 - d % 2))
    main((B - 1, 1), (B - 2, 0), None)
    for i in range(tail):
        slot(i, None, (B - 1, 1), None)


def lagged(i, lag, slots, now, last):
    at, step = (now, i - lag) if i >= lag else (last, i - lag + slots)
    return (*at, step) if at else None



def stage_softmax_attention(K, tag):
    nc = K.nc
    H, DH = 16, 64
    G = H // 2
    with ExitStack() as scope:
        K.scope = scope
        sb = K.sb
        N = Norm(K, tag)
        xnt = sb(f"{tag}_xnt", [P, W])
        v = sb(f"{tag}_v", [P, 2, TS, H * DH])
        qt = sb(f"{tag}_qt", [P, 2, S])
        kt = sb(f"{tag}_kt", [P, 2, S])
        nmax = sb(f"{tag}_nmax", [P, H, TS])
        rsum = sb(f"{tag}_rsum", [P, H, TS])
        rinv = sb(f"{tag}_rinv", [P, H, TS])
        probs = sb(f"{tag}_probs", [P, 4, TS, S])
        probst = sb(f"{tag}_probst", [P, 2, TS * S])
        on = sb(f"{tag}_out_normalised", [P, 2, TS, P])
        outt = sb(f"{tag}_outt", [P, 2, G, S])
        (link_s, xnt_ready, v_ps, v_ready, qk_ps, qk_ready, sc_ready, max_ready, exp_ready,
         pt_ps, pt_ready, av_ps, on_ready, ot_ps, ot_ready, y_ps, done) = make_sems(
            K, tag, "dve_chain xnt_ready v_product v_ready qk_product qk_ready scores_ready max_ready "
                    "exp_ready probst_transposed probst_ready av_product out_normalised out_transposed "
                    "out_ready y_product seq_done")
        wq, wk, wv, wo = (field(K, "a0", n) for n in ("wq", "wk", "wv", "wo"))
        bq, bk, bv, bo = (field(K, "a0", n) for n in ("bq", "bk", "bv", "bo"))
        STATS, APPLY, XT, V0, Y0, ADD = 7, 9, 12, 13, 6, 7
        TAIL = ADD + 1
        v_at = lambda i: [n for n in range(4) if min(V0 + n, H - 1) == i]
        with nc.Block() as block:
            K.start_loads(block, tag)

            @block.vector
            def _(dve):
                for sem in (qk_ready, on_ready, ot_ready, done):
                    dve.sem_inc(sem, 1)
                dve.wait_ge(K.loaded["a0"], 16)

                def queries_keys(s, p):
                    dve.wait_ge(qk_ps, s * G + p + 1)
                    dve.tensor_scalar(qt[:, p % 2, :], K.ps[0][:, 0:S], bq[:, p:p + 1], DH ** -0.5,
                                      ALU.add, ALU.mult)
                    dve.tensor_scalar(kt[:, p % 2, :], K.ps[0][:, S:2 * S], bk[:, p:p + 1], None,
                                      ALU.add).then_inc(qk_ready, 1)

                def prepare(i, s, q):
                    xs = lambda j: K.x[:, bass.ds(s * W + j * P, P)]
                    if i == STATS:
                        link = chain(dve, link_s)
                        for j in range(TS):
                            k = dve.bn_stats(N.bn[:, j, :], xs(j))
                        link(k)
                        for j in range(TS):
                            k = dve.bn_aggr(N.mv[:, j, :], N.bn[:, j, :])
                        k.then_inc(N.stats, 1)
                    if i == APPLY:
                        dve.wait_ge(N.rstd, s + 1)
                        for j in range(TS):
                            k = dve.tensor_scalar(N.out[:, j * P:(j + 1) * P], xs(j), N.mv[:, j, 0:1],
                                                  N.rs[:, j:j + 1], ALU.subtract, ALU.mult)
                        k.then_inc(N.xn, 1)
                    if i == XT:
                        dve.wait_ge(N.xt, s + 1)
                        dve.tensor_copy(xnt[:, :], K.ps[7][:, 0:W]).then_inc(xnt_ready, 1)
                    for n in v_at(i):
                        j, c = n // 2, n % 2
                        dve.wait_ge(v_ps, s * 4 + n + 1)
                        dve.tensor_tensor(v[:, q, j, c * 512:(c + 1) * 512], K.ps[7][:, :],
                                          bv[:, c * 512:(c + 1) * 512], ALU.add).then_inc(v_ready, 1)

                def slot(i, now, last, nxt):
                    if now:
                        s, q = now
                        dve.wait_ge(sc_ready, s * H + i + 1)
                        dve.tensor_reduce(nmax[:, i, :], K.ps[2 + i % 2][:, :].rearrange("p (t k) -> p t k", t=TS),
                                          AX_X, ALU.max, negate=True).then_inc(max_ready, 1)
                        if i % 2 == 0 and i // 2 + 1 < G:
                            queries_keys(s, i // 2 + 1)
                    if nxt and i == H - 2:
                        queries_keys(nxt[0], 0)
                    at = lagged(i, 3, H, now, last)
                    if at and at[2] % 2 == 1:
                        s, q, h = at
                        p = h // 2
                        link = chain(dve, link_s)
                        dve.wait_ge(av_ps, s * H + h + 3)
                        link(dve.reciprocal(rinv[:, h - 1:h + 1, :], rsum[:, h - 1:h + 1, :]))
                        dve.wait_ge(ot_ps, s * G + p + 1)
                        for t in range(TS):
                            k = dve.tensor_tensor(on[:, p % 2, t, :].rearrange("p (h d) -> p h d", h=2),
                                                  K.ps[6][:, t * P:(t + 1) * P].rearrange("p (h d) -> p h d", h=2),
                                                  rinv[:, h - 1:h + 1, t].unsqueeze(2).broadcast_to([P, 2, DH]),
                                                  ALU.mult)
                        k.then_inc(on_ready, 1)
                    at = lagged(i, 6, H, now, last)
                    if at and at[2] % 2 == 1:
                        s, q, h = at
                        dve.wait_ge(ot_ps, s * G + h // 2 + 3)
                        dve.tensor_copy(outt[:, q, h // 2, :], K.ps[1][:, 0:S]).then_inc(ot_ready, 1)
                    if last and i == ADD:
                        s, q = last
                        link = chain(dve, link_s)
                        for j in range(TS):
                            xj = K.x[:, bass.ds(s * W + j * P, P)]
                            k = dve.tensor_tensor(xj, xj, bo, ALU.add)
                        link(k)
                        dve.wait_ge(y_ps, s + 1)
                        xs = K.x[:, bass.ds(s * W, W)]
                        dve.tensor_tensor(xs, K.ps[7][:, 0:W], xs, ALU.add).then_inc(done, 1)
                    if nxt:
                        prepare(i, *nxt)

                for i in range(H):
                    prepare(i, 0, 0)
                queries_keys(0, 0)
                over_sequences(dve, slot, H, TAIL)

            @block.gpsimd
            def _(pool):
                with pool.Fori(0, B) as s:
                    norm_pool(K, N, pool, s)

            @block.scalar
            def _(act):
                act.sem_inc(exp_ready, 2)
                act.sem_inc(pt_ready, 2)

                def slot(i, now, last, nxt):
                    if now:
                        g = now[0] * H + i
                        act.wait_ge(max_ready, g + 1)
                        act.wait_ge(pt_ps, g + 1)
                        for t in range(TS):
                            k = act.activation(probs[:, i % 4, t, :], K.ps[2 + i % 2][:, t * S:(t + 1) * S],
                                               ACT.Exp, bias=nmax[:, i, t:t + 1],
                                               accum_out=rsum[:, i, t:t + 1])
                        k.then_inc(exp_ready, 1)
                    at = lagged(i, 2, H, now, last)
                    if at:
                        s, q, h = at
                        act.wait_ge(pt_ps, s * H + h + 5)
                        act.wait_ge(av_ps, s * H + h + 1)
                        act.activation(probst[:, h % 2, :], K.ps[4 + h % 2][:, :], ACT.Copy).then_inc(pt_ready, 1)
                over_sequences(act, slot, H, 2)

            @block.tensor
            def _(pe):
                pe.sem_inc(pt_ps, 4)
                pe.sem_inc(av_ps, 2)
                pe.sem_inc(ot_ps, 2)
                pe.wait_ge(K.consts_ready, K.N_CONST)
                pe.wait_ge(K.loaded["a0"], 16)

                def project(s, p):
                    pe.wait_ge(qk_ready, s * G + p + 1)
                    pe.matmul(K.ps[0][:, 0:S], wq[:, p * P:(p + 1) * P], xnt[:, :], start=True, stop=True)
                    pe.matmul(K.ps[0][:, S:2 * S], wk[:, p * P:(p + 1) * P], xnt[:, :],
                              start=True, stop=True).then_inc(qk_ps, 1)

                def prepare(i, s, q, free):
                    if i == XT:
                        pe.wait_ge(done, free)
                        norm_tensor(K, N, pe, s, K.ps[7])
                    for n in v_at(i):
                        j, c = n // 2, n % 2
                        if n == 0:
                            pe.wait_ge(xnt_ready, s + 1)
                        else:
                            pe.wait_ge(v_ready, s * 4 + n)
                        pe.matmul(K.ps[7][:, :], xnt[:, j * P:(j + 1) * P],
                                  wv[:, c * 512:(c + 1) * 512], start=True, stop=True).then_inc(v_ps, 1)

                def slot(i, now, last, nxt):
                    if now:
                        s, q = now
                        g, p, r = s * H + i, i // 2, 64 * (i % 2)
                        if r == 0:
                            pe.wait_ge(qk_ready, s * G + p + 2)
                        pe.wait_ge(exp_ready, g + 1)
                        for t in range(TS):
                            k = pe.matmul(K.ps[2 + i % 2][:, t * S:(t + 1) * S],
                                          qt[r:r + 64, p % 2, t * P:(t + 1) * P], kt[r:r + 64, p % 2, :],
                                          start=True, stop=True)
                        k.then_inc(sc_ready, 1)
                        if i % 2 == 0 and p + 1 < G:
                            project(s, p + 1)
                    if nxt and i == H - 2:
                        project(nxt[0], 0)
                    at = lagged(i, 2, H, now, last)
                    if at:
                        s, q, h = at
                        pe.wait_ge(exp_ready, s * H + h + 3)
                        pe.wait_ge(pt_ready, s * H + h + 1)
                        for c in range(TS):
                            for t in range(TS):
                                k = pe.transpose(K.ps[4 + h % 2][:, c * S + t * P:c * S + (t + 1) * P],
                                                 probs[:, h % 4, t, c * P:(c + 1) * P], K.ident[:, :])
                        k.then_inc(pt_ps, 1)
                    at = lagged(i, 3, H, now, last)
                    if at:
                        s, q, h = at
                        if h == 0:
                            pe.wait_ge(v_ready, s * 4 + 4)
                        if h % 2 == 0:
                            pe.wait_ge(on_ready, s * G + h // 2 + 1)
                        pe.wait_ge(pt_ready, s * H + h + 3)
                        for t in range(TS):
                            for c in range(TS):
                                k = pe.matmul(K.ps[6][:, t * P + (h % 2) * DH:t * P + (h % 2 + 1) * DH],
                                              probst[:, h % 2, c * S + t * P:c * S + (t + 1) * P],
                                              v[:, q, c, h * DH:(h + 1) * DH], start=(c == 0), stop=(c == 1))
                        k.then_inc(av_ps, 1)
                    at = lagged(i, 5, H, now, last)
                    if at and at[2] % 2 == 1:
                        s, q, h = at
                        p = h // 2
                        pe.wait_ge(on_ready, s * G + p + 2)
                        pe.wait_ge(ot_ready, s * G + p + 1)
                        for t in range(TS):
                            k = pe.transpose(K.ps[1][:, t * P:(t + 1) * P], on[:, p % 2, t, :], K.ident[:, :])
                        k.then_inc(ot_ps, 1)
                    if last and Y0 <= i < Y0 + TS:
                        s, q = last
                        j = i - Y0
                        pe.wait_ge(ot_ready, (s + 1) * G + 1)
                        for p in range(G):
                            k = pe.matmul(K.ps[7][:, j * P:(j + 1) * P], outt[:, q, p, j * P:(j + 1) * P],
                                          wo[:, p * P:(p + 1) * P], start=(p == 0), stop=(p == G - 1))
                        if j == TS - 1:
                            k.then_inc(y_ps, 1)
                    if nxt:
                        prepare(i, *nxt, nxt[0])

                for i in range(H):
                    prepare(i, 0, 0, 1)
                project(0, 0)
                over_sequences(pe, slot, H, TAIL)



E = 16
HI, MID, LO = 0, 32, 64
PARTS = LO + E


class Router:
    def __init__(self, K, stage, topk):
        sb = K.sb
        self.topk = topk
        self.lg_ps, self.top, self.wexp, self.comb, self.combt_ps, self.parts = make_sems(
            K, stage, "logits_product top_ready weights_exp comb_ready combt_product parts_ready")
        self.lg = sb(f"{stage}_logits", [P, TS, E])
        self.top8 = sb(f"{stage}_top8", [P, TS, 8])
        self.idx = sb(f"{stage}_idx", [P, TS, 8], U32)
        self.idxf = sb(f"{stage}_idxf", [P, TS, 8])
        self.negm = sb(f"{stage}_negmax", [P, TS])
        self.wexps = sb(f"{stage}_wexp", [P, TS, topk])
        self.wsum = sb(f"{stage}_wsum", [P, TS])
        self.winv = sb(f"{stage}_winv", [P, TS])
        self.hot = sb(f"{stage}_onehot", [P, TS, topk, E])
        self.raw = sb(f"{stage}_comb_raw", [P, TS, E])
        self.out = sb(f"{stage}_comb", [P, TS, E])
        self.t32 = sb(f"{stage}_combt", [E, W])
        self.rest = sb(f"{stage}_comb_rest", [E, W])
        self.mid = sb(f"{stage}_comb_mid", [E, W], BF16)
        self.part = sb(f"{stage}_comb_parts", [PARTS, W], BF16)


def route_tensor_logits(K, R, pe, xnt, rw):
    for j in range(TS):
        i = pe.matmul(K.ps[1][:, j * E:(j + 1) * E], xnt[:, j * P:(j + 1) * P], rw, start=True, stop=True)
    i.then_inc(R.lg_ps, 1)


def route_vector(K, R, dve, link, s, rb):
    dve.wait_ge(R.lg_ps, s + 1)
    link(dve.tensor_tensor(R.lg[:, :, :].rearrange("p t e -> p (t e)"), K.ps[1][:, 0:TS * E], rb, ALU.add))
    for j in range(TS):
        i = dve.max(R.top8[:, j, :], R.lg[:, j, :])
    link(i)
    dve.tensor_scalar(R.negm[:, :], R.top8[:, :, 0], -1.0, None, ALU.mult).then_inc(R.top, 1)
    for j in range(TS):
        i = dve.max_index(R.idx[:, j, :], R.top8[:, j, :], R.lg[:, j, :])
    link(i)
    link(dve.tensor_copy(R.idxf[:, :, :], R.idx[:, :, :]))
    dve.wait_ge(R.wexp, s + 1)
    dve.tensor_reduce(R.wsum[:, :], R.wexps[:, :, :], AX_X, ALU.add)
    for j in range(TS):
        for k in range(R.topk):
            i = dve.tensor_scalar(R.hot[:, j, k, :], K.iota16[:, :], R.idxf[:, j, k:k + 1],
                                  R.wexps[:, j, k:k + 1], ALU.is_equal, ALU.mult)
    link(i)
    dve.reciprocal(R.winv[:, :], R.wsum[:, :])
    for j in range(TS):
        i = dve.tensor_reduce(R.raw[:, j, :], R.hot[:, j, :, :].rearrange("p k e -> p e k"), AX_X, ALU.add)
    link(i)
    for j in range(TS):
        i = dve.tensor_scalar(R.out[:, j, :], R.raw[:, j, :], R.winv[:, j:j + 1], None, ALU.mult)
    i.then_inc(R.comb, 1)


def route_scalar(K, R, act, s):
    act.wait_ge(R.top, s + 1)
    for j in range(TS):
        i = act.activation(R.wexps[:, j, :], R.top8[:, j, 0:R.topk], ACT.Exp, bias=R.negm[:, j:j + 1])
    i.then_inc(R.wexp, 1)


def route_tensor_transpose(K, R, pe, s):
    pe.wait_ge(R.comb, s + 1)
    for j in range(TS):
        i = pe.transpose(K.ps[1][0:E, W + j * P:W + (j + 1) * P], R.out[:, j, :], K.ident[:, :])
    i.then_inc(R.combt_ps, 1)


def route_vector_parts(K, R, dve, link, s):
    dve.wait_ge(R.combt_ps, s + 1)
    link(dve.tensor_copy(R.t32[:, :], K.ps[1][0:E, W:2 * W]))
    link(dve.tensor_copy(R.part[HI:HI + E, :], R.t32[:, :]))
    link(dve.tensor_tensor(R.rest[:, :], R.t32[:, :], R.part[HI:HI + E, :], ALU.subtract))
    link(dve.tensor_copy(R.mid[:, :], R.rest[:, :]))
    dve.tensor_copy(R.part[MID:MID + E, :], R.mid[:, :])
    dve.tensor_tensor(R.part[LO:LO + E, :], R.rest[:, :], R.mid[:, :], ALU.subtract).then_inc(R.parts, 1)



def stage_gated_experts(K, tag):
    nc = K.nc
    G = E // 2
    with ExitStack() as scope:
        K.scope = scope
        sb = K.sb
        N = Norm(K, tag)
        R = Router(K, tag, 2)
        xnt = sb(f"{tag}_xnt", [P, W])
        act_g = sb(f"{tag}_silu", [P, 2, W])
        gated = sb(f"{tag}_gated", [P, 2, W])
        hid = sb(f"{tag}_hidden", [P, 3, W])
        (link_s, xnt_ready, gu_ps, silu_ready, c_ps, gated_ready, hid_ready, y_ps, done, down_done, zeroed) = make_sems(
            K, tag, "dve_chain xnt_ready gate_up_product silu_ready comb_product gated_ready hidden_ready "
                    "y_product seq_done down_issued parts_zeroed")
        f = lambda n: field(K, "m1", n)
        GATE = [f("gate")[:, g * P:(g + 1) * P] for g in range(G)] + [f("shg")]
        UP = [f("up")[:, g * P:(g + 1) * P] for g in range(G)] + [f("shu")]
        DOWN = [f("down")[:, g * P:(g + 1) * P] for g in range(G)] + [f("shd")]
        ORDER = [G] + list(range(G))
        NG = G + 1
        STATS, APPLY, XT = NG - 4, NG - 3, NG - 2

        def over_sequences(eng, prepare, main):
            for n in (STATS, APPLY, XT):
                prepare(0, n)
            with eng.Fori(0, B - 1) as s:
                main(s, True)
            main(B - 1, False)
        with nc.Block() as block:
            K.start_loads(block, tag)

            @block.vector
            def _(dve):
                dve.sem_inc(done, 1)
                dve.wait_ge(K.consts_ready, K.N_CONST)
                dve.wait_ge(K.loaded["m1"], 16)
                link = chain(dve, link_s)
                link(dve.memset(R.part[:, :], 0.0))

                def prepare(s, n):
                    xs = lambda j: K.x[:, bass.ds(s * W + j * P, P)]
                    if n == STATS:
                        norm_stats(N, dve, xs)
                    if n == APPLY:
                        norm_apply(N, dve, xs, s)
                    if n == XT:
                        dve.wait_ge(N.xt, s + 1)
                        dve.tensor_copy(xnt[:, :], K.ps[0][:, 0:W]).then_inc(xnt_ready, 1)

                def main(s, more):
                    link = chain(dve, link_s)
                    route_vector(K, R, dve, link, s, f("rb"))
                    route_vector_parts(K, R, dve, link, s)
                    for n, g in enumerate(ORDER):
                        dve.wait_ge(silu_ready, s * NG + n + 1)
                        if n >= 3:
                            dve.wait_ge(down_done, s * NG + n - 2)
                        dst = hid[:, n % 3, :] if g == G else gated[:, n % 2, :]
                        i = dve.tensor_tensor(dst, act_g[:, n % 2, :], K.ps[2 + n % 2][:, W:2 * W], ALU.mult)
                        if g == G:
                            link(i)
                            dve.sem_inc(gated_ready, 1)
                            dve.sem_inc(hid_ready, 1)
                        else:
                            i.then_inc(gated_ready, 1)
                            dve.wait_ge(gated_ready, s * NG + n + 1)
                            dve.wait_ge(c_ps, s * G + n)
                            dve.tensor_tensor(hid[:, n % 3, :], gated[:, n % 2, :], K.ps[4 + n % 2][:, 0:W],
                                              ALU.mult).then_inc(hid_ready, 1)
                        if more:
                            prepare(s + 1, n)
                    dve.wait_ge(y_ps, s + 1)
                    for j in range(TS):
                        xj = K.x[:, bass.ds(s * W + j * P, P)]
                        i = dve.scalar_tensor_tensor(xj, K.ps[6 + j][:, 0:P], 0.5, xj, ALU.mult, ALU.add)
                    i.then_inc(done, 1)
                over_sequences(dve, prepare, main)

            @block.gpsimd
            def _(pool):
                with pool.Fori(0, B) as s:
                    norm_pool(K, N, pool, s)

            @block.scalar
            def _(act):
                with act.Fori(0, B) as s:
                    route_scalar(K, R, act, s)
                    for n in range(NG):
                        act.wait_ge(gu_ps, s * NG + n + 1)
                        if n >= 2:
                            act.wait_ge(gated_ready, s * NG + n - 1)
                        act.activation(act_g[:, n % 2, :], K.ps[2 + n % 2][:, 0:W], ACT.Silu).then_inc(silu_ready, 1)

            @block.tensor
            def _(pe):
                pe.wait_ge(K.consts_ready, K.N_CONST)
                pe.wait_ge(K.loaded["m1"], 16)

                def prepare(s, n):
                    if n == XT:
                        norm_tensor(K, N, pe, s, K.ps[0])

                def main(s, more):
                    pe.wait_ge(xnt_ready, s + 1)
                    pe.wait_ge(done, s + 1)
                    route_tensor_logits(K, R, pe, xnt, f("rw"))

                    def gate_up(n):
                        if n >= 2:
                            pe.wait_ge(gated_ready, s * NG + n - 1)
                        pe.matmul(K.ps[2 + n % 2][:, 0:W], GATE[ORDER[n]], xnt[:, :], start=True, stop=True)
                        pe.matmul(K.ps[2 + n % 2][:, W:2 * W], UP[ORDER[n]], xnt[:, :],
                                  start=True, stop=True).then_inc(gu_ps, 1)

                    def spread(n):
                        g = ORDER[n]
                        if n >= 3:
                            pe.wait_ge(hid_ready, s * NG + n - 1)
                        pe.matmul(K.ps[4 + n % 2][:, 0:W], K.sel64[:, 2 * g * 64:(2 * g + 2) * 64],
                                  R.part[:, :], start=True, stop=True).then_inc(c_ps, 1)

                    gate_up(0)
                    gate_up(1)
                    route_tensor_transpose(K, R, pe, s)
                    pe.wait_ge(R.parts, s + 1)
                    for n in range(NG):
                        if n >= 1 and n + 1 < NG:
                            gate_up(n + 1)
                        if n + 1 < NG:
                            spread(n + 1)
                        pe.wait_ge(hid_ready, s * NG + n + 1)
                        for j in range(TS):
                            i = pe.matmul(K.ps[6 + j][:, 0:P], hid[:, n % 3, j * P:(j + 1) * P], DOWN[ORDER[n]],
                                          start=(n == 0), stop=(n == NG - 1))
                        i.then_inc(down_done, 1)
                        if n == NG - 1:
                            pe.wait_ge(down_done, s * NG + NG)
                            pe.sem_inc(y_ps, 1)
                        if more:
                            prepare(s + 1, n)
                over_sequences(pe, prepare, main)



def stage_gelu_experts(K, tag):
    nc = K.nc
    with ExitStack() as scope:
        K.scope = scope
        sb = K.sb
        N = Norm(K, tag)
        R = Router(K, tag, 4)
        xnt = sb(f"{tag}_xnt", [P, W])
        gelu = sb(f"{tag}_gelu", [P, 2, 2, W])
        hid = sb(f"{tag}_hidden", [P, 3, 2, W])
        (link_s, xnt_ready, h_ps, gelu_ready, c_ps, hid_ready, y_ps, done, down_done) = make_sems(
            K, tag, "dve_chain xnt_ready hidden_product gelu_ready comb_product hidden_ready "
                    "y_product seq_done down_issued")
        f = lambda n: field(K, "m2", n)
        w1, b1, w2 = f("w1"), f("b1"), f("w2")
        STATS, APPLY, XT = E - 5, E - 4, E - 3

        def over_sequences(eng, prepare, main):
            for n in (STATS, APPLY, XT):
                prepare(0, n)
            with eng.Fori(0, B - 1) as s:
                main(s, True)
            main(B - 1, False)
        with nc.Block() as block:
            K.start_loads(block, tag)

            @block.vector
            def _(dve):
                dve.sem_inc(done, 1)
                dve.wait_ge(K.consts_ready, K.N_CONST)
                dve.wait_ge(K.loaded["m2"], 16)
                link = chain(dve, link_s)
                link(dve.memset(R.part[:, :], 0.0))

                def prepare(s, n):
                    xs = lambda j: K.x[:, bass.ds(s * W + j * P, P)]
                    if n == STATS:
                        norm_stats(N, dve, xs)
                    if n == APPLY:
                        norm_apply(N, dve, xs, s)
                    if n == XT:
                        dve.wait_ge(N.xt, s + 1)
                        dve.tensor_copy(xnt[:, :], K.ps[0][:, 0:W]).then_inc(xnt_ready, 1)

                def main(s, more):
                    link = chain(dve, link_s)
                    route_vector(K, R, dve, link, s, f("rb"))
                    route_vector_parts(K, R, dve, link, s)
                    for e in range(E):
                        dve.wait_ge(gelu_ready, s * E + e + 1)
                        dve.wait_ge(c_ps, s * E + e + 1)
                        if e >= 3:
                            dve.wait_ge(down_done, s * E + e - 2)
                        for c in range(2):
                            i = dve.tensor_tensor(hid[:, e % 3, c, :], gelu[:, e % 2, c, :], K.ps[4 + e % 2][:, 0:W],
                                                  ALU.mult)
                        i.then_inc(hid_ready, 1)
                        if more:
                            prepare(s + 1, e)
                    dve.wait_ge(y_ps, s + 1)
                    for j in range(TS):
                        xj = K.x[:, bass.ds(s * W + j * P, P)]
                        i = dve.scalar_tensor_tensor(xj, K.ps[6 + j][:, 0:P], 0.5, xj, ALU.mult, ALU.add)
                    i.then_inc(done, 1)
                over_sequences(dve, prepare, main)

            @block.gpsimd
            def _(pool):
                with pool.Fori(0, B) as s:
                    norm_pool(K, N, pool, s)

            @block.scalar
            def _(act):
                act.wait_ge(K.loaded["m2"], 16)
                with act.Fori(0, B) as s:
                    route_scalar(K, R, act, s)
                    for e in range(E):
                        act.wait_ge(h_ps, s * E + e + 1)
                        if e >= 2:
                            act.wait_ge(hid_ready, s * E + e - 1)
                        for c in range(2):
                            i = act.activation(gelu[:, e % 2, c, :], K.ps[2 + e % 2][:, c * W:(c + 1) * W], ACT.Gelu,
                                               bias=b1[:, 2 * e + c:2 * e + c + 1])
                        i.then_inc(gelu_ready, 1)

            @block.tensor
            def _(pe):
                pe.wait_ge(K.consts_ready, K.N_CONST)
                pe.wait_ge(K.loaded["m2"], 16)

                def prepare(s, n):
                    if n == XT:
                        norm_tensor(K, N, pe, s, K.ps[0])

                def main(s, more):
                    pe.wait_ge(xnt_ready, s + 1)
                    pe.wait_ge(done, s + 1)
                    route_tensor_logits(K, R, pe, xnt, f("rw"))

                    def hidden(e):
                        if e >= 2:
                            pe.wait_ge(gelu_ready, s * E + e - 1)
                        for c in range(2):
                            i = pe.matmul(K.ps[2 + e % 2][:, c * W:(c + 1) * W],
                                          w1[:, e * 256 + c * P:e * 256 + (c + 1) * P], xnt[:, :],
                                          start=True, stop=True)
                        i.then_inc(h_ps, 1)

                    def spread(e):
                        if e >= 2:
                            pe.wait_ge(hid_ready, s * E + e - 1)
                        pe.matmul(K.ps[4 + e % 2][:, 0:W], K.sel[0:PARTS, e * P:(e + 1) * P], R.part[:, :],
                                  start=True, stop=True).then_inc(c_ps, 1)

                    hidden(0)
                    hidden(1)
                    route_tensor_transpose(K, R, pe, s)
                    pe.wait_ge(R.parts, s + 1)
                    for j in range(TS):
                        pe.matmul(K.ps[6 + j][:, 0:P], R.t32[:, j * P:(j + 1) * P], f("b2")[0:E, :],
                                  start=True, stop=False)
                    spread(0)
                    spread(1)
                    for e in range(E):
                        pe.wait_ge(hid_ready, s * E + e + 1)
                        if e + 2 < E:
                            hidden(e + 2)
                            spread(e + 2)
                        for c in range(2):
                            for j in range(TS):
                                i = pe.matmul(K.ps[6 + j][:, 0:P], hid[:, e % 3, c, j * P:(j + 1) * P],
                                              w2[:, (2 * e + c) * P:(2 * e + c + 1) * P],
                                              start=False, stop=(e == E - 1 and c == 1))
                        i.then_inc(down_done, 1)
                        if more:
                            prepare(s + 1, e)
                    pe.wait_ge(down_done, s * E + E)
                    pe.sem_inc(y_ps, 1)
                over_sequences(pe, prepare, main)



def stage_state_space(K, tag):
    nc = K.nc
    L, NS, KC = 4, 16, 4
    C = 2
    R = 4
    with ExitStack() as scope:
        K.scope = scope
        sb = K.sb
        xm = sb(f"{tag}_xm", [P, B * W])
        aneg = sb(f"{tag}_a_neg", [P, L, C * NS])
        xpad = sb(f"{tag}_xn_padded", [P, KC - 1 + S])
        xc = sb(f"{tag}_conv", [P, 2, C, S])
        zs = sb(f"{tag}_gate", [P, 2, C, S])
        dt = sb(f"{tag}_dt", [P, 2, C, S])
        du = sb(f"{tag}_dt_u", [P, 2, C, S])
        part = sb(f"{tag}_bc_parts", [96, 2, S], BF16)
        rest = sb(f"{tag}_bc_rest", [96, S])
        mid = sb(f"{tag}_bc_mid", [96, S], BF16)
        dtr = sb(f"{tag}_dt_rank", [P, S])
        v = sb(f"{tag}_dt_positive", [P, C, S])
        va = sb(f"{tag}_dt_abs", [P, C, S])
        ve = sb(f"{tag}_dt_exp", [P, C, S])
        vl = sb(f"{tag}_dt_ln", [P, C, S])
        vu = sb(f"{tag}_dt_one_plus", [P, C, S])
        vw = sb(f"{tag}_dt_correction", [P, C, S])
        da = sb(f"{tag}_decay", [P, R, C, S])
        csb = sb(f"{tag}_c_spread", [P, R, S])
        dbu = sb(f"{tag}_dbu", [P, R, C, S])
        h = sb(f"{tag}_state", [P, R, C, S])
        hc = sb(f"{tag}_state_c", [P, R, C, S])
        yf = sb(f"{tag}_y", [P, C, S])
        yg = sb(f"{tag}_y_gated", [P, C, S])

        N0 = Norm(K, f"{tag}_in")
        dve_s, exp_s, fold_s = make_sems(K, f"{tag}_in", "dve_chain a_exp folded")
        with nc.Block() as block:
            K.start_loads(block, tag)

            @block.vector
            def _(dve):
                link = chain(dve, dve_s)
                link(dve.memset(xpad[:, :], 0.0))
                link(dve.memset(da[:, :, 1, 0:1], 0.0))
                with dve.Fori(0, B) as s:
                    link = chain(dve, dve_s)
                    for j in range(TS):
                        i = dve.bn_stats(N0.bn[:, j, :], K.x[:, bass.ds(s * W + j * P, P)])
                    link(i)
                    for j in range(TS):
                        i = dve.bn_aggr(N0.mv[:, j, :], N0.bn[:, j, :])
                    i.then_inc(N0.stats, 1)
                    dve.wait_ge(N0.rstd, s + 1)
                    for j in range(TS):
                        dve.tensor_scalar(xm[:, bass.ds(s * W + j * P, P)], K.x[:, bass.ds(s * W + j * P, P)],
                                          N0.mv[:, j, 0:1], N0.rs[:, j:j + 1], ALU.subtract, ALU.mult)
                dve.wait_ge(exp_s, L)
                dve.tensor_scalar(aneg[:, :, :], aneg[:, :, :], -1.0, None, ALU.mult)

            @block.gpsimd
            def _(pool):
                with pool.Fori(0, B) as s:
                    norm_pool(K, N0, pool, s)
                pool.wait_ge(K.loaded["mb"], 16)
                for l in range(L):
                    taps, inx = field(K, "mb", f"taps{l}"), field(K, "mb", f"inx{l}")
                    for k in range(KC):
                        t = taps[:, k * 256:(k + 1) * 256]
                        pool.tensor_tensor(t, t, inx, ALU.mult).then_inc(fold_s, 1)

            @block.scalar
            def _(act):
                act.wait_ge(K.loaded["mb"], 16)
                for l in range(L):
                    act.activation(aneg[:, l, :], field(K, "mb", f"alog{l}"), ACT.Exp).then_inc(exp_s, 1)

        clear_sems(K)
        state_space_layers(K, tag, dict(locals()))
        clear_sems(K)
        add_s, = make_sems(K, tag, "added")
        with nc.Block() as block:
            @block.vector
            def _(dve):
                dve.tensor_tensor(K.x[:, :], K.x[:, :], xm[:, :], ALU.add).then_inc(add_s, 1)
                dve.wait_ge(add_s, 1)


AT = dict(dve_stats=0, pool_rstd=0, dve_norm=1, pe_in=0, act_in=3, pe_conv0=2, pe_conv1=2, pe_gate=2, act_conv=5,
          pe_bc=4, act_bc=6, dve_bc=7, pe_dt=4, act_exp=10, act_ln=10, dve_ln=10, pool_dt=10,
          dve_y=2, pe_out=1, dve_add=5)


def state_space_layers(K, tag, m):
    nc = K.nc
    L, NS, KC, C, R = m["L"], m["NS"], m["KC"], m["C"], m["R"]
    (xm, aneg, xpad, xc, zs, dt, du, part, rest, mid, dtr, v, va, ve, vl, vu, vw, da, csb, dbu, h, hc, yf, yg) = (
        m[n] for n in "xm aneg xpad xc zs dt du part rest mid dtr v va ve vl vu vw da csb dbu h hc yf yg".split())
    flat = lambda a: a.rearrange("p c t -> p (c t)")
    halves = lambda a: a.unsqueeze(1).broadcast_to([P, C, S])
    with ExitStack() as scope:
        K.scope = scope
        N = Norm(K, tag)
        (dve_s, act_s, xn_ready, xin_ps, z_ps, xc_ready, z_ready, bc_ps, part_ready, dtr_ready, dt_ps,
         vu_ready, ln_ready, vw_ready, dt_ready, du_ready, b_ps, c_ps, c_ready, da_ready, h_ready, hc_ready, sum_done,
         yg_ready, out_ps, done, b_used) = make_sems(
            K, tag, "dve_chain act_chain xn_ready conv_product gate_product conv_ready gate_ready "
                    "bc_product parts_ready dt_rank_ready dt_product one_plus_ready ln_ready correction_ready dt_ready "
                    "dtu_ready b_spread c_spread c_ready decay_ready state_ready state_c_ready sum_issued "
                    "y_gated_ready out_product unit_done b_used")
        f = lambda l, n: field(K, "mb", f"{n}{l}")

        def over_units(eng, main):
            for l in range(L):
                main(l, 0, 0, (l - 1, B - 1) if l > 0 else None, (l, 1))
                with eng.Fori(0, (B - 2) // 2) as pair:
                    for d in (1, 2):
                        main(l, pair * 2 + d, d % 2, (l, pair * 2 + (d - 1)), (l, pair * 2 + (d + 1)))
                main(l, B - 1, 1, (l, B - 2), (l + 1, 0) if l + 1 < L else None)

        with nc.Block() as block:
            @block.vector
            def _(dve):
                dve.sem_inc(b_used, 2)
                dve.sem_inc(h_ready, R)
                dve.sem_inc(done, 2)

                def prepare(l, s, q, n):
                    u = s + l * B
                    xs = lambda j: xm[:, bass.ds(s * W + j * P, P)]
                    if n == AT["dve_stats"]:
                        link = chain(dve, dve_s)
                        if l > 0:
                            dve.wait_ge(done, u - B + 3)
                        for j in range(TS):
                            i = dve.bn_stats(N.bn[:, j, :], xs(j))
                        link(i)
                        for j in range(TS):
                            i = dve.bn_aggr(N.mv[:, j, :], N.bn[:, j, :])
                        i.then_inc(N.stats, 1)
                    if n == AT["dve_norm"]:
                        dve.wait_ge(N.rstd, u + 1)
                        for j in range(TS):
                            i = dve.tensor_scalar(N.out[:, j * P:(j + 1) * P], xs(j), N.mv[:, j, 0:1],
                                                  N.rs[:, j:j + 1], ALU.subtract, ALU.mult)
                        i.then_inc(N.xn, 1)
                    if n == AT["dve_bc"]:
                        link = chain(dve, dve_s)
                        dve.wait_ge(bc_ps, u + 1)
                        link(dve.tensor_copy(part[:, q, :], K.ps[0][0:96, 0:S]))
                        link(dve.tensor_tensor(rest[:, :], K.ps[0][0:96, 0:S], part[:, q, :], ALU.subtract))
                        link(dve.tensor_copy(mid[:, :], rest[:, :]))
                        dve.tensor_copy(part[32:64, q, :], mid[32:64, :]).then_inc(part_ready, 1)
                        dve.tensor_tensor(part[64:96, q, :], rest[64:96, :], mid[64:96, :],
                                          ALU.subtract).then_inc(part_ready, 1)
                    if n == AT["dve_ln"]:
                        link = chain(dve, dve_s)
                        dve.wait_ge(vu_ready, u + 1)
                        link(dve.scalar_tensor_tensor(vw[:, :, :], vu[:, :, :], -1.0, ve[:, :, :], ALU.add,
                                                      ALU.subtract))
                        dve.tensor_tensor(vw[:, :, :], vw[:, :, :], v[:, :, :], ALU.subtract).then_inc(vw_ready, 1)

                def end(l, s, q, n):
                    u = s + l * B
                    if n == AT["dve_y"]:
                        link = chain(dve, dve_s)
                        dve.wait_ge(sum_done, (u + 1) * NS + R)
                        for c in range(C):
                            i = dve.scalar_tensor_tensor(yf[:, c, :], xc[:, q, c, :], f(l, "dsk")[:, c:c + 1],
                                                         K.ps[6 + q][:, c * S:(c + 1) * S], ALU.mult, ALU.add)
                        link(i)
                        dve.tensor_tensor(yg[:, :, :], yf[:, :, :], zs[:, q, :, :], ALU.mult).then_inc(yg_ready, 1)
                    if n == AT["dve_add"]:
                        dve.wait_ge(out_ps, u + 1)
                        xs = xm[:, bass.ds(s * W, W)]
                        dve.tensor_tensor(xs, K.ps[6 + q][:, 0:W], xs, ALU.add).then_inc(done, 1)

                def input_term(g, q, n):
                    dve.wait_ge(h_ready, g + 1)
                    dve.wait_ge(b_ps, g + 1)
                    dve.tensor_tensor(dbu[:, n % R, :, :], du[:, q, :, :], halves(K.ps[2 + n % 2][:, 0:S]),
                                      ALU.mult).then_inc(b_used, 1)

                def main(l, s, q, last, nxt):
                    u = s + l * B
                    for n in range(NS):
                        g = u * NS + n
                        if n + 1 < NS:
                            input_term(g + 1, q, n + 1)
                        elif nxt:
                            dve.wait_ge(du_ready, u + 2)
                            input_term(g + 1, 1 - q, 0)
                        dve.wait_ge(b_used, g + 3)
                        dve.wait_ge(hc_ready, g + 1)
                        dve.wait_ge(da_ready, g + 1)
                        dve.tensor_tensor_scan(flat(h[:, n % R, :, :]), flat(da[:, n % R, :, :]),
                                               flat(dbu[:, n % R, :, :]), 0.0, ALU.mult,
                                               ALU.add).then_inc(h_ready, 1)
                        if last:
                            end(*last, 1 - q, n)
                        if nxt:
                            prepare(*nxt, 1 - q, n)
                for n in range(NS):
                    prepare(0, 0, 0, n)
                dve.wait_ge(du_ready, 1)
                input_term(0, 0, 0)
                over_units(dve, main)
                for n in range(NS):
                    end(L - 1, B - 1, 1, n)

            @block.gpsimd
            def _(pool):
                pool.sem_inc(hc_ready, R)

                def prepare(l, s, q, n):
                    u = s + l * B
                    if n == AT["pool_rstd"]:
                        norm_pool(K, N, pool, u)
                    if n == AT["pool_dt"]:
                        pool.wait_ge(ln_ready, u + 1)
                        pool.wait_ge(vw_ready, u + 1)
                        pool.tensor_tensor(dt[:, q, :, :], vl[:, :, :], vw[:, :, :],
                                           ALU.subtract).then_inc(dt_ready, 1)
                        pool.wait_ge(dt_ready, u + 1)
                        pool.tensor_tensor(du[:, q, :, :], dt[:, q, :, :], xc[:, q, :, :], ALU.mult).then_inc(du_ready, 1)

                def main(l, s, q, last, nxt):
                    for n in range(NS):
                        g = (s + l * B) * NS + n
                        pool.wait_ge(c_ready, g + 3)
                        pool.wait_ge(sum_done, g + 1)
                        pool.wait_ge(h_ready, g + 1 + R)
                        pool.tensor_tensor(hc[:, n % R, :, :], h[:, n % R, :, :], halves(csb[:, n % R, :]),
                                           ALU.mult).then_inc(hc_ready, 1)
                        if nxt:
                            prepare(*nxt, 1 - q, n)
                for n in range(NS):
                    prepare(0, 0, 0, n)
                over_units(pool, main)

            @block.scalar
            def _(act):
                act.sem_inc(c_ready, 2)

                def prepare(l, s, q, n):
                    u = s + l * B
                    if n == AT["act_in"]:
                        act.wait_ge(N.xt, u + 1)
                        act.activation(xpad[:, KC - 1:KC - 1 + S], K.ps[0][:, 0:S], ACT.Identity,
                                       bias=f(l, "lnb"), scale=f(l, "lnw")).then_inc(xn_ready, 1)
                    if n == AT["act_conv"]:
                        act.wait_ge(xin_ps, u + 1)
                        for c in range(C):
                            i = act.activation(xc[:, q, c, :], K.ps[0][:, c * S:(c + 1) * S], ACT.Silu,
                                               bias=f(l, "cb")[:, c:c + 1])
                        i.then_inc(xc_ready, 1)
                        act.wait_ge(z_ps, u + 1)
                        act.activation(flat(zs[:, q, :, :]), K.ps[1][:, :], ACT.Silu).then_inc(z_ready, 1)
                    if n == AT["act_bc"]:
                        act.wait_ge(bc_ps, u + 1)
                        act.activation(dtr[96:104, :], K.ps[0][96:104, 0:S], ACT.Copy).then_inc(dtr_ready, 1)
                    if n == AT["act_exp"]:
                        act.sem_clear(act_s)
                        act.wait_ge(dt_ps, u + 1)
                        for c in range(C):
                            i = act.activation(va[:, c, :], K.ps[1][:, c * S:(c + 1) * S], ACT.Abs,
                                               bias=f(l, "dtb")[:, c:c + 1])
                        i.then_inc(act_s, 1)
                        for c in range(C):
                            act.activation(v[:, c, :], K.ps[1][:, c * S:(c + 1) * S], ACT.Relu,
                                           bias=f(l, "dtb")[:, c:c + 1])
                        act.wait_ge(act_s, 1)
                        act.activation(ve[:, :, :], va[:, :, :], ACT.Exp, scale=-1.0).then_inc(act_s, 1)
                    if n == AT["act_ln"]:
                        act.wait_ge(act_s, 2)
                        act.activation(vu[:, :, :], ve[:, :, :], ACT.Identity, bias=K.ones[:, 0:1]).then_inc(vu_ready, 1)
                        act.wait_ge(vu_ready, u + 1)
                        act.activation(vl[:, :, :], vu[:, :, :], ACT.Ln).then_inc(ln_ready, 1)

                def main(l, s, q, last, nxt):
                    u = s + l * B
                    act.wait_ge(du_ready, u + 1)
                    for n in range(NS):
                        g = u * NS + n
                        act.wait_ge(h_ready, g + 1)
                        for c in range(C):
                            i = act.activation(da[:, n % R, c, c:S], dt[:, q, c, c:S], ACT.Exp,
                                               scale=aneg[:, l, c * NS + n:c * NS + n + 1])
                        i.then_inc(da_ready, 1)
                        act.wait_ge(c_ps, g + 1)
                        act.wait_ge(hc_ready, g + 1)
                        act.activation(csb[:, n % R, :], K.ps[4 + n % 2][:, 0:S], ACT.Copy).then_inc(c_ready, 1)
                        if nxt:
                            prepare(*nxt, 1 - q, n)
                for n in range(NS):
                    prepare(0, 0, 0, n)
                over_units(act, main)

            @block.tensor
            def _(pe):
                pe.sem_inc(sum_done, R)

                def convolve(l, c):
                    for k in range(KC):
                        i = pe.matmul(K.ps[0][:, c * S:(c + 1) * S],
                                      f(l, "taps")[:, k * 256 + c * P:k * 256 + (c + 1) * P],
                                      xpad[:, k:k + S], start=(k == 0), stop=(k == KC - 1))
                    return i

                def prepare(l, s, q, n):
                    u = s + l * B
                    if n == AT["pe_in"]:
                        norm_tensor(K, N, pe, u, K.ps[0])
                    if n == AT["pe_conv0"]:
                        pe.wait_ge(xn_ready, u + 1)
                        convolve(l, 0)
                    if n == AT["pe_conv1"]:
                        convolve(l, 1).then_inc(xin_ps, 1)
                    if n == AT["pe_gate"]:
                        for c in range(C):
                            i = pe.matmul(K.ps[1][:, c * S:(c + 1) * S], f(l, "inz")[:, c * P:(c + 1) * P],
                                          xpad[:, KC - 1:KC - 1 + S], start=True, stop=True)
                        i.then_inc(z_ps, 1)
                    if n == AT["pe_bc"]:
                        pe.wait_ge(xc_ready, u + 1)
                        for c in range(C):
                            i = pe.matmul(K.ps[0][0:104, 0:S], f(l, "xp")[:, c * 104:(c + 1) * 104],
                                          xc[:, q, c, :], start=(c == 0), stop=(c == C - 1))
                        i.then_inc(bc_ps, 1)
                    if n == AT["pe_dt"]:
                        pe.wait_ge(dtr_ready, u + 1)
                        pe.wait_ge(z_ready, u + 1)
                        for c in range(C):
                            i = pe.matmul(K.ps[1][:, c * S:(c + 1) * S], f(l, "dtw")[96:104, c * P:(c + 1) * P],
                                          dtr[96:104, :], start=True, stop=True)
                        i.then_inc(dt_ps, 1)

                def spread(g, q, n):
                    pe.wait_ge(b_used, g + 1)
                    pe.matmul(K.ps[2 + n % 2][:, 0:S], K.sel[:, n * P:(n + 1) * P], part[:, q, :],
                              start=True, stop=True).then_inc(b_ps, 1)
                    pe.wait_ge(c_ready, g + 1)
                    pe.matmul(K.ps[4 + n % 2][:, 0:S], K.sel[:, (NS + n) * P:(NS + n + 1) * P], part[:, q, :],
                              start=True, stop=True).then_inc(c_ps, 1)

                def out_product(l, s, q):
                    pe.wait_ge(yg_ready, s + l * B + 1)
                    for j in range(TS):
                        for c in range(C):
                            i = pe.matmul(K.ps[6 + q][:, j * P:(j + 1) * P], yg[:, c, j * P:(j + 1) * P],
                                          f(l, "outw")[:, c * P:(c + 1) * P], start=(c == 0), stop=(c == C - 1))
                    i.then_inc(out_ps, 1)

                AHEAD = 3
                def main(l, s, q, last, nxt):
                    u = s + l * B
                    for n in range(NS):
                        g = u * NS + n
                        if n + AHEAD < NS:
                            spread(g + AHEAD, q, n + AHEAD)
                        elif nxt:
                            if n + AHEAD == NS:
                                pe.wait_ge(part_ready, 2 * (u + 2))
                            spread(g + AHEAD, 1 - q, n + AHEAD - NS)
                        if n == 0:
                            pe.wait_ge(done, u + 1)
                        pe.wait_ge(hc_ready, g + 1 + R)
                        pe.matmul(K.ps[6 + q][:, :], K.ident[:, :], flat(hc[:, n % R, :, :]),
                                  start=(n == 0), stop=(n == NS - 1)).then_inc(sum_done, 1)
                        if last and n == AT["pe_out"]:
                            out_product(*last, 1 - q)
                        if nxt:
                            prepare(*nxt, 1 - q, n)
                for n in range(NS):
                    prepare(0, 0, 0, n)
                pe.wait_ge(part_ready, 2)
                for n in range(AHEAD):
                    spread(n, 0, n)
                over_units(pe, main)
                out_product(L - 1, B - 1, 1)



def stage_window_linear_attention(K, tag):
    nc = K.nc
    H, DH, HALF = 16, 8, 32
    G, KW = 4, 160
    KEY0 = (0, S - KW)
    BAND0 = (HALF, 0)
    BW = P + 2 * HALF
    SCALE = float(np.float32(1.0 / np.sqrt(DH)))
    with ExitStack() as scope:
        K.scope = scope
        sb = K.sb
        N = Norm(K, f"{tag}_a")
        M = Norm(K, f"{tag}_b")
        ht = sb(f"{tag}_ht", [P, W])
        band = field(K, "a2", "band").rearrange("p (h j) -> p h j", h=H)
        qmin = sb(f"{tag}_qmin", [P, S])
        qmax = sb(f"{tag}_qmax", [P, S])
        ql = sb(f"{tag}_ql", [P, S])
        klin = sb(f"{tag}_klin", [P, TS, P])
        kmin = sb(f"{tag}_kmin", [P, TS, P])
        kl = sb(f"{tag}_kl", [P, TS, P])
        vo = sb(f"{tag}_v_ones", [P, TS, 2 * P])
        kvs = sb(f"{tag}_kv_ksum", [P, 2 * P])
        den = sb(f"{tag}_den", [P, S])
        dinv = sb(f"{tag}_dinv", [P, S])
        lint = sb(f"{tag}_lin_t", [P, S])
        q4 = sb(f"{tag}_q4", [P, G, S])
        k4 = sb(f"{tag}_k4", [P, G, S])
        vw = sb(f"{tag}_v_window", [P, TS, P])
        vtail = sb(f"{tag}_v_tail", [HALF, P])
        sc = sb(f"{tag}_scores", [P, 2, TS, KW])
        mx = sb(f"{tag}_max", [P, H, TS])
        nmx = sb(f"{tag}_nmax", [P, H, TS])
        rsum = sb(f"{tag}_rsum", [P, TS, H])
        rinv = sb(f"{tag}_rinv", [P, TS, H])
        pr = sb(f"{tag}_probs", [P, 3, TS, KW])
        pt = sb(f"{tag}_probst", [P, 2, 2, TS * P])
        win = sb(f"{tag}_win", [P, TS, P])
        wint = sb(f"{tag}_win_t", [P, S])
        g1 = sb(f"{tag}_gate1", [P, S])
        gate = sb(f"{tag}_gate", [P, S])
        diff = sb(f"{tag}_diff", [P, S])
        gd = sb(f"{tag}_gate_diff", [P, S])
        ot = sb(f"{tag}_out_t", [P, S])
        (dve_s, masked, ht_ready, ql_ps, qmin_ready, qexp_ready, kv_ps, kmin_ready, kexp_ready, kl_ready, kvs_ps,
         kvs_ready, lin_ps, lin_ready, qk_ps, qk_ready, v_ps, v_ready, sc_ps, max_ready, exp_ready, pt_ps, pt_ready,
         o_ps, win_ready, wint_ps, wint_ready, g1_ps, g1_ready, g2_ps, gate_ready, ot_ready, y_ps, done,
         hold) = make_sems(
            K, tag, "dve_chain band_masked ht_ready ql_product qmin_ready qexp_ready kv_product kmin_ready "
                    "kexp_ready kl_ready kv_sum_product kv_sum_ready lin_product lin_ready qk_product qk_ready "
                    "v_product v_ready scores_product max_ready exp_ready probst_product probst_ready out_product "
                    "win_ready wint_product wint_ready gate1_product gate1_ready gate2_product gate_ready "
                    "mix_ready y_product seq_done hold")
        f = lambda n: field(K, "a2", n)
        STEPS = H + 3
        at, _ = pack_offset("a2", "wkl")
        wkv = K.pack["a2"][:, at:at + 2 * P]
        at, _ = pack_offset("a2", "bkl")
        bkv = K.pack["a2"][:, at:at + 2 * P]
        with nc.Block() as block:
            K.start_loads(block, tag)

            @block.vector
            def _(dve):
                dve.sem_inc(done, 1)
                dve.wait_ge(K.loaded["a2"], 16)
                link = chain(dve, dve_s)
                link(dve.memset(vo[:, :, :], 1.0))
                dve.wait_ge(masked, 2)
                with dve.Fori(0, B) as s:
                    link = chain(dve, dve_s)
                    norm_vector(K, N, dve, link, lambda j: K.x[:, bass.ds(s * W + j * P, P)], s)
                    dve.wait_ge(N.xn, s + 1)
                    norm_vector(K, M, dve, link, lambda j: N.out[:, j * P:(j + 1) * P], s)
                    dve.wait_ge(ql_ps, s + 1)
                    dve.tensor_scalar(qmin[:, :], K.ps[1][:, 0:S], f("bql"), 0.0, ALU.add, ALU.min).then_inc(qmin_ready, 1)
                    link(dve.tensor_scalar(qmax[:, :], K.ps[1][:, 0:S], f("bql"), 0.0, ALU.add, ALU.max))
                    dve.wait_ge(kv_ps, s + 1)
                    for j in range(TS):
                        dve.tensor_tensor(klin[:, j, :], K.ps[7][:, j * W:j * W + P], bkv[:, 0:P], ALU.add)
                        i = dve.tensor_tensor(vo[:, j, 0:P], K.ps[7][:, j * W + P:(j + 1) * W], bkv[:, P:2 * P], ALU.add)
                    link(i)
                    dve.tensor_scalar(kmin[:, :, :], klin[:, :, :], 0.0, None, ALU.min).then_inc(kmin_ready, 1)
                    dve.wait_ge(kexp_ready, s + 1)
                    dve.scalar_tensor_tensor(kl[:, :, :], klin[:, :, :], 0.0, kmin[:, :, :], ALU.max, ALU.add)\
                       .then_inc(kl_ready, 1)
                    dve.tensor_tensor(ql[:, :], qmax[:, :], qmin[:, :], ALU.add).then_inc(kl_ready, 1)
                    for g in range(G):
                        dve.wait_ge(qk_ps, s * G + g + 1)
                        bank = K.ps[(1, 6)[g % 2]]
                        dve.tensor_scalar(q4[:, g, :], bank[:, 0:S], f("bq4")[:, g:g + 1], SCALE, ALU.add, ALU.mult)
                        dve.tensor_scalar(k4[:, g, :], bank[:, S:2 * S], f("bk4")[:, g:g + 1], None,
                                          ALU.add).then_inc(qk_ready, 1)
                    dve.wait_ge(v_ps, s + 1)
                    for j in range(TS):
                        dve.tensor_tensor(vw[:, j, :], K.ps[7][:, j * P:(j + 1) * P], f("bvc"), ALU.add)
                    dve.tensor_tensor(vtail[:, :], K.ps[7][0:HALF, 2 * P:3 * P], f("bvc")[0:HALF, :],
                                      ALU.add).then_inc(v_ready, 1)

                    for i in range(STEPS):
                        if i < H:
                            dve.wait_ge(sc_ps, s * H + i + 1)
                            if i >= 2:
                                dve.wait_ge(exp_ready, s * H + i - 1)
                            dve.sem_inc(hold, 1)
                            for t in range(TS):
                                k = dve.tensor_tensor_reduce(
                                    sc[:, i % 2, t, :], K.ps[2 + i % 2][:, t * KW:(t + 1) * KW],
                                    band[:, i, BAND0[t]:BAND0[t] + KW], 1.0, -3e38, ALU.add, ALU.max, mx[:, i, t:t + 1])
                            link(k)
                            dve.tensor_scalar(nmx[:, i, :], mx[:, i, :], -1.0, None, ALU.mult).then_inc(max_ready, 1)
                        if i == 4:
                            dve.wait_ge(kvs_ps, s + 1)
                            dve.tensor_copy(kvs[:, :], K.ps[0][:, 0:2 * P]).then_inc(kvs_ready, 1)
                        if i == 8:
                            dve.wait_ge(lin_ps, s + 1)
                            link(dve.tensor_scalar(den[:, :], K.ps[0][:, S:2 * S], 1e-6, None, ALU.add))
                            link(dve.reciprocal(dinv[:, :], den[:, :]))
                            dve.tensor_tensor(lint[:, :], K.ps[0][:, 0:S], dinv[:, :], ALU.mult).then_inc(lin_ready, 1)
                    dve.wait_ge(exp_ready, s * H + H)
                    link(dve.reciprocal(rinv[:, :, :], rsum[:, :, :]))
                    dve.wait_ge(o_ps, s * H + H)
                    for j in range(TS):
                        i = dve.tensor_tensor(win[:, j, :].rearrange("p (h d) -> p h d", h=H),
                                              K.ps[6][:, j * P:(j + 1) * P].rearrange("p (h d) -> p h d", h=H),
                                              rinv[:, j, :].unsqueeze(2).broadcast_to([P, H, DH]), ALU.mult)
                    i.then_inc(win_ready, 1)
                    dve.wait_ge(wint_ps, s + 1)
                    dve.tensor_copy(wint[:, :], K.ps[7][:, 0:S]).then_inc(wint_ready, 1)
                    dve.wait_ge(wint_ready, s + 1)
                    link(dve.tensor_tensor(diff[:, :], lint[:, :], wint[:, :], ALU.subtract))
                    dve.wait_ge(gate_ready, s + 1)
                    link(dve.tensor_tensor(gd[:, :], gate[:, :], diff[:, :], ALU.mult))
                    dve.tensor_tensor(ot[:, :], gd[:, :], wint[:, :], ALU.add).then_inc(ot_ready, 1)
                    xs = K.x[:, bass.ds(s * W, W)]
                    link(dve.tensor_tensor(xs, xs, N.out[:, :], ALU.add))
                    for j in range(TS):
                        xj = K.x[:, bass.ds(s * W + j * P, P)]
                        i = dve.tensor_tensor(xj, xj, f("bo"), ALU.add)
                    link(i)
                    dve.wait_ge(y_ps, s + 1)
                    dve.tensor_tensor(xs, K.ps[0][:, 0:W], xs, ALU.add).then_inc(done, 1)

            @block.gpsimd
            def _(pool):
                pool.wait_ge(K.loaded["a2"], 16)
                pool.affine_select(out=band, in_=band, compare_op=ALU.is_ge, fill=-1e30, base=0,
                                   pattern=[[0, H], [1, BW]], channel_multiplier=-1).then_inc(masked, 1)
                pool.wait_ge(masked, 1)
                pool.affine_select(out=band, in_=band, compare_op=ALU.is_ge, fill=-1e30, base=2 * HALF,
                                   pattern=[[0, H], [-1, BW]], channel_multiplier=1).then_inc(masked, 1)
                with pool.Fori(0, B) as s:
                    norm_pool(K, N, pool, s)
                    norm_pool(K, M, pool, s)

            @block.scalar
            def _(act):
                act.wait_ge(K.loaded["a2"], 16)
                with act.Fori(0, B) as s:
                    act.wait_ge(M.xt, s + 1)
                    act.activation(ht[:, :], K.ps[0][:, 0:W], ACT.Identity, bias=f("lnb"), scale=f("lng")).then_inc(ht_ready, 1)
                    act.wait_ge(qmin_ready, s + 1)
                    act.activation(qmin[:, :], qmin[:, :], ACT.Exp)
                    act.wait_ge(kmin_ready, s + 1)
                    act.activation(kmin[:, :, :], kmin[:, :, :], ACT.Exp).then_inc(kexp_ready, 1)
                    for i in range(STEPS):
                        if i < H:
                            act.wait_ge(max_ready, s * H + i + 1)
                            if i >= 3:
                                act.wait_ge(pt_ps, s * H + i - 2)
                            for t in range(TS):
                                k = act.activation(pr[:, i % 3, t, :], sc[:, i % 2, t, :], ACT.Exp,
                                                   bias=nmx[:, i, t:t + 1], accum_out=rsum[:, t, i:i + 1])
                            k.then_inc(exp_ready, 1)
                        if 2 <= i < H + 2:
                            h = i - 2
                            act.wait_ge(pt_ps, s * H + h + 1)
                            if h >= 2:
                                act.wait_ge(o_ps, s * H + h - 1)
                            act.activation(pt[:, h % 2, 0, :], K.ps[4 + h % 2][:, 0:W], ACT.Copy)
                            act.activation(pt[0:HALF, h % 2, 1, :], K.ps[4 + h % 2][0:HALF, W:2 * W],
                                           ACT.Copy).then_inc(pt_ready, 1)
                    act.wait_ge(g1_ps, s + 1)
                    act.activation(g1[:, :], K.ps[7][:, S:2 * S], ACT.Relu, bias=f("bg1")).then_inc(g1_ready, 1)
                    act.wait_ge(g2_ps, s + 1)
                    act.activation(gate[:, :], K.ps[1][:, 0:S], ACT.Sigmoid, bias=f("bg2")).then_inc(gate_ready, 1)

            @block.tensor
            def _(pe):
                pe.wait_ge(K.consts_ready, K.N_CONST)
                pe.wait_ge(K.loaded["a2"], 16)
                with pe.Fori(0, B) as s:
                    norm_tensor(K, M, pe, s, K.ps[0])
                    pe.wait_ge(ht_ready, s + 1)
                    pe.wait_ge(done, s + 1)
                    pe.matmul(K.ps[1][:, 0:S], f("wql"), ht[:, :], start=True, stop=True).then_inc(ql_ps, 1)
                    for j in range(TS):
                        i = pe.matmul(K.ps[7][:, j * W:(j + 1) * W], ht[:, j * P:(j + 1) * P], wkv, start=True, stop=True)
                    i.then_inc(kv_ps, 1)
                    for g in range(G):
                        bank = K.ps[(1, 6)[g % 2]]
                        if g == 0:
                            pe.wait_ge(kmin_ready, s + 1)
                        if g >= 2:
                            pe.wait_ge(qk_ready, s * G + g - 1)
                        pe.matmul(bank[:, 0:S], f("wq4")[:, g * P:(g + 1) * P], ht[:, :], start=True, stop=True)
                        pe.matmul(bank[:, S:2 * S], f("wk4")[:, g * P:(g + 1) * P], ht[:, :],
                                  start=True, stop=True).then_inc(qk_ps, 1)
                    for j in range(TS):
                        pe.matmul(K.ps[7][:, j * P:(j + 1) * P], ht[:, j * P:(j + 1) * P], f("wvc"), start=True, stop=True)
                    pe.matmul(K.ps[7][0:HALF, 2 * P:3 * P], ht[:, P - HALF:P], f("wvc"),
                              start=True, stop=True).then_inc(v_ps, 1)
                    pe.wait_ge(kl_ready, 2 * (s + 1))
                    for j in range(TS):
                        i = pe.matmul(K.ps[0][:, 0:2 * P], kl[:, j, :], vo[:, j, :], start=(j == 0), stop=(j == TS - 1))
                    i.then_inc(kvs_ps, 1)
                    pe.wait_ge(v_ready, s + 1)
                    pe.wait_ge(qk_ready, s * G + G)
                    for i in range(STEPS):
                        if i < H:
                            g, r = i // 4, 32 * (i % 4)
                            if i >= 2:
                                pe.wait_ge(max_ready, s * H + i - 1)
                            for t in range(TS):
                                k = pe.matmul(K.ps[2 + i % 2][:, t * KW:(t + 1) * KW],
                                              q4[r:r + 32, g, t * P:(t + 1) * P], k4[r:r + 32, g, KEY0[t]:KEY0[t] + KW],
                                              start=True, stop=True)
                            k.then_inc(sc_ps, 1)
                        if i == 6:
                            pe.wait_ge(kvs_ready, s + 1)
                            pe.matmul(K.ps[0][:, 0:S], kvs[:, 0:P], ql[:, :], start=True, stop=True)
                            pe.matmul(K.ps[0][:, S:2 * S], kvs[:, P:2 * P], ql[:, :], start=True, stop=True).then_inc(lin_ps, 1)
                        if 2 <= i < H + 2:
                            h = i - 2
                            pe.wait_ge(exp_ready, s * H + h + 1)
                            if h >= 2:
                                pe.wait_ge(pt_ready, s * H + h - 1)
                            bank, pb = K.ps[4 + h % 2], pr[:, h % 3, :, :]
                            pe.transpose(bank[:, 0:P], pb[:, 0, 0:P], K.ident[:, :])
                            pe.transpose(bank[:, P:2 * P], pb[:, 1, HALF:KW], K.ident[:, :])
                            pe.transpose(bank[0:HALF, 2 * P:3 * P], pb[:, 0, P:KW], K.ident[:, :])
                            pe.transpose(bank[0:HALF, 3 * P:4 * P], pb[:, 1, 0:HALF], K.ident[:, :]).then_inc(pt_ps, 1)
                        if 3 <= i:
                            h = i - 3
                            pe.wait_ge(pt_ready, s * H + h + 1)
                            c = slice(h * DH, (h + 1) * DH)
                            for t in range(TS):
                                o = K.ps[6][:, t * P + h * DH:t * P + (h + 1) * DH]
                                pe.matmul(o, pt[:, h % 2, 0, t * P:(t + 1) * P], vw[:, t, c], start=True, stop=False)
                                k = pe.matmul(o, pt[0:HALF, h % 2, 1, t * P:(t + 1) * P],
                                              vw[0:HALF, 1, c] if t == 0 else vtail[:, c], start=False, stop=True)
                            k.then_inc(o_ps, 1)
                    pe.wait_ge(win_ready, s + 1)
                    for j in range(TS):
                        i = pe.transpose(K.ps[7][:, j * P:(j + 1) * P], win[:, j, :], K.ident[:, :])
                    i.then_inc(wint_ps, 1)
                    pe.wait_ge(lin_ready, s + 1)
                    pe.wait_ge(wint_ready, s + 1)
                    for n, src in enumerate((lint, wint, ht)):
                        i = pe.matmul(K.ps[7][:, S:2 * S], f("wg1")[:, n * P:(n + 1) * P], src[:, :],
                                      start=(n == 0), stop=(n == 2))
                    i.then_inc(g1_ps, 1)
                    pe.wait_ge(g1_ready, s + 1)
                    pe.matmul(K.ps[1][:, 0:S], f("wg2"), g1[:, :], start=True, stop=True).then_inc(g2_ps, 1)
                    pe.wait_ge(ot_ready, s + 1)
                    for j in range(TS):
                        i = pe.matmul(K.ps[0][:, j * P:(j + 1) * P], ot[:, j * P:(j + 1) * P], f("wo"), start=True, stop=True)
                    i.then_inc(y_ps, 1)



def stage_quantised_ffn(K, tag):
    nc = K.nc
    NB, U = 3, 4
    with ExitStack() as scope:
        K.scope = scope
        sb = K.sb
        w = sb(f"{tag}_w", [P, 6 * P])
        bn = sb(f"{tag}_bn", [P, U, TS, 6])
        mv = sb(f"{tag}_mv", [P, U, TS, 2])
        rs = sb(f"{tag}_rs", [P, U, TS])
        hcur = sb(f"{tag}_h", [P, U, W])
        hb = sb(f"{tag}_h_bias", [P, U, W])
        ht = sb(f"{tag}_ht", [P, U, W])
        y = sb(f"{tag}_y", [P, U, W])
        yn = sb(f"{tag}_yn", [P, U, W])
        gt = sb(f"{tag}_gelu_t", [P, U, W])
        (dve_s, pool_s, lora_ps, w_ready, stats, rstd, h_ready, ht_ps, ht_ready, y_ps, yn_ready, ynt_ps, gt_ready,
         z_ps, hb_ready, pool_hold, y_sb) = make_sems(
            K, tag, "dve_chain pool_chain lora_product w_ready stats rstd h_ready ht_product ht_ready y_product "
                    "yn_ready ynt_product gelu_ready z_product h_bias_ready pool_hold y_ready")
        f = lambda n: field(K, "f3", n)
        bias = f("bias")
        NL = (NB + 1) * U
        with nc.Block() as block:
            K.start_loads(block, tag)

            @block.vector
            def _(dve):
                dve.wait_ge(K.loaded["f3"], 16)
                dve.wait_ge(K.loaded_q, 16)
                link = chain(dve, dve_s)
                link(dve.tensor_scalar(w[:, :], K.qw[:, :], 7.5, 1.0 / 7.5, ALU.subtract, ALU.mult))
                link(dve.tensor_tensor(w[:, :], w[:, :], f("scale"), ALU.mult))
                dve.wait_ge(lora_ps, 1)
                dve.tensor_tensor(w[:, 0:512], w[:, 0:512], K.ps[0][:, :], ALU.add).then_inc(w_ready, 1)
                dve.tensor_tensor(w[:, 512:768], w[:, 512:768], K.ps[1][:, 0:256], ALU.add).then_inc(w_ready, 1)
                with dve.Fori(0, B // U) as s:
                    link = chain(dve, dve_s)

                    def statistics(u, src):
                        for j in range(TS):
                            i = dve.bn_stats(bn[:, u, j, :], src(j))
                        link(i)
                        for j in range(TS):
                            i = dve.bn_aggr(mv[:, u, j, :], bn[:, u, j, :])
                        i.then_inc(stats, 1)

                    def normalise(u, src, dst):
                        for j in range(TS):
                            i = dve.tensor_scalar(dst[:, u, j * P:(j + 1) * P], src(j), mv[:, u, j, 0:1],
                                                  rs[:, u, j:j + 1], ALU.subtract, ALU.mult)
                        return i

                    xt = lambda u: lambda j: K.x[:, bass.ds((s * U + u) * W + j * P, P)]
                    yt = lambda u: lambda j: y[:, u, j * P:(j + 1) * P]
                    for u in range(U):
                        statistics(u, xt(u))
                    for u in range(U):
                        dve.wait_ge(rstd, s * NL + u + 1)
                        normalise(u, xt(u), hcur).then_inc(h_ready, 1)
                    for b in range(NB):
                        e = s * (NB * U) + b * U
                        for u in range(U):
                            dve.wait_ge(y_ps, e + u + 1)
                            link(dve.tensor_tensor(
                                y[:, u, :].rearrange("p (t o) -> p t o", t=TS),
                                K.ps[2 + u % 2][:, 0:W].rearrange("p (t o) -> p t o", t=TS),
                                bias[:, 2 * b * P:(2 * b + 1) * P].unsqueeze(1).broadcast_to([P, TS, P]), ALU.add))
                            dve.sem_inc(y_sb, 1)
                            statistics(u, yt(u))
                        for u in range(U):
                            dve.wait_ge(rstd, s * NL + (b + 1) * U + u + 1)
                            normalise(u, yt(u), yn).then_inc(yn_ready, 1)
                        for u in range(U):
                            dve.wait_ge(hb_ready, e + u + 1)
                            dve.wait_ge(z_ps, e + u + 1)
                            dve.tensor_tensor(hcur[:, u, :], K.ps[6 + u % 2][:, 0:W], hb[:, u, :],
                                              ALU.add).then_inc(h_ready, 1)
                    for u in range(U):
                        dve.wait_ge(h_ready, s * NL + NB * U + u + 1)
                        xs = K.x[:, bass.ds((s * U + u) * W, W)]
                        link(dve.scalar_tensor_tensor(xs, hcur[:, u, :], 0.5, xs, ALU.mult, ALU.add))

            @block.gpsimd
            def _(pool):
                pool.wait_ge(K.loaded["f3"], 16)
                with pool.Fori(0, B // U) as s:
                    pool.sem_clear(pool_s)
                    count = [0]

                    def rsqrt(u, e):
                        pool.wait_ge(stats, e + 1)
                        pool.sem_inc(pool_hold, 1)
                        pool.tensor_scalar(rs[:, u, :], mv[:, u, :, 1], EPS, None, ALU.add).then_inc(pool_s, 1)
                        count[0] += 1
                        pool.wait_ge(pool_s, count[0])
                        pool.tensor_tensor(rs[:, u, :], rs[:, u, :], K.neg_half[:, 0:TS], ALU.pow).then_inc(rstd, 1)

                    for u in range(U):
                        rsqrt(u, s * NL + u)
                    for b in range(NB):
                        for u in range(U):
                            pool.wait_ge(h_ready, s * NL + b * U + u + 1)
                            for j in range(TS):
                                i = pool.tensor_tensor(hb[:, u, j * P:(j + 1) * P], hcur[:, u, j * P:(j + 1) * P],
                                                       bias[:, (2 * b + 1) * P:(2 * b + 2) * P], ALU.add)
                            i.then_inc(hb_ready, 1)
                        for u in range(U):
                            rsqrt(u, s * NL + (b + 1) * U + u)

            @block.scalar
            def _(act):
                act.wait_ge(K.loaded["f3"], 16)
                with act.Fori(0, B // U) as s:
                    for b in range(NB):
                        e = s * (NB * U) + b * U
                        for u in range(U):
                            act.wait_ge(ht_ps, e + u + 1)
                            act.activation(ht[:, u, :], K.ps[0 + u % 2][:, 0:W], ACT.Copy).then_inc(ht_ready, 1)
                        for u in range(U):
                            act.wait_ge(ynt_ps, e + u + 1)
                            act.activation(gt[:, u, :], K.ps[4 + u % 2][:, 0:W], ACT.Gelu, bias=f("bet")[:, b:b + 1],
                                           scale=f("gam")[:, b:b + 1]).then_inc(gt_ready, 1)

            @block.tensor
            def _(pe):
                pe.wait_ge(K.consts_ready, K.N_CONST)
                pe.wait_ge(K.loaded["f3"], 16)
                for i in range(6):
                    k = pe.matmul(K.ps[i // 4][:, (i % 4) * P:(i % 4 + 1) * P], f("la")[0:32, i * P:(i + 1) * P],
                                  f("lb")[0:32, i * P:(i + 1) * P], start=True, stop=True)
                k.then_inc(lora_ps, 1)
                pe.wait_ge(w_ready, 2)
                with pe.Fori(0, B // U) as s:
                    for b in range(NB):
                        e = s * (NB * U) + b * U
                        for u in range(U):
                            pe.wait_ge(h_ready, s * NL + b * U + u + 1)
                            if u >= 2 or b > 0:
                                pe.wait_ge(ht_ready, e + u - 1)
                            for j in range(TS):
                                i = pe.transpose(K.ps[0 + u % 2][:, j * P:(j + 1) * P], hcur[:, u, j * P:(j + 1) * P],
                                                 K.ident[:, :])
                            i.then_inc(ht_ps, 1)
                        for u in range(U):
                            pe.wait_ge(ht_ready, e + u + 1)
                            if u >= 2 or b > 0:
                                pe.wait_ge(y_sb, e + u - 1)
                            for j in range(TS):
                                i = pe.matmul(K.ps[2 + u % 2][:, j * P:(j + 1) * P], ht[:, u, j * P:(j + 1) * P],
                                              w[:, 2 * b * P:(2 * b + 1) * P], start=True, stop=True)
                            i.then_inc(y_ps, 1)
                        for u in range(U):
                            pe.wait_ge(yn_ready, e + u + 1)
                            if u >= 2 or b > 0:
                                pe.wait_ge(gt_ready, e + u - 1)
                            for j in range(TS):
                                i = pe.transpose(K.ps[4 + u % 2][:, j * P:(j + 1) * P], yn[:, u, j * P:(j + 1) * P],
                                                 K.ident[:, :])
                            i.then_inc(ynt_ps, 1)
                        for u in range(U):
                            pe.wait_ge(gt_ready, e + u + 1)
                            if u >= 2 or b > 0:
                                pe.wait_ge(h_ready, s * NL + (b + 1) * U + u - 1)
                            for j in range(TS):
                                i = pe.matmul(K.ps[6 + u % 2][:, j * P:(j + 1) * P], gt[:, u, j * P:(j + 1) * P],
                                              w[:, (2 * b + 1) * P:(2 * b + 2) * P], start=True, stop=True)
                            i.then_inc(z_ps, 1)



def stage_squared_relu_attention(K, tag):
    nc = K.nc
    H, DK, DV = 16, 16, 64
    G = 4
    TINY = 1e-24
    with ExitStack() as scope:
        K.scope = scope
        sb = K.sb
        N = Norm(K, tag)
        xnt = sb(f"{tag}_xnt", [P, W])
        q4 = sb(f"{tag}_q4", [P, 2, G, S])
        k4 = sb(f"{tag}_k4", [P, 2, G, S])
        sq = sb(f"{tag}_qk_squares", [P, G, 2 * S])
        v = sb(f"{tag}_v", [P, 2, TS, H * DV])
        vsq = sb(f"{tag}_v_squares", [P, 2, 512])
        gt = sb(f"{tag}_gates", [P, 2, TS, H * DV])
        ss = sb(f"{tag}_sums", [P, 3, TS, H])
        ssc = sb(f"{tag}_sums_guarded", [P, 3, TS, H])
        nrm = sb(f"{tag}_norms", [P, 2, TS, H])
        rinv = sb(f"{tag}_norms_inverse", [P, 2, 3, TS, H])
        rel = sb(f"{tag}_relu", [P, 3, TS, S])
        at = sb(f"{tag}_attention", [P, 3, TS, S])
        osq = sb(f"{tag}_out_squares", [P, 2, 512])
        og = sb(f"{tag}_out_gated", [P, TS, H * DV])
        on = sb(f"{tag}_out_norm", [P, TS, H])
        onn = sb(f"{tag}_out_norm_root", [P, TS, H])
        n2 = sb(f"{tag}_n", [P, TS, H])
        nmaxed = sb(f"{tag}_n_guarded", [P, TS, H])
        ninv = sb(f"{tag}_n_inverse", [P, TS, H])
        th = sb(f"{tag}_tanh_n", [P, TS, H])
        fac = sb(f"{tag}_factor", [P, TS, H])
        outt = sq[:, :, :].rearrange("p g (c t) -> p (g c) t", c=2)
        (dve_s, xnt_ready, qk_ps, qk_sq, qk_sb, nrm_ps, v_ps, v_sq, v_sb, g_ps, g_ready, guarded, roots, inv_ready,
         sc_ps, rel_ready, at_ready, o_ps, o_sq, on_ready, oroot, n_ready, th_ready, og_ready, ot_ps, ot_ready,
         y_ps, done, silu_ready, v_summed) = make_sems(
            K, tag, "dve_chain xnt_ready qk_product qk_squares qk_ready norm_product v_product v_squares v_ready "
                    "gate_product gate_ready sums_guarded roots_ready inverse_ready scores_product relu_ready "
                    "attention_ready out_product out_squares out_norm_ready out_root_ready n_ready tanh_ready "
                    "gated_ready outt_product outt_ready y_product seq_done silu_ready v_squares_summed")
        f = lambda n: field(K, "a3", n)
        STATS, APPLY, XT, K0 = 0, 1, 2, 3
        NORMS = 8
        product_bank = lambda k: K.ps[1 - k % 2]
        at_head = lambda i: [k for k in range(13) if min(K0 + k, H - 1) == i]
        read_at = lambda i: [k for k in range(13) if min(K0 + k + 1, H - 1) == i]

        def over_pairs(eng, prepare, main):
            for i in range(H):
                prepare(0, 0, i)
            with eng.Fori(0, B // 2 - 1) as pair:
                for q in range(2):
                    main(pair * 2 + q, q, True)
            main(B - 2, 0, True)
            main(B - 1, 1, False)

        with nc.Block() as block:
            K.start_loads(block, tag)

            @block.vector
            def _(dve):
                dve.sem_inc(done, 1)

                def prepare(s, q, i):
                    xs = lambda j: K.x[:, bass.ds(s * W + j * P, P)]
                    if i == STATS:
                        link = chain(dve, dve_s)
                        for j in range(TS):
                            k = dve.bn_stats(N.bn[:, j, :], xs(j))
                        link(k)
                        for j in range(TS):
                            k = dve.bn_aggr(N.mv[:, j, :], N.bn[:, j, :])
                        k.then_inc(N.stats, 1)
                    if i == APPLY:
                        dve.wait_ge(N.rstd, s + 1)
                        for j in range(TS):
                            k = dve.tensor_scalar(N.out[:, j * P:(j + 1) * P], xs(j), N.mv[:, j, 0:1],
                                                  N.rs[:, j:j + 1], ALU.subtract, ALU.mult)
                        k.then_inc(N.xn, 1)
                    if i == XT:
                        dve.wait_ge(N.xt, s + 1)
                        dve.tensor_copy(xnt[:, :], K.ps[0][:, 0:W]).then_inc(xnt_ready, 1)
                    for k in read_at(i):
                        bank = product_bank(k)
                        if k < 4:
                            dve.wait_ge(qk_sq, s * G + k + 1)
                            dve.tensor_copy(q4[:, q, k, :], bank[:, 0:S])
                            dve.tensor_copy(k4[:, q, k, :], bank[:, S:2 * S]).then_inc(qk_sb, 1)
                        elif k < 8:
                            n = k - 4
                            j, c = n // 2, n % 2
                            link = chain(dve, dve_s)
                            dve.wait_ge(v_sq, s * 4 + n + 1)
                            dve.tensor_copy(v[:, q, j, c * 512:(c + 1) * 512], bank[:, :]).then_inc(v_sb, 1)
                            link(dve.tensor_reduce(ss[:, 2, j, c * 8:(c + 1) * 8],
                                                   vsq[:, n % 2, :].rearrange("p (h d) -> p h d", h=8), AX_X, ALU.add))
                            dve.sem_inc(v_summed, 1)
                        elif k == NORMS:
                            link = chain(dve, dve_s)
                            dve.wait_ge(nrm_ps, s + 1)
                            link(dve.tensor_copy(ss[:, 0:2, :, :],
                                                 bank[:, 0:64].rearrange("p (a t h) -> p a t h", a=2, t=TS)))
                            dve.tensor_scalar(ssc[:, :, :, :], ss[:, :, :, :], TINY, None, ALU.max).then_inc(guarded, 1)
                    if i == K0 + NORMS + 3:
                        dve.wait_ge(roots, s + 1)
                        dve.reciprocal(rinv[:, q, 0, :, :], ssc[:, 0, :, :])
                        dve.reciprocal(rinv[:, q, 1:3, :, :], nrm[:, :, :, :]).then_inc(inv_ready, 1)

                def main(s, q, more):
                    dve.wait_ge(inv_ready, s + 1)
                    for h in range(H):
                        dve.wait_ge(rel_ready, s * H + h + 1)
                        if h >= 3:
                            dve.wait_ge(o_ps, s * H + h - 2)
                        for j in range(TS):
                            i = dve.scalar_tensor_tensor(at[:, h % 3, j, :], rel[:, h % 3, j, :],
                                                         rinv[:, q, 2, j, h:h + 1], rel[:, h % 3, j, :], ALU.mult, ALU.mult)
                        i.then_inc(at_ready, 1)
                        if more:
                            prepare(s + 1, 1 - q, h)
                    link = chain(dve, dve_s)
                    for n in range(4):
                        a, j = n // 2, n % 2
                        dve.wait_ge(o_sq, s * 4 + n + 1)
                        dve.tensor_reduce(on[:, j, a * 8:(a + 1) * 8],
                                          osq[:, n % 2, :].rearrange("p (h d) -> p h d", h=8), AX_X,
                                          ALU.add).then_inc(on_ready, 1)
                    dve.wait_ge(oroot, s + 1)
                    dve.tensor_tensor(n2[:, :, :], onn[:, :, :], rinv[:, q, 0, :, :], ALU.mult).then_inc(n_ready, 1)
                    dve.wait_ge(n_ready, s + 1)
                    link(dve.tensor_scalar(nmaxed[:, :, :], n2[:, :, :], 1e-12, None, ALU.max))
                    link(dve.reciprocal(ninv[:, :, :], nmaxed[:, :, :]))
                    link(dve.tensor_tensor(ninv[:, :, :], ninv[:, :, :], rinv[:, q, 0, :, :], ALU.mult))
                    dve.wait_ge(th_ready, s + 1)
                    link(dve.tensor_tensor(fac[:, :, :], th[:, :, :], ninv[:, :, :], ALU.mult))
                    for n in range(4):
                        a, j = n // 2, n % 2
                        hh = slice(a * 8, (a + 1) * 8)
                        cols = og[:, j, a * 512:(a + 1) * 512]
                        link(dve.tensor_tensor(cols, K.ps[4 + n][:, :], gt[:, q, j, a * 512:(a + 1) * 512], ALU.mult))
                        dve.tensor_tensor(cols.rearrange("p (h d) -> p h d", h=8), cols.rearrange("p (h d) -> p h d", h=8),
                                          fac[:, j, hh].unsqueeze(2).broadcast_to([P, 8, DV]), ALU.mult).then_inc(og_ready, 1)
                    dve.wait_ge(y_ps, s + 1)
                    xs = K.x[:, bass.ds(s * W, W)]
                    dve.tensor_tensor(xs, K.ps[0][:, 0:W], xs, ALU.add).then_inc(done, 1)
                over_pairs(dve, prepare, main)

            @block.gpsimd
            def _(pool):
                with pool.Fori(0, B) as s:
                    norm_pool(K, N, pool, s)

            @block.scalar
            def _(act):
                def prepare(s, q, i):
                    for k in read_at(i):
                        bank = product_bank(k)
                        if k < 4:
                            act.wait_ge(qk_ps, s * G + k + 1)
                            act.activation(sq[:, k, :], bank[:, :], ACT.Square).then_inc(qk_sq, 1)
                        elif k < 8:
                            n = k - 4
                            act.wait_ge(v_ps, s * 4 + n + 1)
                            if n >= 2:
                                act.wait_ge(v_summed, s * 4 + n - 1)
                            act.activation(vsq[:, n % 2, :], bank[:, :], ACT.Square).then_inc(v_sq, 1)
                        elif k == NORMS:
                            act.wait_ge(guarded, s + 1)
                            act.activation(nrm[:, :, :, :], ssc[:, 1:3, :, :], ACT.Sqrt).then_inc(roots, 1)
                        else:
                            n = k - NORMS - 1
                            act.wait_ge(g_ps, s * 4 + n + 1)
                            act.activation(gt[:, q, n // 2, (n % 2) * 512:(n % 2 + 1) * 512], bank[:, :],
                                           ACT.Silu).then_inc(silu_ready, 1)
                            if n == 3:
                                act.wait_ge(silu_ready, s * 4 + 4)
                                act.activation(gt[:, q, :, :], gt[:, q, :, :], ACT.Tanh).then_inc(g_ready, 1)

                def main(s, q, more):
                    act.wait_ge(done, s + 1)
                    act.wait_ge(inv_ready, s + 1)
                    for h in range(H):
                        act.wait_ge(sc_ps, s * H + h + 1)
                        if h >= 3:
                            act.wait_ge(at_ready, s * H + h - 2)
                        for j in range(TS):
                            i = act.activation(rel[:, h % 3, j, :], K.ps[2 + h % 2][:, j * S:(j + 1) * S], ACT.Relu,
                                               scale=rinv[:, q, 1, j, h:h + 1])
                        i.then_inc(rel_ready, 1)
                        if more:
                            prepare(s + 1, 1 - q, h)
                    for n in range(4):
                        act.wait_ge(o_ps, s * H + 8 * (n // 2) + 8)
                        if n >= 2:
                            act.wait_ge(on_ready, s * 4 + n - 1)
                        act.activation(osq[:, n % 2, :], K.ps[4 + n][:, :], ACT.Square).then_inc(o_sq, 1)
                    act.wait_ge(on_ready, s * 4 + 4)
                    act.activation(onn[:, :, :], on[:, :, :], ACT.Sqrt).then_inc(oroot, 1)
                    act.wait_ge(n_ready, s + 1)
                    act.activation(th[:, :, :], n2[:, :, :], ACT.Tanh).then_inc(th_ready, 1)
                    for n in range(4):
                        act.wait_ge(ot_ps, s * 4 + n + 1)
                        act.activation(outt[:, 2 * n:2 * n + 2, :].rearrange("p c t -> p (c t)"), K.ps[2 + n % 2][:, :],
                                       ACT.Copy).then_inc(ot_ready, 1)
                over_pairs(act, prepare, main)

            @block.tensor
            def _(pe):
                pe.wait_ge(K.consts_ready, K.N_CONST)
                pe.wait_ge(K.loaded["a3"], 16)

                def prepare(s, q, i):
                    if i == XT:
                        norm_tensor(K, N, pe, s, K.ps[0])
                    for k in at_head(i):
                        bank = product_bank(k)
                        if k == 0:
                            pe.wait_ge(xnt_ready, s + 1)
                        elif 2 <= k < 6:
                            pe.wait_ge(qk_sb, s * G + k - 1)
                        elif 6 <= k < 10:
                            pe.wait_ge(v_sb, s * 4 + k - 5)
                        elif k == 10:
                            pe.wait_ge(guarded, s + 1)
                        elif k > 10:
                            pe.wait_ge(silu_ready, s * 4 + k - 10)
                        if k < 4:
                            pe.matmul(bank[:, 0:S], f("wq4")[:, k * P:(k + 1) * P], xnt[:, :], start=True, stop=True)
                            pe.matmul(bank[:, S:2 * S], f("wk4")[:, k * P:(k + 1) * P], xnt[:, :],
                                      start=True, stop=True).then_inc(qk_ps, 1)
                        elif k == NORMS:
                            for g in range(G):
                                for a in range(2):
                                    for j in range(TS):
                                        c = (a * TS + j) * H + 4 * g
                                        m = pe.matmul(bank[:, c:c + 4], sq[:, g, a * S + j * P:a * S + (j + 1) * P],
                                                      K.quad[:, :], start=True, stop=True)
                            m.then_inc(nrm_ps, 1)
                        else:
                            n, w, sem = (k - 4, "wv", v_ps) if k < NORMS else (k - NORMS - 1, "wg", g_ps)
                            j, c = n // 2, n % 2
                            pe.matmul(bank[:, :], xnt[:, j * P:(j + 1) * P], f(w)[:, c * 512:(c + 1) * 512],
                                      start=True, stop=True).then_inc(sem, 1)

                def main(s, q, more):
                    pe.wait_ge(done, s + 1)
                    pe.wait_ge(inv_ready, s + 1)
                    pe.wait_ge(silu_ready, s * 4 + 4)
                    for i in range(H + 2):
                        if i < H:
                            g, r = i // 4, 32 * (i % 4)
                            if i >= 2:
                                pe.wait_ge(rel_ready, s * H + i - 1)
                            for j in range(TS):
                                k = pe.matmul(K.ps[2 + i % 2][:, j * S:(j + 1) * S], k4[r:r + 32, q, g, j * P:(j + 1) * P],
                                              q4[r:r + 32, q, g, :], start=True, stop=True)
                            k.then_inc(sc_ps, 1)
                        if i >= 2:
                            h = i - 2
                            pe.wait_ge(at_ready, s * H + h + 1)
                            for t in range(TS):
                                for j in range(TS):
                                    k = pe.matmul(K.ps[4 + 2 * (h // 8) + t][:, (h % 8) * DV:(h % 8 + 1) * DV],
                                                  at[:, h % 3, j, t * P:(t + 1) * P], v[:, q, j, h * DV:(h + 1) * DV],
                                                  start=(j == 0), stop=(j == TS - 1))
                            k.then_inc(o_ps, 1)
                        if more and i < H:
                            prepare(s + 1, 1 - q, i)
                    for n in range(4):
                        if n >= 2:
                            pe.wait_ge(ot_ready, s * 4 + n - 1)
                        pe.wait_ge(og_ready, s * 4 + (2 if n < 2 else 4))
                        for c in range(2):
                            for t in range(TS):
                                i = pe.transpose(K.ps[2 + n % 2][:, c * S + t * P:c * S + (t + 1) * P],
                                                 og[:, t, (2 * n + c) * P:(2 * n + c + 1) * P], K.ident[:, :])
                        i.then_inc(ot_ps, 1)
                    for t in range(TS):
                        for c in range(8):
                            if t == 0 and c % 2 == 0:
                                pe.wait_ge(ot_ready, s * 4 + c // 2 + 1)
                            i = pe.matmul(K.ps[0][:, t * P:(t + 1) * P], outt[:, c, t * P:(t + 1) * P],
                                          f("wo")[:, c * P:(c + 1) * P], start=(c == 0), stop=(c == 7))
                    i.then_inc(y_ps, 1)
                over_pairs(pe, prepare, main)



STAGES = {
    "f0a": (stage_signed_ffn,), "at0": (stage_softmax_attention,), "f0b": (stage_signed_ffn,),
    "m1a": (stage_gated_experts,), "mam": (stage_state_space,), "m1b": (stage_gated_experts,),
    "m2a": (stage_gelu_experts,), "at2": (stage_window_linear_attention,), "m2b": (stage_gelu_experts,),
    "f3a": (stage_quantised_ffn,), "at3": (stage_squared_relu_attention,), "f3b": (stage_quantised_ffn,),
}
REGION = {"a0": "r0", "mb": "r0", "a2": "r0", "a3": "r0", "m1": "r1", "m2": "r2", "f3": "r3"}
LOAD_AT = {"mb": "m1a", "a2": "m1b", "a3": "f3a"}


def build(nc, aps, out, stages=tuple(STAGES)):
    K = Core()
    K.nc = nc
    needs = {"f0a": "a0", "at0": "a0", "f0b": "a0", "m1a": "m1", "mam": "mb", "m1b": "m1", "m2a": "m2",
             "at2": "a2", "m2b": "m2", "f3a": "f3", "at3": "a3", "f3b": "f3"}
    used = [p for p in PACKS if p in {needs[s] for s in stages}]
    with ExitStack() as ctx:
        K.sem_scope = ctx.enter_context(ExitStack())
        K.live_sems = []
        K.scope = ctx
        K.sb = lambda name, shape, dt=F32: K.scope.enter_context(nc.sbuf_tensor(name, shape, dt))
        K.ps = [ctx.enter_context(nc.psum_tensor(f"bank{i}", [P, 512], F32)) for i in range(8)]
        K.x = K.sb("x", [P, B * W])
        K.ident = K.sb("identity", [P, P])
        K.neg_half = K.sb("neg_half", [P, 8])
        K.neg_one = K.sb("neg_one", [P, 1])
        K.ones = K.sb("ones", [P, P])
        K.quad = K.sb("quadrant_ones", [P, 4])
        K.iota16 = K.sb("iota16", [P, E])
        K.sel64 = K.sb("select_64", [PARTS, E * 64], BF16)
        K.sel = K.sb("select", [96, 32 * P], BF16)
        K.qw = K.sb("qweights", [P, 6 * P], I32)
        region = {}
        for p in used:
            r = REGION[p]
            region[r] = max(region.get(r, 0), pack_width(p))
        region = {r: K.sb(f"weights_{r}", [P, n]) for r, n in region.items()}
        K.pack = {p: region[REGION[p]] for p in used}
        K.loaded = {p: ctx.enter_context(nc.semaphore(f"loaded_{p}")) for p in used}
        K.loaded_x, K.loaded_q, K.consts_ready, K.const_chain, K.stored = (
            ctx.enter_context(nc.semaphore(n)) for n in
            ("loaded_x", "loaded_q", "consts_ready", "const_chain", "stored"))
        K.N_CONST = 1

        def start_loads(block, tag):
            due = [p for p in used if LOAD_AT.get(p) == tag]
            if due:
                @block.sync
                def _(sp):
                    for p in due:
                        sp.dma_start(K.pack[p][:, 0:pack_width(p)], aps[p]).then_inc(K.loaded[p], 16)
        K.start_loads = start_loads

        with nc.Block() as block:
            @block.sync
            def _(sp):
                sp.dma_start(K.x[:, :], aps["x"]).then_inc(K.loaded_x, 16)
                for p in used:
                    if LOAD_AT.get(p) not in stages:
                        sp.dma_start(K.pack[p][:, 0:pack_width(p)], aps[p]).then_inc(K.loaded[p], 16)
                sp.dma_start(K.qw[:, :], aps["q"]).then_inc(K.loaded_q, 16)
                sp.wait_ge(K.loaded_x, 16)

            @block.gpsimd
            def _(pool):
                n = 0

                def link(ins):
                    nonlocal n
                    n += 1
                    ins.then_inc(K.const_chain, 1)
                    pool.wait_ge(K.const_chain, n)
                pool.memset(K.neg_half[:, :], -0.5)
                pool.memset(K.ones[:, :], 1.0)
                pool.memset(K.neg_one[:, :], -1.0)
                pool.iota(K.iota16[:, :], [[1, E]], base=0, channel_multiplier=0,
                          allow_small_or_imprecise_dtypes=True)
                pool.memset(K.sel64[:, :], 0.0)
                pool.memset(K.sel[:, :], 0.0)
                link(pool.memset(K.ident[:, :], 0.0))
                link(pool.affine_select(out=K.ident[:, :], in_=K.ident[:, :], compare_op=ALU.not_equal, fill=1.0,
                                        base=0, pattern=[[-1, P]], channel_multiplier=1))
                link(pool.memset(K.quad[:, :], 1.0))
                link(pool.affine_select(out=K.quad[:, :], in_=K.quad[:, :], compare_op=ALU.is_ge, fill=0.0, base=0,
                                        pattern=[[-32, 4]], channel_multiplier=1))
                link(pool.affine_select(out=K.quad[:, :], in_=K.quad[:, :], compare_op=ALU.is_ge, fill=0.0, base=31,
                                        pattern=[[32, 4]], channel_multiplier=-1))
                for sel, rows, wide in ((K.sel64, E, 64), (K.sel, 32, P)):
                    for base in (HI, MID, LO):
                        v = sel[:, :].rearrange("p (e c) -> p e c", e=rows)
                        link(pool.affine_select(out=v, in_=v, compare_op=ALU.not_equal, fill=1.0, base=-base,
                                                pattern=[[-1, rows], [0, wide]], channel_multiplier=1))
                pool.sem_inc(K.consts_ready, 1)
        for tag in stages:
            STAGES[tag][0](K, tag)
            clear_sems(K)
        with nc.Block() as block:
            @block.sync
            def _(sp):
                sp.dma_start(out, K.x[:, :]).then_inc(K.stored, 16)
                sp.wait_ge(K.stored, 16)


def host_arrays(i):
    rows = lambda v: np.broadcast_to(np.asarray(v).reshape(1, -1), (P, np.asarray(v).size))
    cols = lambda v, n: np.asarray(v).reshape(n, P).T
    kpm = lambda w: w.reshape(-1, P, w.shape[-1]).transpose(1, 0, 2).reshape(P, -1)

    def pad(a):
        out = np.zeros((P, a.shape[1]), a.dtype)
        out[:a.shape[0]] = a
        return out

    def by_four(w, d):
        out = np.zeros((w.shape[0], 16, 32), w.dtype)
        out[:, :, :d] = w.reshape(w.shape[0], 16, d)
        return out.reshape(w.shape[0], 512)

    g = {}
    Ww, Wb = i["L0_attn_W_w"], i["L0_attn_W_b"]
    g["a0"] = dict(ffn=i["L0_ffn_weight"].T, wq=Ww[:1024].T, wk=Ww[1024:2048].T, wv=Ww[2048:].T,
                   wo=kpm(i["L0_attn_out_w"].T), bq=cols(Wb[:1024], 8), bk=cols(Wb[1024:2048], 8),
                   bv=rows(Wb[2048:]), bo=rows(i["L0_attn_out_b"]))
    g["m1"] = dict(rw=i["L1_ffn_router_w"].T, rb=np.tile(rows(i["L1_ffn_router_bias"]), (1, 2)),
                   up=i["L1_ffn_up_proj"].transpose(1, 0, 2).reshape(P, -1),
                   gate=i["L1_ffn_gate_proj"].transpose(1, 0, 2).reshape(P, -1),
                   down=kpm(i["L1_ffn_down_proj"].reshape(1024, P)), shg=i["L1_ffn_sh_gate"].T,
                   shu=i["L1_ffn_sh_up"].T, shd=i["L1_ffn_sh_down"].T)
    mb = {}
    for l in range(4):
        a = {k[8:]: v[l] for k, v in i.items() if k.startswith("L1_attn_") and "fnorm" not in k}
        bc = a["x_proj_w"][8:40].T
        xp = np.concatenate([bc, bc, bc, a["x_proj_w"][:8].T], axis=1)
        dtw = np.zeros((P, 256), np.float32)
        dtw[96:104] = a["dt_proj_w"].T
        mb.update({f"{k}{l}": v for k, v in dict(
            taps=rows(a["conv_w"][:, 0, :].T), inx=a["in_proj_w"][:256].T, inz=a["in_proj_w"][256:].T,
            cb=cols(a["conv_b"], 2), xp=kpm(xp), dtw=dtw, dtb=cols(a["dt_proj_b"], 2),
            alog=kpm(a["A_log"]), dsk=cols(a["D_skip"], 2), outw=kpm(a["out_proj_w"].T),
            lnw=a["ln_w"][:, None], lnb=a["ln_b"][:, None]).items()})
    g["mb"] = mb
    g["m2"] = dict(rw=i["L2_ffn_router_w"], rb=np.tile(rows(i["L2_ffn_router_b"]), (1, 2)),
                   w1=i["L2_ffn_w1"].transpose(1, 0, 2).reshape(P, -1), b1=cols(i["L2_ffn_b1"], 32),
                   w2=kpm(i["L2_ffn_w2"].reshape(-1, P)), b2=pad(i["L2_ffn_b2"]))
    a = {k[8:]: v for k, v in i.items() if k.startswith("L2_attn_")}
    at = np.clip(np.arange(192)[None, :] + 32 - np.arange(P)[:, None], 0, 128)
    g["a2"] = dict(wql=a["wq_lin"], wkl=a["wk_lin"], wvl=a["wv_lin"], bql=a["bq_lin"][:, None],
                   bkl=rows(a["bk_lin"]), bvl=rows(a["bv_lin"]), wq4=by_four(a["wq_loc"], 8),
                   wk4=by_four(a["wk_loc"], 8), bq4=cols(by_four(rows(a["bq_loc"])[:1], 8), 4),
                   bk4=cols(by_four(rows(a["bk_loc"])[:1], 8), 4), wvc=a["wv_loc"], bvc=rows(a["bv_loc"]),
                   wo=a["wo"], bo=rows(a["bo"]), wg1=kpm(a["wg1"]), bg1=a["bg1"][:, None], wg2=a["wg2"],
                   bg2=a["bg2"][:, None], lng=a["ln_g"][:, None], lnb=a["ln_b"][:, None],
                   band=a["rel_bias"][at].transpose(0, 2, 1).reshape(P, -1))
    g["f3"] = dict(scale=np.repeat(i["L3_ffn_scales"].transpose(2, 0, 1), 16, axis=0).reshape(P, -1),
                   bias=rows(i["L3_ffn_biases"]), la=pad(i["L3_ffn_lora_a"].transpose(1, 0, 2).reshape(32, -1)),
                   lb=pad(i["L3_ffn_lora_b"].transpose(2, 0, 1).reshape(32, -1)),
                   gam=i["L3_ffn_ln_gamma"].T, bet=i["L3_ffn_ln_beta"].T)
    qg, kv = (i[n].reshape(P, 16, 80) for n in ("L3_attn_Wqg", "L3_attn_Wkv"))
    g["a3"] = dict(wq4=by_four(qg[:, :, :16].reshape(P, -1), 16), wk4=by_four(kv[:, :, :16].reshape(P, -1), 16),
                   wg=qg[:, :, 16:].reshape(P, -1), wv=kv[:, :, 16:].reshape(P, -1), wo=kpm(i["L3_attn_Wout"]))
    arrays = {}
    for p, fields in PACKS.items():
        for n, c in fields.items():
            assert g[p][n].shape == (P, c), (p, n, g[p][n].shape, c)
        arrays[p] = np.ascontiguousarray(np.concatenate([g[p][n] for n in fields], axis=1))
    arrays["q"] = np.ascontiguousarray(i["L3_ffn_qweights"].transpose(2, 0, 1).reshape(P, -1))
    arrays["x"] = np.ascontiguousarray(i["L0_attn_x"].reshape(B * TS, P, P).transpose(1, 0, 2).reshape(P, -1))
    return arrays


def kernel(**inputs):
    from concourse import bacc
    from concourse.bass_utils import run_bass_kernel_spmd

    arrays = host_arrays({k: np.asarray(v) for k, v in inputs.items()})
    nc = bacc.Bacc("TRN2", target_bir_lowering=False, num_devices=1)
    aps = {n: nc.dram_tensor(f"in_{n}", a.shape, mybir.dt.from_np(a.dtype), kind="ExternalInput").ap()
           for n, a in arrays.items()}
    out = nc.dram_tensor("out_x", (P, B * W), F32, kind="ExternalOutput").ap()
    build(nc, aps, out)
    r = run_bass_kernel_spmd(nc, [{f"in_{n}": a for n, a in arrays.items()}], core_ids=[0])
    y = r.results[0]["out_x"]
    return np.ascontiguousarray(y.reshape(P, B * TS, P).transpose(1, 0, 2)).reshape(B, S, P)
```
